# Optimizing a Trainium2 kernel written in Bass

```python
import numpy as np
import jax
import jax.numpy as jnp

def _softmax(x, axis=-1):
    return jax.nn.softmax(x, axis=axis)

def _gelu(x):
    return jax.nn.gelu(x, approximate=True)

def _silu(x):
    return jax.nn.silu(x)

def _sigmoid(x):
    return jax.nn.sigmoid(x)

def _layernorm(x, axis=-1, eps=1e-05):
    m = jnp.mean(x, axis=axis, keepdims=True)
    v = jnp.var(x, axis=axis, keepdims=True)
    return (x - m) / jnp.sqrt(v + eps)

def _scatter_add(tgt, idx, src, axis=0):
    return tgt.at[idx].add(src)

def _segment_sum(src, seg, n):
    return jax.ops.segment_sum(src, seg, n)
kernel_name = 'mk_adaln_d2_jaxref_r8_021c7c'

def setup_inputs(seed: int=0):
    np.random.seed(seed)
    _w = jnp.asarray

    def _L0_attn_setup():
        import jax, jax.numpy as jnp
        import numpy as np
        B, S, D = (2, 256, 512)
        NH, NKV = (32, 8)
        HD = D // NH
        NREP = NH // NKV
        SCALE = HD ** (-0.5)
        key = jax.random.key(seed)
        kx, kq, kk, kv, ko = jax.random.split(key, 5)
        s = 0.02
        return {'x': jax.random.normal(kx, (B, S, D), dtype=jnp.float32), 'wq': jax.random.normal(kq, (D, NH * HD), dtype=jnp.float32) * s, 'wk': jax.random.normal(kk, (D, NKV * HD), dtype=jnp.float32) * s, 'wv': jax.random.normal(kv, (D, NKV * HD), dtype=jnp.float32) * s, 'wo': jax.random.normal(ko, (NH * HD, D), dtype=jnp.float32) * s}
    _L0_attn_in = _L0_attn_setup()

    def _L0_ffn_setup():
        import jax, jax.numpy as jnp
        import numpy as np
        HIDDEN = 512
        MOE_INTER = 128
        SHARED_INTER = 512
        NUM_EXPERTS = 16
        TOP_K = 2

        def _moe_forward(x, gate_w, w_gate_up, w_down, shared_w_gate_up, shared_w_down):
            orig_shape = x.shape
            x2 = x.reshape(-1, orig_shape[-1])
            gu_s = x2 @ shared_w_gate_up.T
            g_s, u_s = jnp.split(gu_s, 2, axis=-1)
            shared_out = jax.nn.silu(g_s) * u_s @ shared_w_down.T
            logits = x2 @ gate_w.T
            probs = jax.nn.softmax(logits, axis=-1)
            topk_vals, topk_idx = jax.lax.top_k(probs, TOP_K)
            topk_vals = topk_vals / jnp.sum(topk_vals, axis=-1, keepdims=True)
            combine = jnp.sum(jax.nn.one_hot(topk_idx, NUM_EXPERTS, dtype=x2.dtype) * topk_vals[..., None], axis=1)
            gu = jnp.einsum('th,eih->eti', x2, w_gate_up)
            g, u = jnp.split(gu, 2, axis=-1)
            act = jax.nn.silu(g) * u
            out_e = jnp.einsum('eti,ehi->eth', act, w_down)
            moe_out = jnp.einsum('eth,te->th', out_e, combine)
            return (moe_out + shared_out).reshape(orig_shape)
        key = jax.random.key(seed)
        ks = jax.random.split(key, 6)
        s = 0.02
        hidden_states = jax.random.normal(ks[0], (2, 256, HIDDEN), dtype=jnp.float32)
        gate_w = jax.random.normal(ks[1], (NUM_EXPERTS, HIDDEN), dtype=jnp.float32) * s
        w_gate_up = jax.random.normal(ks[2], (NUM_EXPERTS, 2 * MOE_INTER, HIDDEN), dtype=jnp.float32) * s
        w_down = jax.random.normal(ks[3], (NUM_EXPERTS, HIDDEN, MOE_INTER), dtype=jnp.float32) * s
        shared_w_gate_up = jax.random.normal(ks[4], (2 * SHARED_INTER, HIDDEN), dtype=jnp.float32) * s
        shared_w_down = jax.random.normal(ks[5], (HIDDEN, SHARED_INTER), dtype=jnp.float32) * s
        return {'hidden_states': hidden_states, 'gate_w': gate_w, 'w_gate_up': w_gate_up, 'w_down': w_down, 'shared_w_gate_up': shared_w_gate_up, 'shared_w_down': shared_w_down}
    _L0_ffn_in = _L0_ffn_setup()
    _L0_c = _w((lambda *s: np.random.randn(*s).astype(np.float32) * 0.05)(4, 512))
    _L0_wmod = _w((lambda *s: np.random.randn(*s).astype(np.float32) * 0.05)(512, 6 * 512) * 512 ** (-0.5))

    def _L1_attn_setup():
        import jax, jax.numpy as jnp
        import numpy as np
        B, S, HID = (2, 512, 512)
        H, HKV, D = (32, 8, 128)
        G = H // HKV
        EPS = 1e-06

        def _reference_tuple_inner(hidden_states, Wq, bq, Wk, bk, Wv, bv, Wo, M, z):
            b, s, _ = hidden_states.shape
            q = (hidden_states @ Wq.T + bq).reshape(b, s, H, D)
            k = (hidden_states @ Wk.T + bk).reshape(b, s, HKV, D)
            v = (hidden_states @ Wv.T + bv).reshape(b, s, HKV, D)
            sig_q = jax.nn.elu(q) + 1.0
            sig_k = jax.nn.elu(k) + 1.0
            q_sel = sig_q[:, :, ::G, :]
            num = jnp.einsum('bshd,hde->bshe', q_sel, M)
            den = jnp.einsum('bshd,hd->bsh', q_sel, z)[..., None] + EPS
            retrieved = num / den
            out_heads = jnp.repeat(retrieved, G, axis=2)
            output = out_heads.reshape(b, s, H * D) @ Wo.T
            M_new = M + jnp.einsum('bshd,bshe->hde', sig_k, v)
            z_new = z + sig_k.sum(axis=(0, 1))
            return (output, M_new, z_new)
        key = jax.random.key(seed)
        ks = jax.random.split(key, 10)
        s = 0.02
        return {'hidden_states': jax.random.normal(ks[0], (B, S, HID), jnp.float32), 'Wq': jax.random.normal(ks[1], (H * D, HID), jnp.float32) * s, 'bq': jnp.zeros((H * D,), jnp.float32), 'Wk': jax.random.normal(ks[2], (HKV * D, HID), jnp.float32) * s, 'bk': jnp.zeros((HKV * D,), jnp.float32), 'Wv': jax.random.normal(ks[3], (HKV * D, HID), jnp.float32) * s, 'bv': jnp.zeros((HKV * D,), jnp.float32), 'Wo': jax.random.normal(ks[4], (HID, H * D), jnp.float32) * s, 'M': jax.random.normal(ks[5], (HKV, D, D), jnp.float32), 'z': jax.random.uniform(ks[6], (HKV, D), jnp.float32) * 100.0 + 1.0}
    _L1_attn_in = _L1_attn_setup()

    def _L1_ffn_setup():
        import jax, jax.numpy as jnp
        import numpy as np
        HIDDEN = 512
        INTER = 1376
        BATCH, SEQ = (2, 256)

        def _ternary(key, shape):
            return jax.random.randint(key, shape, -1, 2).astype(jnp.float32)
        key = jax.random.key(seed)
        kx, kg, ku, kd = jax.random.split(key, 4)
        x = jax.random.normal(kx, (BATCH, SEQ, HIDDEN), dtype=jnp.float32)
        gate_w = _ternary(kg, (INTER, HIDDEN))
        up_w = _ternary(ku, (INTER, HIDDEN))
        down_w = _ternary(kd, (HIDDEN, INTER))
        gate_scale = jnp.float32(0.02)
        up_scale = jnp.float32(0.02)
        down_scale = jnp.float32(0.02)
        return {'x': x, 'gate_w': gate_w, 'up_w': up_w, 'down_w': down_w, 'gate_scale': gate_scale, 'up_scale': up_scale, 'down_scale': down_scale}
    _L1_ffn_in = _L1_ffn_setup()
    _L1_c = _w((lambda *s: np.random.randn(*s).astype(np.float32) * 0.05)(4, 512))
    _L1_wmod = _w((lambda *s: np.random.randn(*s).astype(np.float32) * 0.05)(512, 6 * 512) * 512 ** (-0.5))
    _d = {'L0_attn_x': _L0_attn_in['x'], 'L0_attn_wq': _L0_attn_in['wq'], 'L0_attn_wk': _L0_attn_in['wk'], 'L0_attn_wv': _L0_attn_in['wv'], 'L0_attn_wo': _L0_attn_in['wo'], 'L0_ffn_gate_w': _L0_ffn_in['gate_w'], 'L0_ffn_w_gate_up': _L0_ffn_in['w_gate_up'], 'L0_ffn_w_down': _L0_ffn_in['w_down'], 'L0_ffn_shared_w_gate_up': _L0_ffn_in['shared_w_gate_up'], 'L0_ffn_shared_w_down': _L0_ffn_in['shared_w_down'], 'L0_c': _L0_c, 'L0_wmod': _L0_wmod, 'L1_attn_Wq': _L1_attn_in['Wq'], 'L1_attn_bq': _L1_attn_in['bq'], 'L1_attn_Wk': _L1_attn_in['Wk'], 'L1_attn_bk': _L1_attn_in['bk'], 'L1_attn_Wv': _L1_attn_in['Wv'], 'L1_attn_bv': _L1_attn_in['bv'], 'L1_attn_Wo': _L1_attn_in['Wo'], 'L1_attn_M': _L1_attn_in['M'], 'L1_attn_z': _L1_attn_in['z'], 'L1_ffn_gate_w': _L1_ffn_in['gate_w'], 'L1_ffn_up_w': _L1_ffn_in['up_w'], 'L1_ffn_down_w': _L1_ffn_in['down_w'], 'L1_ffn_gate_scale': _L1_ffn_in['gate_scale'], 'L1_ffn_up_scale': _L1_ffn_in['up_scale'], 'L1_ffn_down_scale': _L1_ffn_in['down_scale'], 'L1_c': _L1_c, 'L1_wmod': _L1_wmod}
    _x0 = _d['L0_attn_x']
    _d['L0_attn_x'] = jax.random.normal(jax.random.fold_in(jax.random.key(seed), 1), (4, 256, 512), dtype=_x0.dtype)
    del _x0
    return _d

def reference(L0_attn_x, L0_attn_wq, L0_attn_wk, L0_attn_wv, L0_attn_wo, L0_ffn_gate_w, L0_ffn_w_gate_up, L0_ffn_w_down, L0_ffn_shared_w_gate_up, L0_ffn_shared_w_down, L0_c, L0_wmod, L1_attn_Wq, L1_attn_bq, L1_attn_Wk, L1_attn_bk, L1_attn_Wv, L1_attn_bv, L1_attn_Wo, L1_attn_M, L1_attn_z, L1_ffn_gate_w, L1_ffn_up_w, L1_ffn_down_w, L1_ffn_gate_scale, L1_ffn_up_scale, L1_ffn_down_scale, L1_c, L1_wmod):

    def _L0_attn_ref(x, wq, wk, wv, wo):
        import jax, jax.numpy as jnp
        import numpy as np
        B, S, D = (2, 256, 512)
        NH, NKV = (32, 8)
        HD = D // NH
        NREP = NH // NKV
        SCALE = HD ** (-0.5)
        b, s, _ = x.shape
        q = (x @ wq).reshape(b, s, NH, HD)
        k = (x @ wk).reshape(b, s, NKV, HD)
        v = (x @ wv).reshape(b, s, NKV, HD)
        k = jnp.repeat(k, NREP, axis=2)
        v = jnp.repeat(v, NREP, axis=2)
        scores = jnp.einsum('bihd,bjhd->bhij', q, k) * SCALE
        causal = jnp.tril(jnp.ones((s, s), dtype=bool))
        scores = jnp.where(causal, scores, jnp.finfo(scores.dtype).min)
        attn = jax.nn.softmax(scores, axis=-1)
        out = jnp.einsum('bhij,bjhd->bihd', attn, v)
        out = out.reshape(b, s, NH * HD)
        return out @ wo

    def _L0_ffn_ref(hidden_states, gate_w, w_gate_up, w_down, shared_w_gate_up, shared_w_down):
        import jax, jax.numpy as jnp
        import numpy as np
        HIDDEN = 512
        MOE_INTER = 128
        SHARED_INTER = 512
        NUM_EXPERTS = 16
        TOP_K = 2

        def _moe_forward(x, gate_w, w_gate_up, w_down, shared_w_gate_up, shared_w_down):
            orig_shape = x.shape
            x2 = x.reshape(-1, orig_shape[-1])
            gu_s = x2 @ shared_w_gate_up.T
            g_s, u_s = jnp.split(gu_s, 2, axis=-1)
            shared_out = jax.nn.silu(g_s) * u_s @ shared_w_down.T
            logits = x2 @ gate_w.T
            probs = jax.nn.softmax(logits, axis=-1)
            topk_vals, topk_idx = jax.lax.top_k(probs, TOP_K)
            topk_vals = topk_vals / jnp.sum(topk_vals, axis=-1, keepdims=True)
            combine = jnp.sum(jax.nn.one_hot(topk_idx, NUM_EXPERTS, dtype=x2.dtype) * topk_vals[..., None], axis=1)
            gu = jnp.einsum('th,eih->eti', x2, w_gate_up)
            g, u = jnp.split(gu, 2, axis=-1)
            act = jax.nn.silu(g) * u
            out_e = jnp.einsum('eti,ehi->eth', act, w_down)
            moe_out = jnp.einsum('eth,te->th', out_e, combine)
            return (moe_out + shared_out).reshape(orig_shape)
        return _moe_forward(hidden_states, gate_w, w_gate_up, w_down, shared_w_gate_up, shared_w_down)

    def _L1_attn_ref(hidden_states, Wq, bq, Wk, bk, Wv, bv, Wo, M, z):
        import jax, jax.numpy as jnp
        import numpy as np
        B, S, HID = (2, 512, 512)
        H, HKV, D = (32, 8, 128)
        G = H // HKV
        EPS = 1e-06

        def _reference_tuple_inner(hidden_states, Wq, bq, Wk, bk, Wv, bv, Wo, M, z):
            b, s, _ = hidden_states.shape
            q = (hidden_states @ Wq.T + bq).reshape(b, s, H, D)
            k = (hidden_states @ Wk.T + bk).reshape(b, s, HKV, D)
            v = (hidden_states @ Wv.T + bv).reshape(b, s, HKV, D)
            sig_q = jax.nn.elu(q) + 1.0
            sig_k = jax.nn.elu(k) + 1.0
            q_sel = sig_q[:, :, ::G, :]
            num = jnp.einsum('bshd,hde->bshe', q_sel, M)
            den = jnp.einsum('bshd,hd->bsh', q_sel, z)[..., None] + EPS
            retrieved = num / den
            out_heads = jnp.repeat(retrieved, G, axis=2)
            output = out_heads.reshape(b, s, H * D) @ Wo.T
            M_new = M + jnp.einsum('bshd,bshe->hde', sig_k, v)
            z_new = z + sig_k.sum(axis=(0, 1))
            return (output, M_new, z_new)
        return _reference_tuple_inner(hidden_states, Wq, bq, Wk, bk, Wv, bv, Wo, M, z)[0]

    def _L1_ffn_ref(x, gate_w, up_w, down_w, gate_scale, up_scale, down_scale):
        import jax, jax.numpy as jnp
        import numpy as np
        HIDDEN = 512
        INTER = 1376
        BATCH, SEQ = (2, 256)

        def _ternary(key, shape):
            return jax.random.randint(key, shape, -1, 2).astype(jnp.float32)
        gate = jnp.einsum('bsh,ih->bsi', x, gate_w) * gate_scale
        up = jnp.einsum('bsh,ih->bsi', x, up_w) * up_scale
        inter = jax.nn.silu(gate) * up
        out = jnp.einsum('bsi,hi->bsh', inter, down_w) * down_scale
        return out
    x = L0_attn_x
    mod = (_silu(L0_c) @ L0_wmod).reshape(L0_c.shape[0], 6, 1, -1)
    sa, ca, ga, sb, cb, gb = (mod[:, 0], mod[:, 1], mod[:, 2], mod[:, 3], mod[:, 4], mod[:, 5])
    ga = (2 * (ga >= 0) - 1) * jnp.maximum(jnp.abs(ga), 0.25)
    gb = (2 * (gb >= 0) - 1) * jnp.maximum(jnp.abs(gb), 0.25)
    h = _layernorm(x, axis=-1) * (1 + ca) + sa
    x = x + ga * _L0_attn_ref(h, L0_attn_wq, L0_attn_wk, L0_attn_wv, L0_attn_wo)
    h = _layernorm(x, axis=-1) * (1 + cb) + sb
    x = x + gb * _L0_ffn_ref(h, L0_ffn_gate_w, L0_ffn_w_gate_up, L0_ffn_w_down, L0_ffn_shared_w_gate_up, L0_ffn_shared_w_down)
    mod = (_silu(L1_c) @ L1_wmod).reshape(L1_c.shape[0], 6, 1, -1)
    sa, ca, ga, sb, cb, gb = (mod[:, 0], mod[:, 1], mod[:, 2], mod[:, 3], mod[:, 4], mod[:, 5])
    ga = (2 * (ga >= 0) - 1) * jnp.maximum(jnp.abs(ga), 0.25)
    gb = (2 * (gb >= 0) - 1) * jnp.maximum(jnp.abs(gb), 0.25)
    h = _layernorm(x, axis=-1) * (1 + ca) + sa
    x = x + ga * _L1_attn_ref(h, L1_attn_Wq, L1_attn_bq, L1_attn_Wk, L1_attn_bk, L1_attn_Wv, L1_attn_bv, L1_attn_Wo, L1_attn_M, L1_attn_z)
    h = _layernorm(x, axis=-1) * (1 + cb) + sb
    x = x + gb * _L1_ffn_ref(h, L1_ffn_gate_w, L1_ffn_up_w, L1_ffn_down_w, L1_ffn_gate_scale, L1_ffn_up_scale, L1_ffn_down_scale)
    return x

_drawn_inputs = setup_inputs


def setup_inputs(seed=0):
    import zlib

    import numpy as np

    out = dict(_drawn_inputs(seed))
    spreads = {'L1_attn_bq': (0.0, 2.0), 'L1_attn_bk': (0.0, 0.1), 'L1_attn_bv': (0.0, 0.1)}
    factors = {'L0_attn_wq': 8.0,
     'L0_attn_wk': 8.0,
     'L0_attn_wv': 6.885,
     'L0_attn_wo': 6.986,
     'L0_ffn_gate_w': 8.0,
     'L0_ffn_w_gate_up': 8.0,
     'L0_ffn_w_down': 8.0,
     'L0_ffn_shared_w_gate_up': 4.601,
     'L0_ffn_shared_w_down': 4.605,
     'L0_c': 3.716,
     'L0_wmod': 3.649,
     'L1_attn_Wq': 200.0,
     'L1_attn_Wo': 200.0,
     'L1_attn_M': 200.0,
     'L1_attn_z': 200.0,
     'L1_ffn_gate_w': 5.314,
     'L1_ffn_up_w': 5.245,
     'L1_ffn_down_w': 5.237,
     'L1_c': 5.199,
     'L1_wmod': 5.178}
    for name, (base, spread) in spreads.items():
        noise = np.random.default_rng([zlib.crc32(name.encode()), seed]).standard_normal(out[name].shape)
        drawn = base * np.exp(spread * noise) if base else spread * noise
        out[name] = jnp.asarray(drawn.astype(out[name].dtype))
    for name, factor in factors.items():
        out[name] = (out[name] * factor).astype(out[name].dtype)
    return out
```

```python
from contextlib import ExitStack

import numpy as np

import concourse.bass as bass
from concourse import mybir

FP = mybir.dt.float32
FR = mybir.dt.float32r
BF = mybir.dt.bfloat16
U32 = mybir.dt.uint32
ALU = mybir.AluOpType
ACT = mybir.ActivationFunctionType
AX = mybir.AxisListType

P = 128
D = 512
KC = D // P
B, S = 4, 256
T = B * S
HALF = T // 2
TH = HALF // P
NH, NKV, HD = 32, 8, 16
REP = NH // NKV
VW = HD + 1
QKV = NH * HD + NH * HD + NKV * HD
E = 16
SHARED = 4
H1 = 8
G1 = 4
FF = 1376
FFN_W = KC * 2 * P + D
UP_W = KC * 2 * P
MZ = KC * P
MZ_W = P + 2
HEAD_W = KC * P + MZ_W + G1 * D
EPS = 1e-5
DEN_EPS = 1e-6
NEG = -1e30
MOD_CH = 6

FFN0, HEADS, FFN1 = range(3)
N_STEPS = {FFN0: SHARED + E, HEADS: H1, FFN1: (FF + P - 1) // P}
SEGMENTS = []
_at = 0
for _kind in (FFN0, HEADS, FFN1):
    for _half in range(2):
        SEGMENTS.append((_kind, _half, _at, N_STEPS[_kind]))
        _at += N_STEPS[_kind]
HEAD0 = 2 * N_STEPS[FFN0]
LAST_STEP = _at - 1
UNITS = 2 * NKV


def steps(eng, base, n, body):
    pairs = (n - 3) // 2
    body(base, 0, 0)
    body(base + 1, 0, 1)
    with eng.Fori(0, pairs) as i:
        body(base + 2, i, None)
        body(base + 3, i, None)
    for s in range(2 + 2 * pairs, n):
        body(base + s, 0, s)


def build(nc, d):
    ctx = ExitStack()
    with ctx:
        def sem(name):
            return ctx.enter_context(nc.semaphore(name))

        def sb(name, shape, dt=FP, where=ctx):
            return where.enter_context(nc.sbuf_tensor(name, shape, dt))

        x = sb("x", [P, T // P, D])
        act_hi = sb("act_hi", [P, KC, T], FR)
        act_lo = sb("act_lo", [P, KC, T], FR)
        wmod = sb("wmod", [P, 3, KC, D])
        gates = sb("gates", [P, 2, B, D])
        xn = sb("xn", [P, TH, D])
        h32 = sb("h32", [P, 2, KC, S])
        ident = sb("ident", [P, P])
        ident_bf = sb("ident_bf", [P, P], BF)
        causal = sb("causal", [P, P])
        causal_bf = sb("causal_bf", [P, P], BF)
        cond = sb("cond", [P, 2, KC, B])
        silu_c = sb("silu_c", [P, 2, KC, B])
        modc = sb("modc", [P, 2, MOD_CH * KC, B])
        sign = sb("sign", [P, KC * B])
        mag = sb("mag", [P, KC * B])
        stats = sb("stats", [P, TH, 6])
        mv = sb("mv", [P, TH, 2])
        var_eps = sb("var_eps", [P, TH])
        rstd = sb("rstd", [P, TH])
        minus_half = sb("minus_half", [P, TH])
        scales = sb("scales", [P, 3])
        one = sb("one", [P, 1])
        even_mask = sb("even_mask", [P, 1])
        odd_mask = sb("odd_mask", [P, 1])
        row_u = sb("row_u", [P, 1], U32)
        bq = sb("bq", [P, H1])
        iota_e = sb("iota_e", [P, E])
        ones_row = sb("ones_row", [SHARED, T])
        gw = sb("gw", [P, KC, E])
        gw_hi = sb("gw_hi", [P, KC, E], FR)
        gw_lo = sb("gw_lo", [P, KC, E], FR)

        early = ExitStack()
        wqkv_hi = sb("wqkv_hi", [P, KC, QKV], FR, early)
        wqkv_lo = sb("wqkv_lo", [P, KC, QKV], FR, early)
        wo_hi = sb("wo_hi", [P, KC, D], FR, early)
        wo_lo = sb("wo_lo", [P, KC, D], FR, early)
        loading = ExitStack()
        wqkv_in = sb("wqkv_in", [P, KC, QKV], FP, loading)
        wo_in = sb("wo_in", [P, KC, D], FP, loading)
        loading.close()
        qT = sb("qT", [P, KC, S], FP, early)
        k2 = sb("k2", [P, KC, 2, S], FP, early)
        vT = sb("vT", [P, S], FP, early)
        v1 = sb("v1", [P, 2, NKV, VW], FP, early)
        shifted = sb("shifted", [P, 2, REP, S], FP, early)
        probsT = sb("probsT", [P, 2, 2, REP * P], FP, early)
        row_max = sb("row_max", [P, 2, REP], FP, early)
        rsum = sb("rsum", [P, 2, 16], FP, early)
        heads_out = sb("heads_out", [P, 2, D], FP, early)
        early.close()

        w_in = sb("w_in", [P, 2, HEAD_W])
        w_hi = sb("w_hi", [P, 2, FFN_W], FR)
        w_lo = sb("w_lo", [P, 2, FFN_W], FR)
        silu = sb("silu", [P, 2, HALF])
        inner = sb("inner", [P, 2, HALF])
        inner_hi = sb("inner_hi", [P, 2, HALF], FR)
        inner_lo = sb("inner_lo", [P, 2, HALF], FR)
        share = sb("share", [P, 2, HALF])
        below = sb("below", [P, HALF])
        sig = sb("sig", [P, HALF])
        sig_hi = sb("sig_hi", [P, HALF], FR)
        sig_lo = sb("sig_lo", [P, HALF], FR)
        den = sb("den", [P, 2, 2])
        rden = sb("rden", [P, 2, 2])
        gate1b = sb("gate1b", [P, B, D])
        logits = sb("logits", [P, TH, E])
        top8 = sb("top8", [P, TH, 8])
        top_at = sb("top_at", [P, TH, 8], U32)
        top_f = sb("top_f", [P, TH, 2])
        gap = sb("gap", [P, TH])
        e2 = sb("e2", [P, TH])
        w1 = sb("w1", [P, TH])
        w2 = sb("w2", [P, TH])
        pick1 = sb("pick1", [P, TH, E])
        pick2 = sb("pick2", [P, TH, E])
        combT = sb("combT", [E, HALF])

        ps = ctx.enter_context(nc.psum_tensor("ps", [P, 8, 512], FP))

        x_in = [sem(f"x_in{h}") for h in range(2)]
        small_in = sem("small_in")
        wqkv_arrived = sem("wqkv_arrived")
        wo_arrived = sem("wo_arrived")
        wmod_in = [sem(f"wmod_in{r}") for r in range(3)]
        w_arrived = [sem(f"w_arrived{r}") for r in range(2)]
        ones_stored = sem("ones_stored")
        comb_stored = sem("comb_stored")
        share_in = [sem(f"share_in{r}") for r in range(2)]
        out_stored = sem("out_stored")
        const_zero = sem("const_zero")
        const_ready = sem("const_ready")
        const_bf = sem("const_bf")
        ones_ready = sem("ones_ready")
        silu_c_done = sem("silu_c_done")
        mod_mm = sem("mod_mm")
        mod_ev = sem("mod_ev")
        mod_tmp = sem("mod_tmp")
        gate_mm = sem("gate_mm")
        gate_ev = sem("gate_ev")
        ln_tmp = sem("ln_tmp")
        ln_stats = sem("ln_stats")
        ln_eps = sem("ln_eps")
        ln_rstd = sem("ln_rstd")
        ln_xn = sem("ln_xn")
        turned = sem("turned")
        h32_done = sem("h32_done")
        act_hi_done = sem("act_hi_done")
        act_lo_done = sem("act_lo_done")
        gw_split = sem("gw_split")
        wqkv_hi_done = sem("wqkv_hi_done")
        wqkv_lo_done = sem("wqkv_lo_done")
        q_mm = sem("q_mm")
        k_mm = sem("k_mm")
        v_mm = sem("v_mm")
        q_ev = sem("q_ev")
        k_ev = sem("k_ev")
        vT_ev = sem("vT_ev")
        v_turned = sem("v_turned")
        v_ev = sem("v_ev")
        scored = sem("scored")
        max_done = sem("max_done")
        shift_done = sem("shift_done")
        probs_turned = sem("probs_turned")
        exp_done = sem("exp_done")
        pv_done = sem("pv_done")
        rsum_done = sem("rsum_done")
        heads_ev = sem("heads_ev")
        heads_turned = sem("heads_turned")
        heads_hi = sem("heads_hi")
        heads_lo = sem("heads_lo")
        proj_done = sem("proj_done")
        addend_done = sem("addend_done")
        resid_done = sem("resid_done")
        logits_mm = sem("logits_mm")
        router = sem("router")
        gap_done = sem("gap_done")
        e2_done = sem("e2_done")
        comb_done = sem("comb_done")
        comb_turned = sem("comb_turned")
        comb_ev = sem("comb_ev")
        group_pair = sem("group_pair")
        group_sum = sem("group_sum")
        up_hi = sem("up_hi")
        up_lo = sem("up_lo")
        down_hi = sem("down_hi")
        down_lo = sem("down_lo")
        up_done = sem("up_done")
        down_done = sem("down_done")
        silu_done = sem("silu_done")
        scaled_done = sem("scaled_done")
        inner_done = sem("inner_done")
        inner_hi_done = sem("inner_hi_done")
        inner_lo_done = sem("inner_lo_done")
        q1_done = sem("q1_done")
        below_done = sem("below_done")
        above_done = sem("above_done")
        elu_done = sem("elu_done")
        sig_done = sem("sig_done")
        sig_hi_done = sem("sig_hi_done")
        sig_lo_done = sem("sig_lo_done")
        den_done = sem("den_done")
        rden_done = sem("rden_done")
        ret_done = sem("ret_done")
        ret_turned = sem("ret_turned")

        block = ctx.enter_context(nc.Block())

        def half_tiles(half):
            return range(half * TH, (half + 1) * TH)

        def kind_of(a):
            return next(k for k, _, base, n in SEGMENTS if base <= a < base + n)

        def ffn_count(a):
            return a if a < HEAD0 else a - 2 * H1

        def chunk_of(a, i):
            kind, _, base, _ = next(s for s in SEGMENTS if s[2] <= a < s[2] + s[3])
            return kind, a - base + 2 * i

        @block.sync
        def _(sp):
            for l in range(2):
                sp.dma_start(cond[:, l], d["cond"][l]).then_inc(small_in, 16)
            for j in range(2):
                sp.dma_start(wmod[:, j], d["wmod"][0, j]).then_inc(wmod_in[j], 16)
            for h in range(2):
                sp.dma_start(x[:, h * TH:(h + 1) * TH], d["x"][:, h * TH:(h + 1) * TH]).then_inc(x_in[h], 16)
            sp.dma_start(wqkv_in[:], d["wqkv"]).then_inc(wqkv_arrived, 16)
            sp.dma_start(gw[:], d["gate_w"]).then_inc(small_in, 16)
            sp.dma_start(bq[:], d["bq"]).then_inc(small_in, 16)
            sp.dma_start(scales[:], d["scales"].to_broadcast([P, 3])).then_inc(small_in, 16)
            sp.dma_start(wmod[:, 2], d["wmod"][0, 2]).then_inc(wmod_in[2], 16)
            sp.dma_start(wo_in[:], d["wo"]).then_inc(wo_arrived, 16)
            sp.wait_ge(ones_ready, 1)
            sp.dma_start(d["comb"][0:SHARED, :], ones_row[:]).then_inc(ones_stored, 16)
            for j in range(3, 2 * MOD_CH):
                sp.wait_ge(mod_mm, j - 2)
                sp.dma_start(wmod[:, j % 3], d["wmod"][j // MOD_CH, j % MOD_CH]).then_inc(wmod_in[j % 3], 16)

            def load(a, i, s):
                if a == 0:
                    sp.wait_ge(proj_done, 2)
                if a >= 2:
                    sp.wait_ge(down_lo, a - 1 + 2 * i)
                kind, c = chunk_of(a, i)
                width = HEAD_W if kind == HEADS else FFN_W
                sp.dma_start(w_in[:, a % 2, 0:width], d["chunks"][kind][c]).then_inc(w_arrived[a % 2], 16)

            for _, _, base, n in SEGMENTS:
                steps(sp, base, n, load)
            for h in range(2):
                sp.wait_ge(resid_done, 7 + h)
                sp.dma_start(d["out"][:, h * TH:(h + 1) * TH], x[:, h * TH:(h + 1) * TH]).then_inc(out_stored, 16)
            sp.wait_ge(out_stored, 32)

        @block.gpsimd
        def _(pool):
            g = nc.gpsimd
            g.memset(ident[:], 0.0).then_inc(const_zero, 1)
            g.memset(causal[:], 0.0).then_inc(const_zero, 1)
            g.memset(minus_half[:], -0.5).then_inc(const_zero, 1)
            g.memset(one[:], 1.0).then_inc(const_zero, 1)
            g.memset(ones_row[:], 1.0).then_inc(ones_ready, 1)
            g.iota(iota_e[:], pattern=[[1, E]], base=0, channel_multiplier=0,
                   allow_small_or_imprecise_dtypes=True).then_inc(const_zero, 1)
            pool.wait_ge(const_zero, 5)
            g.affine_select(out=ident[:], in_=ident[:], compare_op=ALU.not_equal, fill=1.0,
                            base=0, pattern=[[-1, P]], channel_multiplier=1).then_inc(const_ready, 1)
            g.affine_select(out=causal[:], in_=causal[:], compare_op=ALU.is_ge, fill=NEG,
                            base=0, pattern=[[-1, P]], channel_multiplier=1).then_inc(const_ready, 1)
            g.iota(row_u[:], pattern=[[0, 1]], base=0, channel_multiplier=1).then_inc(const_ready, 1)

            def ln_root(n):
                pool.wait_ge(ln_stats, n + 1)
                g.tensor_scalar(var_eps[:], mv[:, :, 1], EPS, 1.0, ALU.add, ALU.mult).then_inc(ln_eps, 1)
                pool.wait_ge(ln_eps, n + 1)
                g.tensor_tensor(rstd[:], var_eps[:], minus_half[:], ALU.pow).then_inc(ln_rstd, 1)

            def rest_of_act(m):
                b = m % B
                pool.wait_ge(act_hi_done, m + 1)
                cols = slice(b * S, (b + 1) * S)
                g.tensor_tensor(act_lo[:, :, cols], h32[:, m % 2], act_hi[:, :, cols].bitcast(FP),
                                ALU.subtract).then_inc(act_lo_done, 1)

            def rest_of_weights(a, i):
                kind = kind_of(a)
                r = a % 2
                if kind == HEADS:
                    q = MZ + MZ_W
                    k = a - HEAD0
                    pool.wait_ge(w_arrived[r], 16 * (a // 2 + 1) + 16 * i)
                    g.tensor_tensor(w_in[:, r, q:q + 2 * D], w_in[:, r, q:q + 2 * D],
                                    w_in[:, r, q + 2 * D:q + 4 * D], ALU.add).then_inc(group_pair, 1)
                    pool.wait_ge(group_pair, k + 1 + 2 * i)
                    g.tensor_tensor(w_in[:, r, q:q + D], w_in[:, r, q:q + D],
                                    w_in[:, r, q + D:q + 2 * D], ALU.add).then_inc(group_sum, 1)
                    down, used = q, MZ + MZ_W
                else:
                    down, used = UP_W, UP_W
                pool.wait_ge(up_hi, a + 1 + 2 * i)
                g.tensor_tensor(w_lo[:, r, 0:used], w_in[:, r, 0:used], w_hi[:, r, 0:used].bitcast(FP),
                                ALU.subtract).then_inc(up_lo, 1)
                pool.wait_ge(down_hi, a + 1 + 2 * i)
                g.tensor_tensor(w_lo[:, r, UP_W:UP_W + D], w_in[:, r, down:down + D],
                                w_hi[:, r, UP_W:UP_W + D].bitcast(FP), ALU.subtract).then_inc(down_lo, 1)

            for n in range(2):
                ln_root(n)
                rest_of_act(2 * n)
                rest_of_act(2 * n + 1)
            ln_root(2)
            rest_of_act(4)
            rest_of_act(5)
            ln_root(3)
            rest_of_weights(0, 0)
            for seg, (kind, half, base, n) in enumerate(SEGMENTS):
                def body(a, i, s):
                    if a < LAST_STEP:
                        rest_of_weights(a + 1, i)
                    if s in (0, 1) and seg < 5:
                        rest_of_act(6 + 2 * seg + s)

                steps(pool, base, n, body)
                if seg < 4:
                    ln_root(4 + seg)

        @block.scalar
        def _(act):
            a_ = nc.scalar
            act.wait_ge(small_in, 5 * 16)
            a_.activation(silu_c[:], cond[:], ACT.Silu).then_inc(silu_c_done, 1)
            a_.activation(gw_hi[:], gw[:], ACT.Copy).then_inc(gw_split, 1)
            act.wait_ge(wqkv_arrived, 16)
            a_.activation(wqkv_hi[:], wqkv_in[:], ACT.Copy).then_inc(wqkv_hi_done, 1)

            def split_act(m):
                b = m % B
                act.wait_ge(h32_done, m + 1)
                a_.activation(act_hi[:, :, b * S:(b + 1) * S], h32[:, m % 2], ACT.Copy).then_inc(act_hi_done, 1)

            for m in range(4):
                split_act(m)
            act.wait_ge(wo_arrived, 16)
            a_.activation(wo_hi[:], wo_in[:], ACT.Copy).then_inc(wqkv_hi_done, 1)
            act.wait_ge(wqkv_lo_done, 2)
            with act.Fori(0, B) as b:
                act.wait_ge(k_mm, b + 1)
                kps = ps[:, 2:4, :].rearrange("p c (m s) -> p (c m) s", s=S)
                a_.activation(k2[:, :, 0, :], kps, ACT.Copy, scale=even_mask[:, 0:1])
                a_.activation(k2[:, :, 1, :], kps, ACT.Copy, scale=odd_mask[:, 0:1]).then_inc(k_ev, 1)
                for n in range(UNITS):
                    nj = n // NKV + 1
                    act.wait_ge(probs_turned, UNITS * b + (n + 1))
                    if n >= 2:
                        act.wait_ge(pv_done, UNITS * b + (n - 1))
                    a_.activation(probsT[:, n % 2, 0:nj, :], ps[:, 4:4 + nj, :], ACT.Exp,
                                  scale=float(HD) ** -0.5).then_inc(exp_done, 1)
                act.wait_ge(heads_turned, b + 1)
                a_.activation(act_hi[:, :, bass.ts(b, S)],
                              ps[:, 0:2, :].rearrange("p c (m s) -> p (c m) s", s=S),
                              ACT.Copy).then_inc(heads_hi, 1)

            def gate_rows(c):
                dst = gate1b if c == 3 else gates[:, c % 2]
                act.wait_ge(gate_mm, c + 1)
                if c == 2:
                    act.wait_ge(resid_done, 2)
                a_.activation(dst[:] if c == 3 else dst, ps[:, 4:8, :], ACT.Copy).then_inc(gate_ev, 1)

            gate_rows(0)
            gate_rows(1)
            split_act(4)
            split_act(5)
            gate_rows(2)
            gate_rows(3)

            def split_up(a, i):
                kind, r = kind_of(a), a % 2
                used = MZ + MZ_W if kind == HEADS else UP_W
                act.wait_ge(w_arrived[r], 16 * (a // 2 + 1) + 16 * i)
                if a >= 2:
                    act.wait_ge(up_done, a - 1 + 2 * i)
                a_.activation(w_hi[:, r, 0:used], w_in[:, r, 0:used], ACT.Copy).then_inc(up_hi, 1)

            def split_down(a, i):
                kind, r = kind_of(a), a % 2
                at = MZ + MZ_W if kind == HEADS else UP_W
                if kind == HEADS:
                    act.wait_ge(group_sum, a - HEAD0 + 1 + 2 * i)
                if a >= 2:
                    act.wait_ge(down_done, a - 1 + 2 * i)
                a_.activation(w_hi[:, r, UP_W:UP_W + D], w_in[:, r, at:at + D], ACT.Copy).then_inc(down_hi, 1)

            def split_inner(a, i):
                if a >= 2:
                    act.wait_ge(down_done, a - 1 + 2 * i)
                a_.activation(inner_hi[:, a % 2], inner[:, a % 2], ACT.Copy).then_inc(inner_hi_done, 1)

            def route(h):
                act.wait_ge(gap_done, h + 1)
                a_.activation(e2[:], gap[:], ACT.Exp).then_inc(e2_done, 1)
                act.wait_ge(comb_turned, h + 1)
                if h == 1:
                    act.wait_ge(comb_stored, 16)
                a_.activation(combT[:], ps[0:E, 3, :], ACT.Copy).then_inc(comb_ev, 1)
                act.wait_ge(comb_ev, h + 1)
                act.dma_start(d["comb"][SHARED:SHARED + E, h * HALF:(h + 1) * HALF], combT[:]).then_inc(comb_stored, 16)
                act.wait_ge(comb_stored, 16 * (h + 1))

            def ffn_step(a, i, half, layer0):
                r = a % 2
                if layer0:
                    c = a - half * N_STEPS[FFN0] + 2 * i
                    if a >= 2:
                        act.wait_ge(inner_done, a - 1 + 2 * i)
                    act.dma_start(share[:, r], d["comb"][bass.ds(c, 1), half * HALF:(half + 1) * HALF]
                                  .to_broadcast([P, HALF])).then_inc(share_in[r], 16)
                k = ffn_count(a)
                act.wait_ge(up_done, a + 1 + 2 * i)
                if k >= 2:
                    act.wait_ge(inner_done, k - 1 + 2 * i)
                gate_scale = one[:, 0:1] if layer0 else scales[:, 0:1]
                a_.activation(silu[:, r], ps[:, 2 * r, :], ACT.Silu, scale=gate_scale).then_inc(silu_done, 1)
                act.wait_ge(inner_done, k + 1 + 2 * i)
                split_inner(a, i)

            def head_step(a, i, s):
                r, k = a % 2, a - HEAD0
                if s != 0:
                    act.wait_ge(ret_turned, retrieved_before(a) + 2 * i)
                    act.wait_ge(down_done, a - 2 + 2 * i)
                    a_.activation(inner_hi[:, 1 - r], ps[:, 2 * (1 - r), :], ACT.Copy).then_inc(inner_hi_done, 1)
                act.wait_ge(below_done, k + 1 + 2 * i)
                if k >= 1:
                    act.wait_ge(sig_done, k + 2 * i)
                a_.activation(silu[:, 0], below[:], ACT.Exp).then_inc(elu_done, 1)
                act.wait_ge(sig_done, k + 1 + 2 * i)
                if k >= 1:
                    act.wait_ge(up_done, a + 2 * i)
                a_.activation(sig_hi[:], sig[:], ACT.Copy).then_inc(sig_hi_done, 1)

            def retrieved_before(a):
                return a - HEAD0

            def last_retrieved(a):
                act.wait_ge(ret_turned, a - HEAD0 + 1)
                act.wait_ge(down_done, a - 1)
                a_.activation(inner_hi[:, a % 2], ps[:, 2 * (a % 2), :], ACT.Copy).then_inc(inner_hi_done, 1)

            split_up(0, 0)
            split_down(0, 0)
            act.wait_ge(ones_stored, 16)
            for seg, (kind, half, base, n) in enumerate(SEGMENTS):
                if kind == FFN0:
                    route(half)

                def body(a, i, s):
                    if a < LAST_STEP:
                        split_up(a + 1, i)
                    if kind == HEADS:
                        head_step(a, i, s)
                    else:
                        ffn_step(a, i, half, kind == FFN0)
                    if a < LAST_STEP:
                        split_down(a + 1, i)
                    if s in (0, 1) and seg < 5:
                        split_act(6 + 2 * seg + s)

                steps(act, base, n, body)
                if kind == HEADS:
                    last_retrieved(base + n - 1)

        @block.vector
        def _(dve):
            v = nc.vector
            links = [0]

            def link(ins):
                links[0] += 1
                ins.then_inc(router, 1)
                dve.wait_ge(router, links[0])

            dve.wait_ge(const_ready, 3)
            v.tensor_copy(ident_bf[:], ident[:])
            v.tensor_copy(causal_bf[:], causal[:]).then_inc(const_bf, 1)
            link(v.tensor_scalar(row_u[:], row_u[:], 16, None, ALU.bitwise_and))
            link(v.tensor_copy(even_mask[:], row_u[:]))
            link(v.tensor_scalar(odd_mask[:], even_mask[:], 1.0 / 16, None, ALU.mult))
            link(v.tensor_scalar(even_mask[:], odd_mask[:], -1.0, 1.0, ALU.mult, ALU.add))
            dve.wait_ge(gw_split, 1)
            v.tensor_tensor(gw_lo[:], gw[:], gw_hi[:].bitcast(FP), ALU.subtract).then_inc(gw_split, 1)

            def mod_columns(l, part):
                n = KC
                if part == 0:
                    dve.wait_ge(mod_mm, MOD_CH * l + 2)
                    v.tensor_copy(modc[:, l, 0:n, :], ps[:, 6, 0:n * B].rearrange("p (m b) -> p m b", b=B))
                    v.tensor_scalar(modc[:, l, n:2 * n, :], ps[:, 6, n * B:2 * n * B].rearrange("p (m b) -> p m b", b=B),
                                    1.0, None, ALU.add).then_inc(mod_ev, 1)
                    return
                dve.wait_ge(mod_mm, MOD_CH * (l + 1))
                link(v.tensor_copy(modc[:, l, 2 * n:6 * n, :],
                                   ps[:, 7, 0:4 * n * B].rearrange("p (m b) -> p m b", b=B)))
                link(v.tensor_scalar(modc[:, l, 4 * n:5 * n, :], modc[:, l, 4 * n:5 * n, :], 1.0, None, ALU.add))
                for q in (2, 5):
                    gate = modc[:, l, q * n:(q + 1) * n, :].rearrange("p m b -> p (m b)")
                    link(v.tensor_scalar(sign[:], gate, 0.0, 2.0, ALU.is_ge, ALU.mult))
                    link(v.scalar_tensor_tensor(mag[:], sign[:], -1.0, gate, ALU.add, ALU.mult))
                    link(v.tensor_scalar(mag[:], mag[:], 0.25, None, ALU.max))
                    ins = v.scalar_tensor_tensor(gate, sign[:], -1.0, mag[:], ALU.add, ALU.mult)
                    if q == 2:
                        link(ins)
                ins.then_inc(mod_ev, 1)

            def norm(n):
                tiles = half_tiles(n % 2)
                if n < 2:
                    dve.wait_ge(x_in[n % 2], 16)
                for j, t in enumerate(tiles):
                    v.bn_stats(stats[:, j, :], x[:, t, :]).then_inc(ln_tmp, 1)
                dve.wait_ge(ln_tmp, TH * (n + 1))
                for j in range(TH):
                    v.bn_aggr(mv[:, j, :], stats[:, j, :]).then_inc(ln_stats, 1) if j == TH - 1 else \
                        v.bn_aggr(mv[:, j, :], stats[:, j, :])
                dve.wait_ge(ln_stats, n + 1)
                dve.wait_ge(ln_rstd, n + 1)
                for j, t in enumerate(tiles):
                    ins = v.tensor_scalar(xn[:, j, :], x[:, t, :], mv[:, j, 0:1], rstd[:, j:j + 1],
                                          ALU.subtract, ALU.mult)
                ins.then_inc(ln_xn, 1)

            def modulate(m, banks):
                ln, b = m // B, m % B
                l, q = ln // 2, 3 * (ln % 2)
                dve.wait_ge(turned, m + 1)
                if m >= 2:
                    dve.wait_ge(act_lo_done, m - 1)
                for k in range(KC):
                    src = ps[:, banks + k // 2, (k % 2) * S:(k % 2 + 1) * S]
                    ins = v.tensor_scalar(h32[:, m % 2, k, :], src, modc[:, l, (q + 1) * KC + k, b:b + 1],
                                          modc[:, l, q * KC + k, b:b + 1], ALU.mult, ALU.add)
                ins.then_inc(h32_done, 1)

            def residual(seq, gate, down_scale, bank):
                for j, t in enumerate(half_tiles(seq % 2)):
                    ins = v.scalar_tensor_tensor(xn[:, j, :], ps[:, bank + j, :], down_scale,
                                                 gate[:, t // 2, :], ALU.mult, ALU.mult)
                ins.then_inc(addend_done, 1)
                dve.wait_ge(addend_done, seq + 1)
                tiles = half_tiles(seq % 2)
                v.tensor_tensor(x[:, tiles[0]:tiles[0] + TH, :], x[:, tiles[0]:tiles[0] + TH, :], xn[:],
                                ALU.add).then_inc(resid_done, 1)
                dve.wait_ge(resid_done, seq + 1)

            mod_columns(0, 0)
            dve.wait_ge(mod_ev, 1)
            norm(0)
            modulate(0, 0)
            modulate(1, 2)
            norm(1)
            modulate(2, 0)
            modulate(3, 2)
            dve.wait_ge(wqkv_hi_done, 1)
            v.tensor_tensor(wqkv_lo[:], wqkv_in[:], wqkv_hi[:].bitcast(FP), ALU.subtract).then_inc(wqkv_lo_done, 1)
            dve.wait_ge(wqkv_hi_done, 2)
            v.tensor_tensor(wo_lo[:], wo_in[:], wo_hi[:].bitcast(FP), ALU.subtract).then_inc(wqkv_lo_done, 1)
            dve.wait_ge(wqkv_lo_done, 2)
            v.memset(v1[:, :, :, HD:VW], 1.0)

            with dve.Fori(0, B) as b:
                dve.wait_ge(q_mm, b + 1)
                v.tensor_copy(qT[:], ps[:, 0:2, :].rearrange("p c (m s) -> p (c m) s", s=S)).then_inc(q_ev, 1)
                dve.wait_ge(v_mm, b + 1)
                v.tensor_copy(vT[:], ps[:, 4, 0:S]).then_inc(vT_ev, 1)
                dve.wait_ge(v_turned, b + 1)
                v.tensor_copy(v1[:, :, :, 0:HD], ps[:, 5, 0:S].rearrange("p (j g e) -> p j g e", j=2, e=HD)).then_inc(v_ev, 1)

                def normalise(q):
                    iblk, bank = q // 2, 6 + q % 2
                    dve.wait_ge(pv_done, UNITS * b + (4 * q + 4))
                    o = ps[:, bank, 0:16 * VW].rearrange("p (h e) -> p h e", e=VW)
                    v.reciprocal(rsum[:, q % 2, :], o[:, :, HD]).then_inc(rsum_done, 1)
                    dve.wait_ge(rsum_done, 4 * b + (q + 1))
                    dst = heads_out[:, iblk, (q % 2) * 256:(q % 2 + 1) * 256].rearrange("p (h e) -> p h e", e=HD)
                    v.tensor_tensor(dst, o[:, :, 0:HD], rsum[:, q % 2, :].unsqueeze(2).to_broadcast([P, 16, HD]),
                                    ALU.mult).then_inc(heads_ev, 1)

                for n in range(UNITS):
                    iblk, r = n // NKV, n % 2
                    w = P * (iblk + 1)
                    sc = ps[:, 2 * r:2 * r + 2, 0:2 * w].rearrange("p c (h s) -> p c h s", h=2)
                    dve.wait_ge(scored, UNITS * b + (n + 1))
                    v.tensor_reduce(row_max[:, r, :].rearrange("p (c h) -> p c h", c=2), sc, AX.X, ALU.max).then_inc(max_done, 1)
                    dve.wait_ge(max_done, UNITS * b + (n + 1))
                    if n >= 2:
                        dve.wait_ge(probs_turned, UNITS * b + (n - 1))
                    v.tensor_tensor(shifted[:, r, :, 0:w].rearrange("p (c h) s -> p c h s", c=2), sc,
                                    row_max[:, r, :].rearrange("p (c h) -> p c h", c=2).unsqueeze(3)
                                    .to_broadcast([P, 2, 2, w]), ALU.subtract).then_inc(shift_done, 1)
                    if n >= 6 and (n - 6) % 4 == 0:
                        normalise((n - 6) // 4)
                normalise(3)
                dve.wait_ge(heads_hi, b + 1)
                v.tensor_tensor(act_lo[:, :, bass.ts(b, S)],
                                ps[:, 0:2, :].rearrange("p c (m s) -> p (c m) s", s=S),
                                act_hi[:, :, bass.ts(b, S)].bitcast(FP), ALU.subtract).then_inc(heads_lo, 1)

            mod_columns(0, 1)
            dve.wait_ge(proj_done, 1)
            dve.wait_ge(gate_ev, 2)
            residual(0, gates[:, 0], 1.0, 4)
            norm(2)
            modulate(4, 4)
            modulate(5, 6)
            dve.wait_ge(proj_done, 2)
            residual(1, gates[:, 0], 1.0, 0)
            norm(3)
            mod_columns(1, 0)
            mod_columns(1, 1)

            def route(h):
                dve.wait_ge(logits_mm, h + 1)
                link(v.tensor_copy(logits[:], ps[:, 2, 0:TH * E].rearrange("p (t e) -> p t e", e=E)))
                for j in range(TH):
                    link(v.max(top8[:, j, :], logits[:, j, :]))
                    link(v.max_index(top_at[:, j, :], top8[:, j, :], logits[:, j, :]))
                v.tensor_tensor(gap[:], top8[:, :, 1], top8[:, :, 0], ALU.subtract).then_inc(gap_done, 1)
                link(v.tensor_copy(top_f[:], top_at[:, :, 0:2]))
                dve.wait_ge(e2_done, h + 1)
                link(v.tensor_scalar(w2[:], e2[:], 1.0, None, ALU.add))
                link(v.reciprocal(w1[:], w2[:]))
                link(v.tensor_tensor(w2[:], w1[:], e2[:], ALU.mult))
                for j in range(TH):
                    v.tensor_scalar(pick1[:, j, :], iota_e[:], top_f[:, j, 0:1], w1[:, j:j + 1], ALU.is_equal, ALU.mult)
                    ins = v.tensor_scalar(pick2[:, j, :], iota_e[:], top_f[:, j, 1:2], w2[:, j:j + 1], ALU.is_equal, ALU.mult)
                link(ins)
                v.tensor_tensor(pick1[:], pick1[:], pick2[:], ALU.add).then_inc(comb_done, 1)

            def rest_of_inner(a, i):
                dve.wait_ge(inner_hi_done, a + 1 + 2 * i)
                if a >= 2:
                    dve.wait_ge(down_done, a - 1 + 2 * i)

            def ffn_step(a, i, layer0):
                r = a % 2
                dve.wait_ge(silu_done, ffn_count(a) + 1 + 2 * i)
                up_scale = 1.0 if layer0 else scales[:, 1:2]
                dst = inner[:, r]
                ins = v.scalar_tensor_tensor(dst, ps[:, 2 * r + 1, :], up_scale, silu[:, r], ALU.mult, ALU.mult)
                if layer0:
                    ins.then_inc(scaled_done, 1)
                    dve.wait_ge(scaled_done, a + 1 + 2 * i)
                    dve.wait_ge(share_in[r], 16 * (a // 2 + 1) + 16 * i)
                    ins = v.tensor_tensor(dst, inner[:, r], share[:, r], ALU.mult)
                ins.then_inc(inner_done, 1)
                rest_of_inner(a, i)
                v.tensor_tensor(inner_lo[:, r], inner[:, r], inner_hi[:, r].bitcast(FP),
                                ALU.subtract).then_inc(inner_lo_done, 1)

            def rest_of_retrieved(a, i):
                rest_of_inner(a, i)
                v.tensor_tensor(inner_lo[:, a % 2], ps[:, 2 * (a % 2), :], inner_hi[:, a % 2].bitcast(FP),
                                ALU.subtract).then_inc(inner_lo_done, 1)

            def head_step(a, i, s):
                r, k = a % 2, a - HEAD0
                if s != 0:
                    rest_of_retrieved(a - 1, i)
                dve.wait_ge(q1_done, k + 1 + 2 * i)
                if k >= 1:
                    dve.wait_ge(elu_done, k + 2 * i)
                bias = bq[:, bass.ds(k % H1 + 2 * i, 1)]
                v.tensor_scalar(below[:], ps[:, 2 * r, :], bias, 0.0, ALU.add, ALU.min).then_inc(below_done, 1)
                v.tensor_scalar(silu[:, 1], ps[:, 2 * r, :], bias, 0.0, ALU.add, ALU.max).then_inc(above_done, 1)
                dve.wait_ge(above_done, k + 1 + 2 * i)
                dve.wait_ge(elu_done, k + 1 + 2 * i)
                if k >= 1:
                    dve.wait_ge(sig_lo_done, k + 2 * i)
                v.tensor_tensor(sig[:], silu[:, 0], silu[:, 1], ALU.add).then_inc(sig_done, 1)
                dve.wait_ge(sig_hi_done, k + 1 + 2 * i)
                v.tensor_tensor(sig_lo[:], sig[:], sig_hi[:].bitcast(FP), ALU.subtract).then_inc(sig_lo_done, 1)
                dve.wait_ge(up_done, a + 1 + 2 * i)
                nd = [ps[:, c, 0:2 * MZ_W].rearrange("p (t w) -> p t w", w=MZ_W) for c in (1, 3)]
                for c in range(2):
                    ins = v.tensor_scalar(den[:, c, :], nd[c][:, :, P], DEN_EPS, None, ALU.add)
                ins.then_inc(den_done, 1)
                dve.wait_ge(den_done, k + 1 + 2 * i)
                v.reciprocal(rden[:], den[:]).then_inc(rden_done, 1)
                dve.wait_ge(rden_done, k + 1 + 2 * i)
                for c in range(2):
                    ins = v.tensor_tensor(inner[:, r, c * S:(c + 1) * S].rearrange("p (t e) -> p t e", t=2),
                                          nd[c][:, :, 0:P], rden[:, c, :].unsqueeze(2).to_broadcast([P, 2, P]), ALU.mult)
                ins.then_inc(ret_done, 1)

            for seg, (kind, half, base, n) in enumerate(SEGMENTS):
                if kind == FFN0:
                    route(half)

                def body(a, i, s):
                    if kind == HEADS:
                        head_step(a, i, s)
                    else:
                        ffn_step(a, i, kind == FFN0)
                    if s in (0, 1) and seg < 5:
                        modulate(6 + 2 * seg + s, 2 * ((a + 1) % 2))

                steps(dve, base, n, body)
                if kind == HEADS:
                    rest_of_retrieved(base + n - 1, 0)
                dve.wait_ge(down_done, base + n)
                gate = (gates[:, 1], gates[:, 0], gate1b[:])[kind]
                residual(2 + seg, gate, scales[:, 2:3] if kind == FFN1 else 1.0, 4)
                if seg < 4:
                    norm(4 + seg)

        @block.tensor
        def _(pe):
            t_ = nc.tensor

            def three(out, w, xs, first, last):
                t_.matmul(out, w[0], xs[0], start=first, stop=False)
                t_.matmul(out, w[0], xs[1], start=False, stop=False)
                return t_.matmul(out, w[1], xs[0], start=False, stop=last)

            def modulation(l, j):
                at = MOD_CH * l + j
                bank, col = (6, j) if j < 2 else (7, j - 2)
                pe.wait_ge(wmod_in[at % 3], 16 * (at // 3 + 1))
                for m in range(KC):
                    for k in range(KC):
                        c = (col * KC + m) * B
                        ins = t_.matmul(ps[:, bank, c:c + B], wmod[:, at % 3, k, m * P:(m + 1) * P],
                                        silu_c[:, l, k, :], start=k == 0, stop=k == KC - 1)
                ins.then_inc(mod_mm, 1)

            def gate_rows(c):
                l, q = c // 2, (2, 5)[c % 2]
                for b in range(B):
                    for m in range(KC):
                        ins = t_.matmul(ps[:, 4 + b, m * P:(m + 1) * P],
                                        modc[:, l, q * KC + m, b:b + 1].to_broadcast([P, P]), ident[:],
                                        start=True, stop=True)
                ins.then_inc(gate_mm, 1)

            def turn(m, bank):
                for k in range(KC):
                    for j in range(2):
                        c = (k % 2) * S + j * P
                        ins = t_.transpose(ps[:, bank + k // 2, c:c + P],
                                           xn[:, 2 * (m % 2) + j, k * P:(k + 1) * P], ident[:])
                ins.then_inc(turned, 1)

            pe.wait_ge(silu_c_done, 1)
            modulation(0, 0)
            modulation(0, 1)
            pe.wait_ge(const_ready, 1)
            for m in range(4):
                pe.wait_ge(ln_xn, m // 2 + 1)
                if m >= 2:
                    pe.wait_ge(h32_done, m - 1)
                turn(m, 2 * (m % 2))

            pe.wait_ge(h32_done, 4)
            pe.wait_ge(act_lo_done, 4)
            pe.wait_ge(wqkv_lo_done, 1)
            pe.wait_ge(const_bf, 1)
            with pe.Fori(0, B) as b:
                xs = lambda k: (act_hi[:, k, bass.ts(b, S)], act_lo[:, k, bass.ts(b, S)])
                wl = lambda k, c: (wqkv_hi[:, k, c:c + P], wqkv_lo[:, k, c:c + P])
                pe.wait_ge(heads_lo, b)
                for part, done in ((0, q_mm), (1, k_mm)):
                    for m in range(KC):
                        for k in range(KC):
                            ins = three(ps[:, 2 * part + m // 2, (m % 2) * S:(m % 2 + 1) * S],
                                        wl(k, part * D + m * P), xs(k), k == 0, k == KC - 1)
                    ins.then_inc(done, 1)
                for k in range(KC):
                    ins = three(ps[:, 4, 0:S], wl(k, 2 * D), xs(k), k == 0, k == KC - 1)
                ins.then_inc(v_mm, 1)
                pe.wait_ge(q_ev, b + 1)
                pe.wait_ge(k_ev, b + 1)

                def score(n):
                    iblk, gr, r = n // NKV, n % NKV, n % 2
                    w = P * (iblk + 1)
                    if n >= 2:
                        pe.wait_ge(shift_done, UNITS * b + (n - 1))
                    for pr in range(2):
                        row = 64 * (gr % 2) + 32 * pr
                        t_.matmul(ps[:, 2 * r + pr, 0:2 * w],
                                  qT[row:row + 32, gr // 2, iblk * P:(iblk + 1) * P],
                                  k2[row:row + 32, gr // 2, :, 0:w], start=True, stop=True)
                    for pr in range(2):
                        ins = t_.matmul(ps[:, 2 * r + pr, 0:2 * w].rearrange("p (h s) -> p h s", h=2)[:, :, w - P:w],
                                        ident_bf[:], causal_bf[:].unsqueeze(1).to_broadcast([P, 2, P]),
                                        start=False, stop=True, skip_group_check=True)
                    ins.then_inc(scored, 1)

                def turn_scores(n):
                    r = n % 2
                    pe.wait_ge(shift_done, UNITS * b + (n + 1))
                    if n >= 1:
                        pe.wait_ge(exp_done, UNITS * b + n)
                    for j in range(n // NKV + 1):
                        for h in range(REP):
                            ins = t_.transpose(ps[:, 4 + j, h * P:(h + 1) * P],
                                               shifted[:, r, h, j * P:(j + 1) * P], ident[:])
                    ins.then_inc(probs_turned, 1)

                def weigh(n):
                    iblk, gr, r = n // NKV, n % NKV, n % 2
                    pe.wait_ge(exp_done, UNITS * b + (n + 1))
                    if n >= NKV and gr % 4 == 0:
                        pe.wait_ge(heads_ev, 4 * b + (n // 4 - 1))
                    for h in range(REP):
                        c = ((gr % 4) * REP + h) * VW
                        for j in range(iblk + 1):
                            ins = t_.matmul(ps[:, 6 + gr // 4, c:c + VW], probsT[:, r, j, h * P:(h + 1) * P],
                                            v1[:, j, gr, :], start=j == 0, stop=j == iblk)
                    ins.then_inc(pv_done, 1)

                score(0)
                pe.wait_ge(vT_ev, b + 1)
                for j in range(2):
                    ins = t_.transpose(ps[:, 5, j * P:(j + 1) * P], vT[:, j * P:(j + 1) * P], ident[:])
                ins.then_inc(v_turned, 1)
                score(1)
                pe.wait_ge(v_ev, b + 1)
                turn_scores(0)
                for n in range(2, UNITS):
                    score(n)
                    turn_scores(n - 1)
                    weigh(n - 2)
                turn_scores(UNITS - 1)
                weigh(UNITS - 2)
                weigh(UNITS - 1)
                pe.wait_ge(heads_ev, 4 * b + 4)
                for iblk in range(2):
                    for k in range(KC):
                        c = (k % 2) * S + iblk * P
                        ins = t_.transpose(ps[:, k // 2, c:c + P], heads_out[:, iblk, k * P:(k + 1) * P], ident[:])
                ins.then_inc(heads_turned, 1)

            for j in range(2, MOD_CH):
                modulation(0, j)
            pe.wait_ge(mod_ev, 2)
            gate_rows(0)
            pe.wait_ge(gate_ev, 1)
            gate_rows(1)
            pe.wait_ge(gate_ev, 2)
            pe.wait_ge(heads_lo, B)
            pe.wait_ge(wqkv_lo_done, 2)
            for half in range(2):
                for j in range(TH):
                    t = half * TH + j
                    for k in range(KC):
                        ins = three(ps[:, 4 * (1 - half) + j, :],
                                    (act_hi[:, k, t * P:(t + 1) * P], act_lo[:, k, t * P:(t + 1) * P]),
                                    (wo_hi[:, k, :], wo_lo[:, k, :]), k == 0, k == KC - 1)
                ins.then_inc(proj_done, 1)
            for m in (4, 5):
                pe.wait_ge(ln_xn, 3)
                turn(m, 4 + 2 * (m % 2))
            pe.wait_ge(h32_done, 6)
            for j in range(MOD_CH):
                modulation(1, j)
            pe.wait_ge(mod_ev, 4)
            gate_rows(2)
            pe.wait_ge(gate_ev, 3)
            gate_rows(3)
            pe.wait_ge(gate_ev, 4)

            def route(h):
                if h == 0:
                    pe.wait_ge(resid_done, 2)
                    pe.wait_ge(gw_split, 2)
                pe.wait_ge(act_lo_done, 6 + 2 * h)
                for j in range(TH):
                    t = h * TH + j
                    for k in range(KC):
                        for q, (xa, wa) in enumerate(((act_hi, gw_hi), (act_hi, gw_lo), (act_lo, gw_hi), (act_lo, gw_lo))):
                            ins = t_.matmul(ps[:, 2, j * E:(j + 1) * E], xa[:, k, t * P:(t + 1) * P], wa[:, k, :],
                                            start=(k, q) == (0, 0), stop=(k, q) == (KC - 1, 3))
                ins.then_inc(logits_mm, 1)
                pe.wait_ge(comb_done, h + 1)
                for j in range(TH):
                    ins = t_.transpose(ps[0:E, 3, j * P:(j + 1) * P], pick1[:, j, :], ident[:])
                ins.then_inc(comb_turned, 1)
                pe.wait_ge(comb_ev, h + 1)

            def down(a, i, s, seg):
                r = a % 2
                pe.wait_ge(down_lo, a + 1 + 2 * i)
                pe.wait_ge(inner_lo_done, a + 1 + 2 * i)
                if s == 0:
                    pe.wait_ge(resid_done, seg + 2)
                last = s is not None and s == SEGMENTS[seg][3] - 1
                for j in range(TH):
                    ins = three(ps[:, 4 + j, :], (inner_hi[:, r, j * P:(j + 1) * P], inner_lo[:, r, j * P:(j + 1) * P]),
                                (w_hi[:, r, UP_W:UP_W + D], w_lo[:, r, UP_W:UP_W + D]), s == 0, last)
                ins.then_inc(down_done, 1)

            def xs_of(half):
                cols = slice(half * HALF, (half + 1) * HALF)
                return lambda k: (act_hi[:, k, cols], act_lo[:, k, cols])

            def ffn_step(a, i, s, seg, half):
                r, xs = a % 2, xs_of(half)
                pe.wait_ge(up_lo, a + 1 + 2 * i)
                if a >= 2:
                    pe.wait_ge(inner_done_of(a - 2), inner_count(a - 2) + 1 + 2 * i)
                for q in range(2):
                    for k in range(KC):
                        c = (2 * k + q) * P
                        ins = three(ps[:, 2 * r + q, :], (w_hi[:, r, c:c + P], w_lo[:, r, c:c + P]), xs(k),
                                    k == 0, k == KC - 1)
                ins.then_inc(up_done, 1)
                if s != 0:
                    down(a - 1, i, None if s is None else s - 1, seg)

            def inner_done_of(a):
                return ret_done if kind_of(a) == HEADS else inner_done

            def inner_count(a):
                if kind_of(a) == HEADS:
                    return a - HEAD0
                return ffn_count(a)

            def turn_retrieved(a, i):
                r, k = a % 2, a - HEAD0
                pe.wait_ge(ret_done, k + 1 + 2 * i)
                for j in range(TH):
                    ins = t_.transpose(ps[:, 2 * r, j * P:(j + 1) * P], inner[:, r, j * P:(j + 1) * P], ident[:])
                ins.then_inc(ret_turned, 1)

            def head_step(a, i, s, seg, half):
                r, xs, k_ = a % 2, xs_of(half), a - HEAD0
                pe.wait_ge(up_lo, a + 1 + 2 * i)
                for k in range(KC):
                    if k == KC // 2 and s != 0:
                        turn_retrieved(a - 1, i)
                    ins = three(ps[:, 2 * r, :], (w_hi[:, r, k * P:(k + 1) * P], w_lo[:, r, k * P:(k + 1) * P]),
                                xs(k), k == 0, k == KC - 1)
                ins.then_inc(q1_done, 1)
                if s != 0:
                    down(a - 1, i, None if s is None else s - 1, seg)
                pe.wait_ge(sig_lo_done, k_ + 1 + 2 * i)
                if k_ >= 1:
                    pe.wait_ge(ret_done, k_ + 2 * i)
                for j in range(TH):
                    c = (j % 2) * MZ_W
                    ins = three(ps[:, 2 * (j // 2) + 1, c:c + MZ_W],
                                (sig_hi[:, j * P:(j + 1) * P], sig_lo[:, j * P:(j + 1) * P]),
                                (w_hi[:, r, MZ:MZ + MZ_W], w_lo[:, r, MZ:MZ + MZ_W]), True, True)
                ins.then_inc(up_done, 1)

            for seg, (kind, half, base, n) in enumerate(SEGMENTS):
                if kind == FFN0:
                    route(half)
                pe.wait_ge(act_lo_done, 6 + 2 * seg)

                def body(a, i, s):
                    s_at = a - base
                    if s_at in (1, 2) and seg < 5:
                        pe.wait_ge(h32_done, 6 + 2 * seg + s_at)
                    (head_step if kind == HEADS else ffn_step)(a, i, s, seg, half)
                    if s in (0, 1) and seg < 5:
                        m = 6 + 2 * seg + s
                        pe.wait_ge(ln_xn, m // 2 + 1)
                        if kind == HEADS:
                            pe.wait_ge(ret_done, a - HEAD0 + 1)
                        elif a >= 1:
                            pe.wait_ge(inner_done_of(a - 1), inner_count(a - 1) + 1)
                        turn(m, 2 * ((a + 1) % 2))

                steps(pe, base, n, body)
                a = base + n - 1
                if kind == HEADS:
                    turn_retrieved(a, 0)
                down(a, 0, n - 1, seg)


def _chunks(w_gate, w_up, w_down):
    gu = np.stack([w_gate, w_up])
    gu = gu.reshape(2, P, KC, P).transpose(3, 2, 0, 1).reshape(P, UP_W)
    return np.concatenate([gu, w_down.T], axis=1)


def _by_k(w):
    return np.ascontiguousarray(w.reshape(KC, P, -1).transpose(1, 0, 2))


def kernel(**inputs):
    import concourse.bacc as bacc
    from concourse.bass_utils import run_bass_kernel_spmd

    f = {k: np.asarray(v) for k, v in inputs.items()}
    nc = bacc.Bacc("TRN2", target_bir_lowering=False, num_devices=1)

    per_q = np.repeat(f["L0_attn_wk"].reshape(D, NKV, HD), REP, axis=1).reshape(D, NH * HD)
    wqkv = np.concatenate([f["L0_attn_wq"], per_q, f["L0_attn_wv"]], axis=1)
    sgu, sdn = f["L0_ffn_shared_w_gate_up"], f["L0_ffn_shared_w_down"]
    rows = [slice(c * P, (c + 1) * P) for c in range(SHARED)]
    ffn0 = [_chunks(sgu[:D][r], sgu[D:][r], sdn[:, r]) for r in rows]
    ffn0 += [_chunks(f["L0_ffn_w_gate_up"][e, :P], f["L0_ffn_w_gate_up"][e, P:], f["L0_ffn_w_down"][e])
             for e in range(E)]
    pad = N_STEPS[FFN1] * P - FF
    gate, up = (np.pad(f[k], ((0, pad), (0, 0))) for k in ("L1_ffn_gate_w", "L1_ffn_up_w"))
    down = np.pad(f["L1_ffn_down_w"], ((0, 0), (0, pad)))
    rows = [slice(c * P, (c + 1) * P) for c in range(N_STEPS[FFN1])]
    ffn1 = [_chunks(gate[r], up[r], down[:, r]) for r in rows]
    heads = []
    for h in range(H1):
        q = f["L1_attn_Wq"][h * G1 * P:(h * G1 + 1) * P]
        q = q.reshape(P, KC, P).transpose(2, 1, 0).reshape(P, KC * P)
        z = f["L1_attn_z"][h][:, None]
        wo = f["L1_attn_Wo"][:, h * G1 * P:(h + 1) * G1 * P]
        wo = wo.reshape(D, G1, P).transpose(2, 1, 0).reshape(P, G1 * D)
        heads.append(np.concatenate([q, f["L1_attn_M"][h], z, z, wo], axis=1))
    arrays = {
        "x": f["L0_attn_x"].reshape(T // P, P, D).transpose(1, 0, 2),
        "cond": np.stack([f[f"L{l}_c"].reshape(B, KC, P).transpose(2, 1, 0) for l in range(2)]),
        "wmod": np.stack([f[f"L{l}_wmod"].reshape(KC, P, MOD_CH, D).transpose(2, 1, 0, 3) for l in range(2)]),
        "wqkv": _by_k(wqkv),
        "wo": _by_k(f["L0_attn_wo"]),
        "gate_w": _by_k(f["L0_ffn_gate_w"].T),
        "bq": f["L1_attn_bq"].reshape(H1, G1, P)[:, 0].T,
        "scales": np.stack([f[f"L1_ffn_{k}_scale"].reshape(()) for k in ("gate", "up", "down")]).reshape(1, 3),
        "ffn0": np.stack(ffn0), "heads": np.stack(heads), "ffn1": np.stack(ffn1),
    }
    arrays = {f"in_{k}": np.ascontiguousarray(a) for k, a in arrays.items()}
    d = {k[3:]: nc.dram_tensor(k, a.shape, FP, kind="ExternalInput").ap() for k, a in arrays.items()}
    d["chunks"] = {FFN0: d["ffn0"], HEADS: d["heads"], FFN1: d["ffn1"]}
    d["comb"] = nc.dram_tensor("comb", [SHARED + E, T], FP, kind="Internal").ap()
    d["out"] = nc.dram_tensor("out", [P, T // P, D], FP, kind="ExternalOutput").ap()
    build(nc, d)
    r = run_bass_kernel_spmd(nc, [arrays], core_ids=[0])
    return np.asarray(r.results[0]["out"]).transpose(1, 0, 2).reshape(B, S, D)
```

```python
from contextlib import ExitStack

import numpy as np

import concourse.bass as bass
from concourse import mybir

FP = mybir.dt.float32
FR = mybir.dt.float32r
BF = mybir.dt.bfloat16
U32 = mybir.dt.uint32
ALU = mybir.AluOpType
ACT = mybir.ActivationFunctionType
AX = mybir.AxisListType

P = 128
D = 512
KC = D // P
B, S = 4, 256
T = B * S
HALF = T // 2
TH = HALF // P
NH, NKV, HD = 32, 8, 16
REP = NH // NKV
VW = HD + 1
QKV = NH * HD + 2 * NKV * HD
STACK = 4 * HD
PAIRS = NH // 2
E = 16
SHARED = 4
H1 = 8
G1 = 4
FF = 1376
FFN_W = KC * 2 * P + D
UP_W = KC * 2 * P
MZ = KC * P
MZ_W = P + 2
HEAD_W = KC * P + MZ_W + G1 * D
EPS = 1e-5
DEN_EPS = 1e-6
NEG = -1e30
MOD_CH = 6
ROUTE_BANK = (6, 2)
SHARES_BANK = (6, 0)
MOD_BANK = (0, 1, 2, 3, 6, 7, 4, 5, 6, 7, 4, 5)

FFN0, HEADS, FFN1 = range(3)
N_STEPS = {FFN0: SHARED + E, HEADS: H1, FFN1: (FF + P - 1) // P}
SEGMENTS = []
_at = 0
for _kind in (FFN0, HEADS, FFN1):
    for _half in range(2):
        SEGMENTS.append((_kind, _half, _at, N_STEPS[_kind]))
        _at += N_STEPS[_kind]
HEAD0 = 2 * N_STEPS[FFN0]
LAST_STEP = _at - 1
UNITS = 2 * NKV
TURN_Q1 = 1
TURN_XN = 3
PROJECT = (5, 7)
TURN_Q0 = 9


def steps(eng, base, n, body):
    pairs = (n - 3) // 2
    body(base, 0, 0)
    body(base + 1, 0, 1)
    with eng.Fori(0, pairs) as i:
        body(base + 2, i, None)
        body(base + 3, i, None)
    for s in range(2 + 2 * pairs, n):
        body(base + s, 0, s)


def build(nc, d):
    ctx = ExitStack()
    with ctx:
        def sem(name):
            return ctx.enter_context(nc.semaphore(name))

        def sb(name, shape, dt=FP, where=ctx):
            return where.enter_context(nc.sbuf_tensor(name, shape, dt))

        x = sb("x", [P, T // P, D])
        act_hi = sb("act_hi", [P, KC, T], FR)
        act_lo = sb("act_lo", [P, KC, T], FR)
        wmod = sb("wmod", [P, 2, KC, D])
        xn = sb("xn", [P, TH, D])
        h32 = sb("h32", [P, 2, KC, S])
        ident = sb("ident", [P, P])
        ident_r = sb("ident_r", [P, P], FR)
        ident_bf = sb("ident_bf", [P, P], BF)
        causal = sb("causal", [P, P])
        causal_bf = sb("causal_bf", [P, P], BF)
        cond = sb("cond", [P, 2, KC, B])
        silu_c = sb("silu_c", [P, 2, KC, B])
        mod_row = sb("mod_row", [B, 2, D])
        gate_row = sb("gate_row", [B, 2, D])
        row_of = sb("row_of", [B, B, P])
        modc = sb("modc", [P, 2, MOD_CH * KC, B])
        sign = sb("sign", [B, D])
        stats = sb("stats", [P, TH, 6])
        mv = sb("mv", [P, TH, 2])
        var_eps = sb("var_eps", [P, TH])
        rstd = sb("rstd", [P, TH])
        mv0 = sb("mv0", [P, T // P, 2])
        rstd0 = sb("rstd0", [P, T // P])
        minus_half = sb("minus_half", [P, TH])
        scales = sb("scales", [P, 3])
        one = sb("one", [P, 1])
        bq = sb("bq", [P, H1])
        iota_e = sb("iota_e", [P, E])
        ones_row = sb("ones_row", [SHARED, P])
        gw = sb("gw", [P, KC, E])
        gw_parts = sb("gw_parts", [P, KC, 2 * E], FR)

        early = ExitStack()
        wo_hi = sb("wo_hi", [P, KC, D], FR, early)
        wo_lo = sb("wo_lo", [P, KC, D], FR, early)
        wqkv_hi = sb("wqkv_hi", [P, KC, QKV], FR, early)
        wqkv_lo = sb("wqkv_lo", [P, KC, QKV], FR, early)
        xa_hi = sb("xa_hi", [P, KC, S], FR, early)
        xa_lo = sb("xa_lo", [P, KC, S], FR, early)
        q_parts = sb("q_parts", [P, 2, NH, 4, HD], FR, early)
        k_parts = sb("k_parts", [P, 2, NKV, 4, HD], FR, early)
        v_next = sb("v_next", [P, 2, NKV, HD], FP, early)
        v1 = sb("v1", [P, 2, NKV, VW], FP, early)
        row_max = sb("row_max", [P, 2, REP], FP, early)
        rsum = sb("rsum", [P, 2, 16], FP, early)
        loading = ExitStack()
        wqkv_in = sb("wqkv_in", [P, KC, QKV], FP, loading)
        wo_in = sb("wo_in", [P, KC, D], FP, loading)
        loading.close()
        q_stack = sb("q_stack", [P, 2, PAIRS, P], FR, early)
        k_stack = sb("k_stack", [P, NKV // 2, S], FR, early)
        shifted = sb("shifted", [P, 2, REP, S], FP, early)
        probsT = sb("probsT", [P, 2, 2, REP * P], FP, early)
        early.close()

        w_in = sb("w_in", [P, 2, HEAD_W])
        w_hi = sb("w_hi", [P, 2, FFN_W], FR)
        w_lo = sb("w_lo", [P, 2, FFN_W], FR)
        silu = sb("silu", [P, 2, HALF])
        inner = sb("inner", [P, 2, HALF])
        inner_hi = sb("inner_hi", [P, 2, HALF], FR)
        inner_lo = sb("inner_lo", [P, 2, HALF], FR)
        share = sb("share", [P, 2, HALF])
        below = sb("below", [P, HALF])
        sig = sb("sig", [P, HALF])
        sig_hi = sb("sig_hi", [P, HALF], FR)
        sig_lo = sb("sig_lo", [P, HALF], FR)
        den = sb("den", [P, 2, 2])
        rden = sb("rden", [P, 2, 2])
        logits = sb("logits", [P, TH, E])
        top8 = sb("top8", [P, TH, 8])
        top_at = sb("top_at", [P, TH, 8], U32)
        top_f = sb("top_f", [P, TH, 2])
        gap = sb("gap", [P, TH])
        e2 = sb("e2", [P, TH])
        w1 = sb("w1", [P, TH])
        w2 = sb("w2", [P, TH])
        pick1 = sb("pick1", [P, TH, E])
        pick2 = sb("pick2", [P, TH, E])
        combT = sb("combT", [E, HALF])
        logitsT = sb("logitsT", [2 * E, HALF])
        gate1b = sb("gate1b", [P, B, D])
        gates = sb("gates", [P, 2, B, D])

        heads_out = xn[:, 2:4, :]
        sums = h32[0:VW, 1].rearrange("v k s -> v (k s)").rearrange("v (r q) -> v r q", r=2)
        ps = ctx.enter_context(nc.psum_tensor("ps", [P, 8, 512], FP))

        x_in = [sem(f"x_in{h}") for h in range(2)]
        small_in = sem("small_in")
        late_in = sem("late_in")
        wqkv_arrived = sem("wqkv_arrived")
        wo_arrived = sem("wo_arrived")
        wmod_in = [sem(f"wmod_in{r}") for r in range(2)]
        w_arrived = [sem(f"w_arrived{r}") for r in range(2)]
        ones_stored = sem("ones_stored")
        comb_stored = sem("comb_stored")
        share_in = [sem(f"share_in{r}") for r in range(2)]
        out_stored = sem("out_stored")
        const_zero = sem("const_zero")
        const_ready = sem("const_ready")
        const_bf = sem("const_bf")
        ones_ready = sem("ones_ready")
        silu_c_done = sem("silu_c_done")
        mod_mm = sem("mod_mm")
        row_ev = sem("row_ev")
        mod_turned = sem("mod_turned")
        mod_cols = sem("mod_cols")
        gate_row_done = sem("gate_row_done")
        gate_mm = sem("gate_mm")
        gate_ev = sem("gate_ev")
        ln_tmp = sem("ln_tmp")
        ln_stats = sem("ln_stats")
        ln_eps = sem("ln_eps")
        ln_rstd = sem("ln_rstd")
        xn0_done = sem("xn0_done")
        ln_xn = sem("ln_xn")
        turned = sem("turned")
        h32_done = sem("h32_done")
        act_hi_done = sem("act_hi_done")
        act_lo_done = sem("act_lo_done")
        gw_split = sem("gw_split")
        wqkv_hi_done = sem("wqkv_hi_done")
        wqkv_lo_done = sem("wqkv_lo_done")
        qkv_mm = sem("qkv_mm")
        qkv_hi_done = sem("qkv_hi_done")
        qkv_lo_done = sem("qkv_lo_done")
        q_turned = sem("q_turned")
        q_ev = sem("q_ev")
        k_turned = sem("k_turned")
        k_ev = sem("k_ev")
        v_ev = sem("v_ev")
        scored = sem("scored")
        max_done = sem("max_done")
        shift_done = sem("shift_done")
        probs_turned = sem("probs_turned")
        exp_done = sem("exp_done")
        pv_done = sem("pv_done")
        sums_ev = sem("sums_ev")
        sums_turned = sem("sums_turned")
        rsum_done = sem("rsum_done")
        heads_ev = sem("heads_ev")
        heads_turned = sem("heads_turned")
        heads_hi = sem("heads_hi")
        heads_taken = sem("heads_taken")
        proj_done = sem("proj_done")
        addend_done = sem("addend_done")
        resid_done = sem("resid_done")
        logits_mm = sem("logits_mm")
        logits_ev = sem("logits_ev")
        logits_turned = sem("logits_turned")
        logits_done = sem("logits_done")
        router = sem("router")
        gap_done = sem("gap_done")
        e2_done = sem("e2_done")
        comb_done = sem("comb_done")
        comb_turned = sem("comb_turned")
        comb_ev = sem("comb_ev")
        group_pair = sem("group_pair")
        group_sum = sem("group_sum")
        up_hi = sem("up_hi")
        up_lo = sem("up_lo")
        down_hi = sem("down_hi")
        down_lo = sem("down_lo")
        up_done = sem("up_done")
        down_done = sem("down_done")
        silu_done = sem("silu_done")
        scaled_done = sem("scaled_done")
        inner_done = sem("inner_done")
        inner_hi_done = sem("inner_hi_done")
        inner_lo_done = sem("inner_lo_done")
        q1_done = sem("q1_done")
        below_done = sem("below_done")
        above_done = sem("above_done")
        elu_done = sem("elu_done")
        sig_done = sem("sig_done")
        sig_hi_done = sem("sig_hi_done")
        sig_lo_done = sem("sig_lo_done")
        den_done = sem("den_done")
        rden_done = sem("rden_done")
        ret_done = sem("ret_done")
        ret_turned = sem("ret_turned")

        block = ctx.enter_context(nc.Block())

        def cols_count(l, q):
            return 4 * l + (0, 1, None, 2, 3)[q]

        def mod_used(at):
            l, q = at // MOD_CH, at % MOD_CH
            return (gate_row_done, 2 * l + (1 if q == 2 else 2)) if q in (2, 5) else \
                (mod_turned, cols_count(l, q) + 1)

        def half_tiles(half):
            return range(half * TH, (half + 1) * TH)

        def kind_of(a):
            return next(k for k, _, base, n in SEGMENTS if base <= a < base + n)

        def ffn_count(a):
            return a if a < HEAD0 else a - 2 * H1

        def chunk_of(a, i):
            kind, _, base, _ = next(s for s in SEGMENTS if s[2] <= a < s[2] + s[3])
            return kind, a - base + 2 * i

        @block.sync
        def _(sp):
            for l in range(2):
                sp.dma_start(cond[:, l], d["cond"][l]).then_inc(small_in, 16)
            sp.dma_start(wmod[:, 0], d["wmod"][0, 0]).then_inc(wmod_in[0], 16)
            sp.dma_start(x[:, 0:TH], d["x"][:, 0:TH]).then_inc(x_in[0], 16)
            sp.dma_start(wmod[:, 1], d["wmod"][0, 1]).then_inc(wmod_in[1], 16)
            sp.dma_start(wqkv_in[:], d["wqkv"]).then_inc(wqkv_arrived, 16)
            sp.dma_start(x[:, TH:2 * TH], d["x"][:, TH:2 * TH]).then_inc(x_in[1], 16)
            for j in range(2, 4):
                sp.wait_ge(mod_mm, j - 1)
                sp.dma_start(wmod[:, j % 2], d["wmod"][0, j]).then_inc(wmod_in[j % 2], 16)
            sp.dma_start(wo_in[:], d["wo"]).then_inc(wo_arrived, 16)
            sp.dma_start(gw[:], d["gate_w"]).then_inc(late_in, 16)
            sp.dma_start(bq[:], d["bq"]).then_inc(late_in, 16)
            sp.dma_start(scales[:], d["scales"].to_broadcast([P, 3])).then_inc(late_in, 16)
            sp.wait_ge(ones_ready, 1)
            sp.dma_start(d["comb"][0:SHARED, :].rearrange("s (r t) -> s r t", t=P),
                         ones_row[:].unsqueeze(1).to_broadcast([SHARED, T // P, P])).then_inc(ones_stored, 16)
            for j in range(4, 2 * MOD_CH):
                sp.wait_ge(mod_mm, j - 1)
                sp.dma_start(wmod[:, j % 2], d["wmod"][j // MOD_CH, j % MOD_CH]).then_inc(wmod_in[j % 2], 16)

            def load(a, i, s):
                if a == 0:
                    sp.wait_ge(proj_done, 2)
                if a >= 2:
                    sp.wait_ge(down_lo, a - 1 + 2 * i)
                kind, c = chunk_of(a, i)
                width = HEAD_W if kind == HEADS else FFN_W
                sp.dma_start(w_in[:, a % 2, 0:width], d["chunks"][kind][c]).then_inc(w_arrived[a % 2], 16)

            for _, _, base, n in SEGMENTS:
                steps(sp, base, n, load)
            for h in range(2):
                sp.wait_ge(resid_done, 7 + h)
                sp.dma_start(d["out"][:, h * TH:(h + 1) * TH], x[:, h * TH:(h + 1) * TH]).then_inc(out_stored, 16)
            sp.wait_ge(out_stored, 32)

        @block.gpsimd
        def _(pool):
            g = nc.gpsimd
            g.memset(ident[:], 0.0).then_inc(const_zero, 1)
            g.memset(causal[:], 0.0).then_inc(const_zero, 1)
            g.memset(minus_half[:], -0.5).then_inc(const_zero, 1)
            g.memset(one[:], 1.0).then_inc(const_zero, 1)
            g.memset(ones_row[:], 1.0).then_inc(ones_ready, 1)
            g.memset(row_of[:], 0.0).then_inc(const_zero, 1)
            g.iota(iota_e[:], pattern=[[1, E]], base=0, channel_multiplier=0,
                   allow_small_or_imprecise_dtypes=True).then_inc(const_zero, 1)
            pool.wait_ge(const_zero, 6)
            g.affine_select(out=ident[:], in_=ident[:], compare_op=ALU.not_equal, fill=1.0,
                            base=0, pattern=[[-1, P]], channel_multiplier=1).then_inc(const_ready, 1)
            g.affine_select(out=causal[:], in_=causal[:], compare_op=ALU.is_ge, fill=NEG,
                            base=0, pattern=[[-1, P]], channel_multiplier=1).then_inc(const_ready, 1)
            g.affine_select(out=row_of[:], in_=row_of[:], compare_op=ALU.not_equal, fill=1.0,
                            base=0, pattern=[[-1, B], [0, P]], channel_multiplier=1).then_inc(const_ready, 1)

            def ln_root(n):
                h = slice(n * TH, (n + 1) * TH)
                var, root = (mv0[:, h, 1], rstd0[:, h]) if n < 2 else (mv[:, :, 1], rstd[:])
                pool.wait_ge(ln_stats, n + 1)
                g.tensor_scalar(var_eps[:], var, EPS, 1.0, ALU.add, ALU.mult).then_inc(ln_eps, 1)
                pool.wait_ge(ln_eps, n + 1)
                g.tensor_tensor(root, var_eps[:], minus_half[:], ALU.pow).then_inc(ln_rstd, 1)

            def rest_of_batch(c):
                pool.wait_ge(act_hi_done, c + 1)
                g.tensor_tensor(xa_lo[:], h32[:, 0], xa_hi[:].bitcast(FP), ALU.subtract).then_inc(act_lo_done, 1)

            def rest_of_act(m):
                b = m % B
                pool.wait_ge(act_hi_done, m + 1)
                cols = slice(b * S, (b + 1) * S)
                g.tensor_tensor(act_lo[:, :, cols], h32[:, m % 2], act_hi[:, :, cols].bitcast(FP),
                                ALU.subtract).then_inc(act_lo_done, 1)

            def rest_of_weights(a, i):
                kind = kind_of(a)
                r = a % 2
                if kind == HEADS:
                    q = MZ + MZ_W
                    k = a - HEAD0
                    pool.wait_ge(w_arrived[r], 16 * (a // 2 + 1) + 16 * i)
                    g.tensor_tensor(w_in[:, r, q:q + 2 * D], w_in[:, r, q:q + 2 * D],
                                    w_in[:, r, q + 2 * D:q + 4 * D], ALU.add).then_inc(group_pair, 1)
                    pool.wait_ge(group_pair, k + 1 + 2 * i)
                    g.tensor_tensor(w_in[:, r, q:q + D], w_in[:, r, q:q + D],
                                    w_in[:, r, q + D:q + 2 * D], ALU.add).then_inc(group_sum, 1)
                    down, used = q, MZ + MZ_W
                else:
                    down, used = UP_W, UP_W
                pool.wait_ge(up_hi, a + 1 + 2 * i)
                g.tensor_tensor(w_lo[:, r, 0:used], w_in[:, r, 0:used], w_hi[:, r, 0:used].bitcast(FP),
                                ALU.subtract).then_inc(up_lo, 1)
                pool.wait_ge(down_hi, a + 1 + 2 * i)
                g.tensor_tensor(w_lo[:, r, UP_W:UP_W + D], w_in[:, r, down:down + D],
                                w_hi[:, r, UP_W:UP_W + D].bitcast(FP), ALU.subtract).then_inc(down_lo, 1)

            ln_root(0)
            ln_root(1)
            rest_of_batch(0)
            with pool.Fori(0, B - 1) as b:
                rest_of_batch(b + 1)
            ln_root(2)
            rest_of_act(4)
            rest_of_act(5)
            ln_root(3)
            rest_of_weights(0, 0)
            for seg, (kind, half, base, n) in enumerate(SEGMENTS):
                def body(a, i, s):
                    if a < LAST_STEP:
                        rest_of_weights(a + 1, i)
                    if s in (0, 1) and seg < 5:
                        rest_of_act(6 + 2 * seg + s)

                steps(pool, base, n, body)
                if seg < 4:
                    ln_root(4 + seg)

        @block.scalar
        def _(act):
            a_ = nc.scalar
            act.wait_ge(small_in, 2 * 16)
            a_.activation(silu_c[:], cond[:], ACT.Silu).then_inc(silu_c_done, 1)

            def take_row(at):
                act.wait_ge(mod_mm, at + 1)
                if at >= 2:
                    done, count = mod_used(at - 2)
                    act.wait_ge(done, count)
                a_.activation(mod_row[:, at % 2], ps[0:B, MOD_BANK[at], :], ACT.Copy).then_inc(row_ev, 1)

            def split_act(m):
                b = m % B
                act.wait_ge(h32_done, m + 1)
                a_.activation(act_hi[:, :, b * S:(b + 1) * S], h32[:, m % 2], ACT.Copy).then_inc(act_hi_done, 1)

            def split_batch(c):
                act.wait_ge(h32_done, c + 1)
                a_.activation(xa_hi[:], h32[:, 0], ACT.Copy).then_inc(act_hi_done, 1)

            def split_qkv(c, j):
                act.wait_ge(qkv_mm, 2 * c + (j + 1))
                a_.activation(q_parts[:, j, :, 0::2, :], ps[:, 4, :].rearrange("p (h e) -> p h e", e=HD)
                              .unsqueeze(2).to_broadcast([P, NH, 2, HD]), ACT.Copy)
                k = ps[:, 5, 0:P].rearrange("p (g e) -> p g e", e=HD)
                a_.activation(k_parts[:, j, :, 0:2, :], k.unsqueeze(2).to_broadcast([P, NKV, 2, HD]),
                              ACT.Copy).then_inc(qkv_hi_done, 1)

            def take_q(c, iblk):
                act.wait_ge(q_turned, 4 * c + (2 * iblk + 1))
                a_.activation(q_stack[:, iblk, 0:PAIRS // 2, :], ps[:, 4:6, :], ACT.Copy).then_inc(q_ev, 1)

            def take_k(c):
                act.wait_ge(k_turned, c + 1)
                a_.activation(k_stack[:, 0:2, :].rearrange("p g t -> p (g t)"), ps[:, 4, :], ACT.Copy).then_inc(k_ev, 1)

            take_row(0)
            take_row(1)
            act.wait_ge(wqkv_arrived, 16)
            a_.activation(wqkv_hi[:], wqkv_in[:], ACT.Copy).then_inc(wqkv_hi_done, 1)
            split_batch(0)
            split_qkv(0, 0)
            take_row(2)
            split_qkv(0, 1)
            take_row(3)
            act.wait_ge(wo_arrived, 16)
            a_.activation(wo_hi[:], wo_in[:], ACT.Copy).then_inc(wqkv_hi_done, 1)
            act.wait_ge(const_ready, 1)
            act.wait_ge(wqkv_lo_done, 2)
            take_q(0, 0)
            take_row(4)
            take_k(0)
            act.wait_ge(late_in, 3 * 16)
            a_.activation(gw_parts[:, :, 0:E], gw[:], ACT.Copy).then_inc(gw_split, 1)
            take_row(5)

            def attend(b, more):
                def take_sums(n):
                    act.wait_ge(pv_done, UNITS * b + (n + 1))
                    if n >= 2:
                        act.wait_ge(sums_turned, UNITS * b + (n - 1))
                    a_.activation(sums[:, n % 2], ps[0:VW, 6, :], ACT.Copy).then_inc(sums_ev, 1)

                for n in range(UNITS):
                    nj = n // NKV + 1
                    act.wait_ge(probs_turned, UNITS * b + (n + 1))
                    if n >= 2:
                        act.wait_ge(pv_done, UNITS * b + (n - 1))
                    a_.activation(probsT[:, n % 2, 0:nj, :], ps[:, 2 * (n % 2):2 * (n % 2) + nj, :], ACT.Exp,
                                  scale=float(HD) ** -0.5).then_inc(exp_done, 1)
                    if n + 1 == TURN_Q1:
                        take_q(b, 1)
                    if more and n + 1 == TURN_XN:
                        split_batch(b + 1)
                    for j in range(2):
                        if more and n + 1 == PROJECT[j]:
                            split_qkv(b + 1, j)
                    if more and n + 1 == TURN_Q0:
                        take_q(b + 1, 0)
                    if more and n + 1 == UNITS - 1:
                        take_k(b + 1)
                    if n >= 1:
                        take_sums(n - 1)
                take_sums(UNITS - 1)
                act.wait_ge(heads_turned, b + 1)
                a_.activation(act_hi[:, :, b * S:(b + 1) * S] if isinstance(b, int) else act_hi[:, :, bass.ts(b, S)],
                              ps[:, 4:6, :].rearrange("p c (m s) -> p (c m) s", s=S),
                              ACT.Copy).then_inc(heads_hi, 1)

            with act.Fori(0, B - 1) as b:
                attend(b, True)
            attend(B - 1, False)

            def take_logits(h):
                act.wait_ge(logits_mm, h + 1)
                a_.activation(logitsT[:], ps[0:2 * E, ROUTE_BANK[h], :], ACT.Copy).then_inc(logits_ev, 1)

            def soften(h):
                act.wait_ge(gap_done, h + 1)
                a_.activation(e2[:], gap[:], ACT.Exp).then_inc(e2_done, 1)

            def store_shares(h):
                act.wait_ge(comb_turned, h + 1)
                if h == 1:
                    act.wait_ge(comb_stored, 16)
                a_.activation(combT[:], ps[0:E, SHARES_BANK[h], :], ACT.Copy).then_inc(comb_ev, 1)
                act.wait_ge(comb_ev, h + 1)
                act.dma_start(d["comb"][SHARED:SHARED + E, h * HALF:(h + 1) * HALF], combT[:]).then_inc(comb_stored, 16)

            def gate_rows(c):
                dst = gate1b[:] if c == 3 else gates[:, c % 2]
                act.wait_ge(gate_mm, c + 1)
                if c == 2:
                    act.wait_ge(resid_done, 2)
                a_.activation(dst, ps[:, 0:4, :], ACT.Copy).then_inc(gate_ev, 1)

            gate_rows(0)
            split_act(4)
            split_act(5)
            for at in range(MOD_CH, MOD_CH + 4):
                take_row(at)
            gate_rows(1)
            take_logits(0)
            take_row(MOD_CH + 4)
            soften(0)
            gate_rows(2)
            take_row(MOD_CH + 5)
            gate_rows(3)
            store_shares(0)

            def split_up(a, i):
                kind, r = kind_of(a), a % 2
                used = MZ + MZ_W if kind == HEADS else UP_W
                act.wait_ge(w_arrived[r], 16 * (a // 2 + 1) + 16 * i)
                if a >= 2:
                    act.wait_ge(up_done, a - 1 + 2 * i)
                a_.activation(w_hi[:, r, 0:used], w_in[:, r, 0:used], ACT.Copy).then_inc(up_hi, 1)

            def split_down(a, i):
                kind, r = kind_of(a), a % 2
                at = MZ + MZ_W if kind == HEADS else UP_W
                if kind == HEADS:
                    act.wait_ge(group_sum, a - HEAD0 + 1 + 2 * i)
                if a >= 2:
                    act.wait_ge(down_done, a - 1 + 2 * i)
                a_.activation(w_hi[:, r, UP_W:UP_W + D], w_in[:, r, at:at + D], ACT.Copy).then_inc(down_hi, 1)

            def split_inner(a, i):
                if a >= 2:
                    act.wait_ge(down_done, a - 1 + 2 * i)
                a_.activation(inner_hi[:, a % 2], inner[:, a % 2], ACT.Copy).then_inc(inner_hi_done, 1)

            def ffn_step(a, i, half, layer0):
                r = a % 2
                if layer0:
                    c = a - half * N_STEPS[FFN0] + 2 * i
                    if a >= 2:
                        act.wait_ge(inner_done, a - 1 + 2 * i)
                    act.dma_start(share[:, r], d["comb"][bass.ds(c, 1), half * HALF:(half + 1) * HALF]
                                  .to_broadcast([P, HALF])).then_inc(share_in[r], 16)
                k = ffn_count(a)
                act.wait_ge(up_done, a + 1 + 2 * i)
                if k >= 2:
                    act.wait_ge(inner_done, k - 1 + 2 * i)
                gate_scale = one[:, 0:1] if layer0 else scales[:, 0:1]
                a_.activation(silu[:, r], ps[:, 2 * r, :], ACT.Silu, scale=gate_scale).then_inc(silu_done, 1)
                act.wait_ge(inner_done, k + 1 + 2 * i)
                split_inner(a, i)

            def head_step(a, i, s):
                r, k = a % 2, a - HEAD0
                if s != 0:
                    act.wait_ge(ret_turned, retrieved_before(a) + 2 * i)
                    act.wait_ge(down_done, a - 2 + 2 * i)
                    a_.activation(inner_hi[:, 1 - r], ps[:, 2 * (1 - r), :], ACT.Copy).then_inc(inner_hi_done, 1)
                act.wait_ge(below_done, k + 1 + 2 * i)
                if k >= 1:
                    act.wait_ge(sig_done, k + 2 * i)
                a_.activation(silu[:, 0], below[:], ACT.Exp).then_inc(elu_done, 1)
                act.wait_ge(sig_done, k + 1 + 2 * i)
                if k >= 1:
                    act.wait_ge(up_done, a + 2 * i)
                a_.activation(sig_hi[:], sig[:], ACT.Copy).then_inc(sig_hi_done, 1)

            def retrieved_before(a):
                return a - HEAD0

            def last_retrieved(a):
                act.wait_ge(ret_turned, a - HEAD0 + 1)
                act.wait_ge(down_done, a - 1)
                a_.activation(inner_hi[:, a % 2], ps[:, 2 * (a % 2), :], ACT.Copy).then_inc(inner_hi_done, 1)

            split_up(0, 0)
            split_down(0, 0)
            act.wait_ge(ones_stored, 16)
            for seg, (kind, half, base, n) in enumerate(SEGMENTS):
                if kind == FFN0:
                    act.wait_ge(comb_stored, 16 * (half + 1))

                def body(a, i, s):
                    if a < LAST_STEP:
                        split_up(a + 1, i)
                    if kind == HEADS:
                        head_step(a, i, s)
                    else:
                        ffn_step(a, i, half, kind == FFN0)
                    if a < LAST_STEP:
                        split_down(a + 1, i)
                    if s in (0, 1) and seg < 5:
                        split_act(6 + 2 * seg + s)
                    if seg == 0 and s == n - 2:
                        take_logits(1)
                        soften(1)
                    if seg == 0 and s == n - 1:
                        store_shares(1)

                steps(act, base, n, body)
                if kind == HEADS:
                    last_retrieved(base + n - 1)

        @block.vector
        def _(dve):
            v = nc.vector
            links = [0]

            def link(ins):
                links[0] += 1
                ins.then_inc(router, 1)
                dve.wait_ge(router, links[0])

            dve.wait_ge(const_ready, 3)
            v.tensor_copy(ident_r[:], ident[:])
            v.tensor_copy(ident_bf[:], ident[:])
            v.tensor_copy(causal_bf[:], causal[:]).then_inc(const_bf, 1)

            def mod_columns(l, q):
                dve.wait_ge(mod_turned, cols_count(l, q) + 1)
                v.tensor_scalar(modc[:, l, q * KC:(q + 1) * KC, :],
                                ps[:, MOD_BANK[MOD_CH * l + q], 0:KC * B].rearrange("p (m b) -> p m b", b=B),
                                1.0 if q in (1, 4) else 0.0, None, ALU.add).then_inc(mod_cols, 1)

            def make_gate(l, w):
                at = MOD_CH * l + (2, 5)[w]
                dve.wait_ge(row_ev, at + 1)
                if l == 1:
                    dve.wait_ge(gate_mm, w + 1)
                row = mod_row[:, at % 2]
                link(v.tensor_scalar(sign[:], row, 0.0, 2.0, ALU.is_ge, ALU.mult))
                gate = gate_row[:, w]
                link(v.scalar_tensor_tensor(gate, sign[:], -1.0, row, ALU.add, ALU.mult))
                link(v.tensor_scalar(gate, gate, 0.25, None, ALU.max))
                v.scalar_tensor_tensor(gate, sign[:], -1.0, gate, ALU.add, ALU.mult).then_inc(gate_row_done, 1)
                dve.wait_ge(gate_row_done, 2 * l + w + 1)

            def norm(n):
                tiles = half_tiles(n % 2)
                if n < 2:
                    dve.wait_ge(x_in[n % 2], 16)
                for j, t in enumerate(tiles):
                    v.bn_stats(stats[:, j, :], x[:, t, :]).then_inc(ln_tmp, 1)
                dve.wait_ge(ln_tmp, TH * (n + 1))
                for j, t in enumerate(tiles):
                    ins = v.bn_aggr(mv0[:, t, :] if n < 2 else mv[:, j, :], stats[:, j, :])
                ins.then_inc(ln_stats, 1)
                dve.wait_ge(ln_stats, n + 1)
                if n < 2:
                    return
                dve.wait_ge(ln_rstd, n + 1)
                for j, t in enumerate(tiles):
                    ins = v.tensor_scalar(xn[:, j, :], x[:, t, :], mv[:, j, 0:1], rstd[:, j:j + 1],
                                          ALU.subtract, ALU.mult)
                ins.then_inc(ln_xn, 1)

            def norm_batch(c):
                for j in range(2):
                    t = bass.ds(2 * c + j, 1)
                    ins = v.tensor_scalar(xn[:, j:j + 1, :], x[:, t, :], mv0[:, t, 0], rstd0[:, t],
                                          ALU.subtract, ALU.mult)
                ins.then_inc(xn0_done, 1)

            def modulate_batch(c):
                dve.wait_ge(turned, c + 1)
                dve.wait_ge(act_lo_done, c)
                for k in range(KC):
                    src = ps[:, 4 + k // 2, (k % 2) * S:(k % 2 + 1) * S]
                    ins = v.tensor_scalar(h32[:, 0, k, :], src, modc[:, 0, KC + k, bass.ds(c, 1)],
                                          modc[:, 0, k, bass.ds(c, 1)], ALU.mult, ALU.add)
                ins.then_inc(h32_done, 1)

            def rest_of_qkv(c, j):
                dve.wait_ge(qkv_hi_done, 2 * c + (j + 1))
                q = ps[:, 4, :].rearrange("p (h e) -> p h e", e=HD)
                v.tensor_tensor(q_parts[:, j, :, 1::2, :], q.unsqueeze(2).to_broadcast([P, NH, 2, HD]),
                                q_parts[:, j, :, 0::2, :].bitcast(FP), ALU.subtract)
                k = ps[:, 5, 0:P].rearrange("p (g e) -> p g e", e=HD)
                v.tensor_tensor(k_parts[:, j, :, 2:4, :], k.unsqueeze(2).to_broadcast([P, NKV, 2, HD]),
                                k_parts[:, j, :, 0:2, :].bitcast(FP), ALU.subtract)
                v.tensor_copy(v_next[:, j], ps[:, 5, P:2 * P].rearrange("p (g e) -> p g e", e=HD)).then_inc(qkv_lo_done, 1)

            def take_q(c, iblk):
                dve.wait_ge(q_turned, 4 * c + (2 * iblk + 2))
                v.tensor_copy(q_stack[:, iblk, PAIRS // 2:PAIRS, :].rearrange("p a t -> p (a t)"),
                              ps[:, 4:6, :].rearrange("p c n -> p (c n)")).then_inc(q_ev, 1)

            def take_k(c):
                dve.wait_ge(k_turned, c + 1)
                v.tensor_copy(k_stack[:, 2:4, :].rearrange("p g t -> p (g t)"), ps[:, 5, :]).then_inc(k_ev, 1)

            def take_v(c):
                dve.wait_ge(qkv_lo_done, 2 * c + 2)
                v.tensor_copy(v1[:, :, :, 0:HD], v_next[:]).then_inc(v_ev, 1)

            def modulate(m, banks):
                ln, b = m // B, m % B
                l, q = ln // 2, 3 * (ln % 2)
                dve.wait_ge(turned, m + 1)
                if m >= 2:
                    dve.wait_ge(act_lo_done, m - 1)
                for k in range(KC):
                    src = ps[:, banks + k // 2, (k % 2) * S:(k % 2 + 1) * S]
                    ins = v.tensor_scalar(h32[:, m % 2, k, :], src, modc[:, l, (q + 1) * KC + k, b:b + 1],
                                          modc[:, l, q * KC + k, b:b + 1], ALU.mult, ALU.add)
                ins.then_inc(h32_done, 1)

            def residual(seq, gate, down_scale, bank):
                for j, t in enumerate(half_tiles(seq % 2)):
                    ins = v.scalar_tensor_tensor(xn[:, j, :], ps[:, bank + j, :], down_scale,
                                                 gate[:, t // 2, :], ALU.mult, ALU.mult)
                ins.then_inc(addend_done, 1)
                dve.wait_ge(addend_done, seq + 1)
                tiles = half_tiles(seq % 2)
                v.tensor_tensor(x[:, tiles[0]:tiles[0] + TH, :], x[:, tiles[0]:tiles[0] + TH, :], xn[:],
                                ALU.add).then_inc(resid_done, 1)
                dve.wait_ge(resid_done, seq + 1)

            norm(0)
            mod_columns(0, 0)
            mod_columns(0, 1)
            dve.wait_ge(mod_cols, 2)
            dve.wait_ge(ln_rstd, 1)
            norm_batch(0)
            modulate_batch(0)
            dve.wait_ge(wqkv_hi_done, 1)
            v.tensor_tensor(wqkv_lo[:], wqkv_in[:], wqkv_hi[:].bitcast(FP), ALU.subtract).then_inc(wqkv_lo_done, 1)
            norm(1)
            rest_of_qkv(0, 0)
            make_gate(0, 0)
            rest_of_qkv(0, 1)
            dve.wait_ge(wqkv_hi_done, 2)
            v.tensor_tensor(wo_lo[:], wo_in[:], wo_hi[:].bitcast(FP), ALU.subtract).then_inc(wqkv_lo_done, 1)
            v.memset(v1[:, :, :, HD:VW], 1.0).then_inc(heads_taken, 1)
            take_v(0)
            dve.wait_ge(wqkv_lo_done, 2)
            take_q(0, 0)
            mod_columns(0, 3)
            take_k(0)
            mod_columns(0, 4)
            make_gate(0, 1)
            dve.wait_ge(gw_split, 1)
            v.tensor_tensor(gw_parts[:, :, E:2 * E], gw[:], gw_parts[:, :, 0:E].bitcast(FP), ALU.subtract).then_inc(gw_split, 1)
            dve.wait_ge(ln_rstd, 2)

            def attend(b, more):
                def normalise(q):
                    iblk = q // 2
                    dve.wait_ge(sums_turned, UNITS * b + (4 * q + 4))
                    o = ps[:, 7, 0:16 * VW].rearrange("p (h e) -> p h e", e=VW)
                    v.reciprocal(rsum[:, q % 2, :], o[:, :, HD]).then_inc(rsum_done, 1)
                    dve.wait_ge(rsum_done, 4 * b + (q + 1))
                    dst = heads_out[:, iblk, (q % 2) * 256:(q % 2 + 1) * 256].rearrange("p (h e) -> p h e", e=HD)
                    v.tensor_tensor(dst, o[:, :, 0:HD], rsum[:, q % 2, :].unsqueeze(2).to_broadcast([P, 16, HD]),
                                    ALU.mult).then_inc(heads_ev, 1)

                for n in range(UNITS):
                    iblk, r = n // NKV, n % 2
                    w = P * (iblk + 1)
                    sc = ps[:, 2 * r:2 * r + 2, 0:2 * w].rearrange("p c (h s) -> p c h s", h=2)
                    dve.wait_ge(scored, UNITS * b + (n + 1))
                    v.tensor_reduce(row_max[:, r, :].rearrange("p (c h) -> p c h", c=2), sc, AX.X, ALU.max).then_inc(max_done, 1)
                    dve.wait_ge(max_done, UNITS * b + (n + 1))
                    if n >= 2:
                        dve.wait_ge(probs_turned, UNITS * b + (n - 1))
                    v.tensor_tensor(shifted[:, r, :, 0:w].rearrange("p (c h) s -> p c h s", c=2), sc,
                                    row_max[:, r, :].rearrange("p (c h) -> p c h", c=2).unsqueeze(3)
                                    .to_broadcast([P, 2, 2, w]), ALU.subtract).then_inc(shift_done, 1)
                    if n >= 6 and (n - 6) % 4 == 0:
                        normalise((n - 6) // 4)
                    if more and n == 0:
                        norm_batch(b + 1)
                    if n == TURN_Q1 + 1:
                        take_q(b, 1)
                    if more and n == TURN_XN:
                        modulate_batch(b + 1)
                    for j in range(2):
                        if more and n == PROJECT[j]:
                            rest_of_qkv(b + 1, j)
                    if more and n == TURN_Q0 + 1:
                        take_q(b + 1, 0)
                if more:
                    take_k(b + 1)
                normalise(3)
                if more:
                    take_v(b + 1)
                dve.wait_ge(heads_hi, b + 1)
                lo = act_lo[:, :, b * S:(b + 1) * S] if isinstance(b, int) else act_lo[:, :, bass.ts(b, S)]
                hi = act_hi[:, :, b * S:(b + 1) * S] if isinstance(b, int) else act_hi[:, :, bass.ts(b, S)]
                v.tensor_tensor(lo, ps[:, 4:6, :].rearrange("p c (m s) -> p (c m) s", s=S),
                                hi.bitcast(FP), ALU.subtract).then_inc(heads_taken, 1)

            with dve.Fori(0, B - 1) as b:
                attend(b, True)
            attend(B - 1, False)

            def route(h):
                dve.wait_ge(logits_turned, h + 1)
                parts = ps[:, ROUTE_BANK[h], 0:2 * TH * E].rearrange("p (t a e) -> p t a e", a=2, e=E)
                link(v.tensor_copy(logits[:], parts[:, :, 0, :]))
                v.tensor_tensor(logits[:], logits[:], parts[:, :, 1, :], ALU.add).then_inc(logits_done, 1)
                dve.wait_ge(logits_done, h + 1)
                for j in range(TH):
                    link(v.max(top8[:, j, :], logits[:, j, :]))
                    link(v.max_index(top_at[:, j, :], top8[:, j, :], logits[:, j, :]))
                v.tensor_tensor(gap[:], top8[:, :, 1], top8[:, :, 0], ALU.subtract).then_inc(gap_done, 1)
                link(v.tensor_copy(top_f[:], top_at[:, :, 0:2]))
                dve.wait_ge(e2_done, h + 1)
                link(v.tensor_scalar(w2[:], e2[:], 1.0, None, ALU.add))
                link(v.reciprocal(w1[:], w2[:]))
                link(v.tensor_tensor(w2[:], w1[:], e2[:], ALU.mult))
                for j in range(TH):
                    v.tensor_scalar(pick1[:, j, :], iota_e[:], top_f[:, j, 0:1], w1[:, j:j + 1], ALU.is_equal, ALU.mult)
                    ins = v.tensor_scalar(pick2[:, j, :], iota_e[:], top_f[:, j, 1:2], w2[:, j:j + 1], ALU.is_equal, ALU.mult)
                link(ins)
                v.tensor_tensor(pick1[:], pick1[:], pick2[:], ALU.add).then_inc(comb_done, 1)

            dve.wait_ge(proj_done, 1)
            dve.wait_ge(gate_ev, 1)
            residual(0, gates[:, 0], 1.0, 4)
            norm(2)
            modulate(4, 4)
            modulate(5, 6)
            dve.wait_ge(proj_done, 2)
            residual(1, gates[:, 0], 1.0, 0)
            norm(3)
            mod_columns(1, 0)
            mod_columns(1, 1)
            make_gate(1, 0)
            route(0)
            mod_columns(1, 3)
            mod_columns(1, 4)
            make_gate(1, 1)

            def rest_of_inner(a, i):
                dve.wait_ge(inner_hi_done, a + 1 + 2 * i)
                if a >= 2:
                    dve.wait_ge(down_done, a - 1 + 2 * i)

            def ffn_step(a, i, layer0):
                r = a % 2
                dve.wait_ge(silu_done, ffn_count(a) + 1 + 2 * i)
                up_scale = 1.0 if layer0 else scales[:, 1:2]
                dst = inner[:, r]
                ins = v.scalar_tensor_tensor(dst, ps[:, 2 * r + 1, :], up_scale, silu[:, r], ALU.mult, ALU.mult)
                if layer0:
                    ins.then_inc(scaled_done, 1)
                    dve.wait_ge(scaled_done, a + 1 + 2 * i)
                    dve.wait_ge(share_in[r], 16 * (a // 2 + 1) + 16 * i)
                    ins = v.tensor_tensor(dst, inner[:, r], share[:, r], ALU.mult)
                ins.then_inc(inner_done, 1)
                rest_of_inner(a, i)
                v.tensor_tensor(inner_lo[:, r], inner[:, r], inner_hi[:, r].bitcast(FP),
                                ALU.subtract).then_inc(inner_lo_done, 1)

            def rest_of_retrieved(a, i):
                rest_of_inner(a, i)
                v.tensor_tensor(inner_lo[:, a % 2], ps[:, 2 * (a % 2), :], inner_hi[:, a % 2].bitcast(FP),
                                ALU.subtract).then_inc(inner_lo_done, 1)

            def head_step(a, i, s):
                r, k = a % 2, a - HEAD0
                if s != 0:
                    rest_of_retrieved(a - 1, i)
                dve.wait_ge(q1_done, k + 1 + 2 * i)
                if k >= 1:
                    dve.wait_ge(elu_done, k + 2 * i)
                bias = bq[:, bass.ds(k % H1 + 2 * i, 1)]
                v.tensor_scalar(below[:], ps[:, 2 * r, :], bias, 0.0, ALU.add, ALU.min).then_inc(below_done, 1)
                v.tensor_scalar(silu[:, 1], ps[:, 2 * r, :], bias, 0.0, ALU.add, ALU.max).then_inc(above_done, 1)
                dve.wait_ge(above_done, k + 1 + 2 * i)
                dve.wait_ge(elu_done, k + 1 + 2 * i)
                if k >= 1:
                    dve.wait_ge(sig_lo_done, k + 2 * i)
                v.tensor_tensor(sig[:], silu[:, 0], silu[:, 1], ALU.add).then_inc(sig_done, 1)
                dve.wait_ge(sig_hi_done, k + 1 + 2 * i)
                v.tensor_tensor(sig_lo[:], sig[:], sig_hi[:].bitcast(FP), ALU.subtract).then_inc(sig_lo_done, 1)
                dve.wait_ge(up_done, a + 1 + 2 * i)
                nd = [ps[:, c, 0:2 * MZ_W].rearrange("p (t w) -> p t w", w=MZ_W) for c in (1, 3)]
                for c in range(2):
                    ins = v.tensor_scalar(den[:, c, :], nd[c][:, :, P], DEN_EPS, None, ALU.add)
                ins.then_inc(den_done, 1)
                dve.wait_ge(den_done, k + 1 + 2 * i)
                v.reciprocal(rden[:], den[:]).then_inc(rden_done, 1)
                dve.wait_ge(rden_done, k + 1 + 2 * i)
                for c in range(2):
                    ins = v.tensor_tensor(inner[:, r, c * S:(c + 1) * S].rearrange("p (t e) -> p t e", t=2),
                                          nd[c][:, :, 0:P], rden[:, c, :].unsqueeze(2).to_broadcast([P, 2, P]), ALU.mult)
                ins.then_inc(ret_done, 1)

            for seg, (kind, half, base, n) in enumerate(SEGMENTS):
                def body(a, i, s):
                    if kind == HEADS:
                        head_step(a, i, s)
                    else:
                        ffn_step(a, i, kind == FFN0)
                    if s in (0, 1) and seg < 5:
                        modulate(6 + 2 * seg + s, 2 * ((a + 1) % 2))
                    if seg == 0 and s == n - 2:
                        route(1)

                steps(dve, base, n, body)
                if kind == HEADS:
                    rest_of_retrieved(base + n - 1, 0)
                dve.wait_ge(down_done, base + n)
                gate = (gates[:, 1], gates[:, 0], gate1b[:])[kind]
                residual(2 + seg, gate, scales[:, 2:3] if kind == FFN1 else 1.0, 4)
                if seg < 4:
                    norm(4 + seg)

        @block.tensor
        def _(pe):
            t_ = nc.tensor

            def three(out, w, xs, first, last):
                t_.matmul(out, w[0], xs[0], start=first, stop=False)
                t_.matmul(out, w[0], xs[1], start=False, stop=False)
                return t_.matmul(out, w[1], xs[0], start=False, stop=last)

            def modulation(at):
                pe.wait_ge(wmod_in[at % 2], 16 * (at // 2 + 1))
                for k in range(KC):
                    ins = t_.matmul(ps[0:B, MOD_BANK[at], :], silu_c[:, at // MOD_CH, k, :], wmod[:, at % 2, k, :],
                                    start=k == 0, stop=k == KC - 1)
                ins.then_inc(mod_mm, 1)

            def turn_row(at):
                pe.wait_ge(row_ev, at + 1)
                for m in range(KC):
                    c = m * B
                    ins = t_.transpose(ps[:, MOD_BANK[at], c:c + B], mod_row[:, at % 2, m * P:(m + 1) * P],
                                       ident[0:B, 0:B])
                ins.then_inc(mod_turned, 1)

            def gate_rows(c):
                pe.wait_ge(gate_row_done, c + 1)
                if c >= 1:
                    pe.wait_ge(gate_ev, c)
                for b in range(B):
                    ins = t_.matmul(ps[:, b, :], row_of[:, b, :], gate_row[:, c % 2, :], start=True, stop=True)
                ins.then_inc(gate_mm, 1)

            def turn(m, bank):
                for k in range(KC):
                    for j in range(2):
                        c = (k % 2) * S + j * P
                        ins = t_.transpose(ps[:, bank + k // 2, c:c + P],
                                           xn[:, 2 * (m % 2) + j, k * P:(k + 1) * P], ident[:])
                ins.then_inc(turned, 1)

            def turn_batch(c):
                pe.wait_ge(xn0_done, c + 1)
                for k in range(KC):
                    for j in range(2):
                        at = (k % 2) * S + j * P
                        ins = t_.transpose(ps[:, 4 + k // 2, at:at + P], xn[:, j, k * P:(k + 1) * P], ident[:])
                ins.then_inc(turned, 1)

            def project(c, j):
                pe.wait_ge(act_lo_done, c + 1)
                if j == 0:
                    pe.wait_ge(h32_done, c + 1)
                else:
                    pe.wait_ge(qkv_lo_done, 2 * c + 1)
                for bank, cols in ((4, slice(0, D)), (5, slice(D, QKV))):
                    for k in range(KC):
                        ins = three(ps[:, bank, 0:cols.stop - cols.start],
                                    (xa_hi[:, k, j * P:(j + 1) * P], xa_lo[:, k, j * P:(j + 1) * P]),
                                    (wqkv_hi[:, k, cols], wqkv_lo[:, k, cols]), k == 0, k == KC - 1)
                ins.then_inc(qkv_mm, 1)

            def stack_q(c, iblk, part):
                if part == 0 and iblk == 0:
                    pe.wait_ge(qkv_lo_done, 2 * c + 2)
                elif part == 0:
                    pe.wait_ge(heads_taken, c + 1)
                    pe.wait_ge(k_ev, 2 * c + 2)
                else:
                    pe.wait_ge(q_ev, 4 * c + (2 * iblk + 1))
                for a in range(PAIRS // 2):
                    h = 2 * (part * PAIRS // 2 + a)
                    both = q_parts[:, iblk, h:h + 2, :, :].rearrange("p h a e -> p (h a e)")
                    ins = t_.matmul(ps[:, 4 + a // 4, (a % 4) * P:(a % 4 + 1) * P], both, ident_r[:],
                                    start=True, stop=True)
                ins.then_inc(q_turned, 1)

            def stack_k(c):
                pe.wait_ge(q_ev, 4 * c + 2)
                for a in range(NKV // 2):
                    for j in range(2):
                        both = k_parts[:, j, 2 * a:2 * a + 2, :, :].rearrange("p g a e -> p (g a e)")
                        at = (a % 2) * S + j * P
                        ins = t_.matmul(ps[:, 4 + a // 2, at:at + P], both, ident_r[:], start=True, stop=True)
                ins.then_inc(k_turned, 1)

            pe.wait_ge(silu_c_done, 1)
            pe.wait_ge(const_ready, 3)
            modulation(0)
            modulation(1)
            turn_row(0)
            turn_row(1)
            turn_batch(0)
            pe.wait_ge(const_bf, 1)
            pe.wait_ge(wqkv_lo_done, 1)
            project(0, 0)
            modulation(2)
            project(0, 1)
            modulation(3)
            stack_q(0, 0, 0)
            turn_row(3)
            stack_q(0, 0, 1)
            modulation(4)
            stack_k(0)
            turn_row(4)
            modulation(5)
            pe.wait_ge(mod_cols, 4)
            pe.wait_ge(row_ev, 6)

            def attend(b, more):
                pe.wait_ge(k_ev, 2 * b + 2)
                pe.wait_ge(q_ev, 4 * b + 2)

                def score(n):
                    iblk, gr, r = n // NKV, n % NKV, n % 2
                    w = P * (iblk + 1)
                    if n >= 2:
                        pe.wait_ge(exp_done, UNITS * b + (n - 1))
                    if n == NKV:
                        pe.wait_ge(q_ev, 4 * b + 4)
                    rows = slice(STACK * (gr % 2), STACK * (gr % 2 + 1))
                    for h in range(REP):
                        t_.matmul(ps[:, 2 * r + h // 2, (h % 2) * w:(h % 2 + 1) * w],
                                  q_stack[rows, iblk, gr // 2 * REP + h, :], k_stack[rows, gr // 2, 0:w],
                                  start=h % 2 == 0, stop=True, skip_group_check=True)
                    for c in range(2):
                        ins = t_.matmul(ps[:, 2 * r + c, 0:2 * w].rearrange("p (h s) -> p h s", h=2)[:, :, w - P:w],
                                        ident_bf[:], causal_bf[:].unsqueeze(1).to_broadcast([P, 2, P]),
                                        start=False, stop=True, skip_group_check=True)
                    ins.then_inc(scored, 1)

                def turn_scores(n):
                    r = n % 2
                    pe.wait_ge(shift_done, UNITS * b + (n + 1))
                    for j in range(n // NKV + 1):
                        for h in range(REP):
                            ins = t_.transpose(ps[:, 2 * r + j, h * P:(h + 1) * P],
                                               shifted[:, r, h, j * P:(j + 1) * P], ident[:])
                    ins.then_inc(probs_turned, 1)

                def weigh(n):
                    iblk, gr, r = n // NKV, n % NKV, n % 2
                    pe.wait_ge(exp_done, UNITS * b + (n + 1))
                    if n == 0:
                        pe.wait_ge(v_ev, b + 1)
                    else:
                        pe.wait_ge(sums_ev, UNITS * b + n)
                    if n % 4 == 1 and n > 4:
                        pe.wait_ge(heads_ev, 4 * b + n // 4)
                    for j in range(iblk + 1):
                        ins = t_.matmul(ps[0:VW, 6, :], v1[:, j, gr, :], probsT[:, r, j, :], start=j == 0, stop=j == iblk)
                    ins.then_inc(pv_done, 1)

                def turn_sums(n):
                    for h in range(REP):
                        c = (n % 4 * REP + h) * VW
                        ins = t_.transpose(ps[:, 7, c:c + VW], sums[:, n % 2, h * P:(h + 1) * P], ident[0:VW, 0:VW])
                    ins.then_inc(sums_turned, 1)

                def meanwhile(n):
                    for part in range(2):
                        if n == TURN_Q1 + part:
                            stack_q(b, 1, part)
                        if more and n == TURN_Q0 + part:
                            stack_q(b + 1, 0, part)
                        if more and n == PROJECT[part]:
                            project(b + 1, part)
                    if more and n == TURN_XN:
                        pe.wait_ge(q_ev, 4 * b + 4)
                        turn_batch(b + 1)

                score(0)
                score(1)
                turn_scores(0)
                meanwhile(1)
                for n in range(2, UNITS):
                    score(n)
                    turn_scores(n - 1)
                    weigh(n - 2)
                    if n >= 3:
                        turn_sums(n - 3)
                    if n < UNITS - 1:
                        meanwhile(n)
                if more:
                    stack_k(b + 1)
                turn_scores(UNITS - 1)
                weigh(UNITS - 2)
                turn_sums(UNITS - 3)
                weigh(UNITS - 1)
                turn_sums(UNITS - 2)

                def turn_heads(iblk):
                    for k in range(KC):
                        c = (k % 2) * S + iblk * P
                        ins = t_.transpose(ps[:, 4 + k // 2, c:c + P], heads_out[:, iblk, k * P:(k + 1) * P], ident[:])
                    return ins

                if more:
                    pe.wait_ge(k_ev, 2 * b + 4)
                pe.wait_ge(sums_ev, UNITS * b + UNITS)
                turn_heads(0)
                turn_sums(UNITS - 1)
                pe.wait_ge(heads_ev, 4 * b + 4)
                ins = turn_heads(1)
                ins.then_inc(heads_turned, 1)

            with pe.Fori(0, B - 1) as b:
                attend(b, True)
            attend(B - 1, False)

            gate_rows(0)
            pe.wait_ge(heads_taken, B + 1)
            pe.wait_ge(wqkv_lo_done, 2)
            for half in range(2):
                if half == 1:
                    pe.wait_ge(gate_ev, 1)
                for j in range(TH):
                    t = half * TH + j
                    for k in range(KC):
                        ins = three(ps[:, 4 * (1 - half) + j, :],
                                    (act_hi[:, k, t * P:(t + 1) * P], act_lo[:, k, t * P:(t + 1) * P]),
                                    (wo_hi[:, k, :], wo_lo[:, k, :]), k == 0, k == KC - 1)
                ins.then_inc(proj_done, 1)
            for m in (4, 5):
                pe.wait_ge(ln_xn, 1)
                turn(m, 4 + 2 * (m % 2))
            for at, freed in ((0, 5), (1, 5), (2, 6), (3, 6)):
                pe.wait_ge(h32_done, freed)
                modulation(MOD_CH + at)
                if at == 2:
                    turn_row(MOD_CH)
                    turn_row(MOD_CH + 1)
            pe.wait_ge(addend_done, 2)
            gate_rows(1)

            def route(h, bank):
                pe.wait_ge(act_lo_done, 6 + 2 * h)
                cols = slice(h * HALF, (h + 1) * HALF)
                for k in range(KC):
                    for q, xa in enumerate((act_hi, act_lo)):
                        ins = t_.matmul(ps[0:2 * E, bank, :], gw_parts[:, k, :], xa[:, k, cols],
                                        start=(k, q) == (0, 0), stop=(k, q) == (KC - 1, 1))
                ins.then_inc(logits_mm, 1)
                pe.wait_ge(logits_ev, h + 1)
                for j in range(TH):
                    ins = t_.transpose(ps[:, bank, 2 * j * E:2 * (j + 1) * E], logitsT[:, j * P:(j + 1) * P],
                                       ident[0:2 * E, 0:2 * E])
                ins.then_inc(logits_turned, 1)

            def turn_shares(h, bank):
                pe.wait_ge(comb_done, h + 1)
                for j in range(TH):
                    ins = t_.transpose(ps[0:E, bank, j * P:(j + 1) * P], pick1[:, j, :], ident[:])
                ins.then_inc(comb_turned, 1)

            pe.wait_ge(row_ev, MOD_CH + 4)
            pe.wait_ge(gw_split, 2)
            route(0, ROUTE_BANK[0])
            pe.wait_ge(mod_cols, 6)
            modulation(MOD_CH + 4)
            turn_row(MOD_CH + 3)
            gate_rows(2)
            modulation(MOD_CH + 5)
            turn_row(MOD_CH + 4)
            gate_rows(3)
            turn_shares(0, SHARES_BANK[0])
            pe.wait_ge(gate_ev, 4)
            pe.wait_ge(mod_cols, 8)
            pe.wait_ge(comb_ev, 1)

            def down(a, i, s, seg):
                r = a % 2
                pe.wait_ge(down_lo, a + 1 + 2 * i)
                pe.wait_ge(inner_lo_done, a + 1 + 2 * i)
                if s == 0:
                    pe.wait_ge(resid_done, seg + 2)
                last = s is not None and s == SEGMENTS[seg][3] - 1
                for j in range(TH):
                    ins = three(ps[:, 4 + j, :], (inner_hi[:, r, j * P:(j + 1) * P], inner_lo[:, r, j * P:(j + 1) * P]),
                                (w_hi[:, r, UP_W:UP_W + D], w_lo[:, r, UP_W:UP_W + D]), s == 0, last)
                ins.then_inc(down_done, 1)

            def xs_of(half):
                cols = slice(half * HALF, (half + 1) * HALF)
                return lambda k: (act_hi[:, k, cols], act_lo[:, k, cols])

            def ffn_step(a, i, s, seg, half):
                r, xs = a % 2, xs_of(half)
                pe.wait_ge(up_lo, a + 1 + 2 * i)
                if a >= 2:
                    pe.wait_ge(inner_done_of(a - 2), inner_count(a - 2) + 1 + 2 * i)
                for q in range(2):
                    for k in range(KC):
                        c = (2 * k + q) * P
                        ins = three(ps[:, 2 * r + q, :], (w_hi[:, r, c:c + P], w_lo[:, r, c:c + P]), xs(k),
                                    k == 0, k == KC - 1)
                ins.then_inc(up_done, 1)
                if s != 0:
                    down(a - 1, i, None if s is None else s - 1, seg)

            def inner_done_of(a):
                return ret_done if kind_of(a) == HEADS else inner_done

            def inner_count(a):
                if kind_of(a) == HEADS:
                    return a - HEAD0
                return ffn_count(a)

            def turn_retrieved(a, i):
                r, k = a % 2, a - HEAD0
                pe.wait_ge(ret_done, k + 1 + 2 * i)
                for j in range(TH):
                    ins = t_.transpose(ps[:, 2 * r, j * P:(j + 1) * P], inner[:, r, j * P:(j + 1) * P], ident[:])
                ins.then_inc(ret_turned, 1)

            def head_step(a, i, s, seg, half):
                r, xs, k_ = a % 2, xs_of(half), a - HEAD0
                pe.wait_ge(up_lo, a + 1 + 2 * i)
                for k in range(KC):
                    if k == KC // 2 and s != 0:
                        turn_retrieved(a - 1, i)
                    ins = three(ps[:, 2 * r, :], (w_hi[:, r, k * P:(k + 1) * P], w_lo[:, r, k * P:(k + 1) * P]),
                                xs(k), k == 0, k == KC - 1)
                ins.then_inc(q1_done, 1)
                if s != 0:
                    down(a - 1, i, None if s is None else s - 1, seg)
                pe.wait_ge(sig_lo_done, k_ + 1 + 2 * i)
                if k_ >= 1:
                    pe.wait_ge(ret_done, k_ + 2 * i)
                for j in range(TH):
                    c = (j % 2) * MZ_W
                    ins = three(ps[:, 2 * (j // 2) + 1, c:c + MZ_W],
                                (sig_hi[:, j * P:(j + 1) * P], sig_lo[:, j * P:(j + 1) * P]),
                                (w_hi[:, r, MZ:MZ + MZ_W], w_lo[:, r, MZ:MZ + MZ_W]), True, True)
                ins.then_inc(up_done, 1)

            for seg, (kind, half, base, n) in enumerate(SEGMENTS):
                pe.wait_ge(act_lo_done, 6 + 2 * seg)

                def body(a, i, s):
                    s_at = a - base
                    if s_at in (1, 2) and seg < 5:
                        pe.wait_ge(h32_done, 6 + 2 * seg + s_at)
                    if seg == 0 and s == n - 1:
                        pe.wait_ge(logits_done, 2)
                    if seg == 1 and s == 0:
                        pe.wait_ge(comb_ev, 2)
                    (head_step if kind == HEADS else ffn_step)(a, i, s, seg, half)
                    if s in (0, 1) and seg < 5:
                        m = 6 + 2 * seg + s
                        pe.wait_ge(ln_xn, m // 2 - 1)
                        if kind == HEADS:
                            pe.wait_ge(ret_done, a - HEAD0 + 1)
                        elif a >= 1:
                            pe.wait_ge(inner_done_of(a - 1), inner_count(a - 1) + 1)
                        turn(m, 2 * ((a + 1) % 2))
                    if seg == 0 and s in (n - 2, n - 1):
                        pe.wait_ge(inner_done_of(a - 1), inner_count(a - 1) + 1)
                        if s == n - 2:
                            route(1, ROUTE_BANK[1])
                        else:
                            turn_shares(1, SHARES_BANK[1])
                steps(pe, base, n, body)
                a = base + n - 1
                if kind == HEADS:
                    turn_retrieved(a, 0)
                down(a, 0, n - 1, seg)


def _chunks(w_gate, w_up, w_down):
    gu = np.stack([w_gate, w_up])
    gu = gu.reshape(2, P, KC, P).transpose(3, 2, 0, 1).reshape(P, UP_W)
    return np.concatenate([gu, w_down.T], axis=1)


def _by_k(w):
    return np.ascontiguousarray(w.reshape(KC, P, -1).transpose(1, 0, 2))


def kernel(**inputs):
    import concourse.bacc as bacc
    from concourse.bass_utils import run_bass_kernel_spmd

    f = {k: np.asarray(v) for k, v in inputs.items()}
    nc = bacc.Bacc("TRN2", target_bir_lowering=False, num_devices=1)

    wq = f["L0_attn_wq"].reshape(D, NKV // 2, 2, REP, HD).transpose(0, 1, 3, 2, 4).reshape(D, NH * HD)
    wqkv = np.concatenate([wq, f["L0_attn_wk"], f["L0_attn_wv"]], axis=1)
    sgu, sdn = f["L0_ffn_shared_w_gate_up"], f["L0_ffn_shared_w_down"]
    rows = [slice(c * P, (c + 1) * P) for c in range(SHARED)]
    ffn0 = [_chunks(sgu[:D][r], sgu[D:][r], sdn[:, r]) for r in rows]
    ffn0 += [_chunks(f["L0_ffn_w_gate_up"][e, :P], f["L0_ffn_w_gate_up"][e, P:], f["L0_ffn_w_down"][e])
             for e in range(E)]
    pad = N_STEPS[FFN1] * P - FF
    gate, up = (np.pad(f[k], ((0, pad), (0, 0))) for k in ("L1_ffn_gate_w", "L1_ffn_up_w"))
    down = np.pad(f["L1_ffn_down_w"], ((0, 0), (0, pad)))
    rows = [slice(c * P, (c + 1) * P) for c in range(N_STEPS[FFN1])]
    ffn1 = [_chunks(gate[r], up[r], down[:, r]) for r in rows]
    heads = []
    for h in range(H1):
        q = f["L1_attn_Wq"][h * G1 * P:(h * G1 + 1) * P]
        q = q.reshape(P, KC, P).transpose(2, 1, 0).reshape(P, KC * P)
        z = f["L1_attn_z"][h][:, None]
        wo = f["L1_attn_Wo"][:, h * G1 * P:(h + 1) * G1 * P]
        wo = wo.reshape(D, G1, P).transpose(2, 1, 0).reshape(P, G1 * D)
        heads.append(np.concatenate([q, f["L1_attn_M"][h], z, z, wo], axis=1))
    arrays = {
        "x": f["L0_attn_x"].reshape(T // P, P, D).transpose(1, 0, 2),
        "cond": np.stack([f[f"L{l}_c"].reshape(B, KC, P).transpose(2, 1, 0) for l in range(2)]),
        "wmod": np.stack([f[f"L{l}_wmod"].reshape(KC, P, MOD_CH, D).transpose(2, 1, 0, 3) for l in range(2)]),
        "wqkv": _by_k(wqkv),
        "wo": _by_k(f["L0_attn_wo"]),
        "gate_w": _by_k(f["L0_ffn_gate_w"].T),
        "bq": f["L1_attn_bq"].reshape(H1, G1, P)[:, 0].T,
        "scales": np.stack([f[f"L1_ffn_{k}_scale"].reshape(()) for k in ("gate", "up", "down")]).reshape(1, 3),
        "ffn0": np.stack(ffn0), "heads": np.stack(heads), "ffn1": np.stack(ffn1),
    }
    arrays = {f"in_{k}": np.ascontiguousarray(a) for k, a in arrays.items()}
    d = {k[3:]: nc.dram_tensor(k, a.shape, FP, kind="ExternalInput").ap() for k, a in arrays.items()}
    d["chunks"] = {FFN0: d["ffn0"], HEADS: d["heads"], FFN1: d["ffn1"]}
    d["comb"] = nc.dram_tensor("comb", [SHARED + E, T], FP, kind="Internal").ap()
    d["out"] = nc.dram_tensor("out", [P, T // P, D], FP, kind="ExternalOutput").ap()
    build(nc, d)
    r = run_bass_kernel_spmd(nc, [arrays], core_ids=[0])
    return np.asarray(r.results[0]["out"]).transpose(1, 0, 2).reshape(B, S, D)
```

```python
from contextlib import ExitStack

import numpy as np

import concourse.bass as bass
from concourse import mybir

FP = mybir.dt.float32
FR = mybir.dt.float32r
BF = mybir.dt.bfloat16
U32 = mybir.dt.uint32
ALU = mybir.AluOpType
ACT = mybir.ActivationFunctionType
AX = mybir.AxisListType

P = 128
D = 512
KC = D // P
B, S = 4, 256
T = B * S
HALF = T // 2
TH = HALF // P
NH, NKV, HD = 32, 8, 16
REP = NH // NKV
VW = HD + 1
QKV = NH * HD + 2 * NKV * HD
STACK = 4 * HD
PAIRS = NH // 2
E = 16
SHARED = 4
H1 = 8
G1 = 4
FF = 1376
FFN_W = KC * 2 * P + D
UP_W = KC * 2 * P
MZ = KC * P
MZ_W = P + 2
HEAD_W = KC * P + MZ_W + G1 * D
EPS = 1e-5
DEN_EPS = 1e-6
NEG = -1e30
MOD_CH = 6
ROUTE_BANK = (6, 2)
SHARES_BANK = (6, 0)
MOD_BANK = (0, 1, 2, 3, 6, 7, 4, 5, 6, 7, 4, 5)

FFN0, HEADS, FFN1 = range(3)
N_STEPS = {FFN0: SHARED + E, HEADS: H1, FFN1: (FF + P - 1) // P}
SEGMENTS = []
_at = 0
for _kind in (FFN0, HEADS, FFN1):
    for _half in range(2):
        SEGMENTS.append((_kind, _half, _at, N_STEPS[_kind]))
        _at += N_STEPS[_kind]
HEAD0 = 2 * N_STEPS[FFN0]
LAST_STEP = _at - 1
UNITS = 2 * NKV
TURN_Q1 = (2, 4)
TURN_XN = 5
PROJECT = (9, 11)
TURN_Q0 = (13, 14)

PEELED = 5

OTHER_HALF = {(FFN0, FFN0): (0, 0, 1, 2, 3, 4), (FFN0, HEADS): (0, 1, 2, 3, 4, 5),
              (HEADS, HEADS): (1, 2, 3, 4, 5, 6), (HEADS, FFN1): (0, 0, 1, 2, 3, 4),
              (FFN1, FFN1): (0, 0, None, None, None, None)}


def other_half(seg):
    return OTHER_HALF[SEGMENTS[max(seg, 1) - 1][0], SEGMENTS[max(seg, 1)][0]]


def turning(seg, s):
    turns = other_half(seg)[4:]
    return 6 + 2 * seg + turns.index(s) if s is not None and s in turns else None


def is_first(seg, s):
    return seg == 2 and s == 0


def steps(eng, base, n, body):
    if n == H1:
        for s in range(n):
            body(base + s, 0, s)
        return
    pairs = (n - PEELED - 2) // 2
    for s in range(PEELED):
        body(base + s, 0, s)
    with eng.Fori(0, pairs) as i:
        body(base + PEELED, i, None)
        body(base + PEELED + 1, i, None)
    for s in range(PEELED + 2 * pairs, n):
        body(base + s, 0, s)


def build(nc, d):
    ctx = ExitStack()
    with ctx:
        def sem(name):
            return ctx.enter_context(nc.semaphore(name))

        def sb(name, shape, dt=FP, where=ctx):
            return where.enter_context(nc.sbuf_tensor(name, shape, dt))

        x = sb("x", [P, T // P, D])
        act_hi = sb("act_hi", [P, KC, T], FR)
        act_lo = sb("act_lo", [P, KC, T], FR)
        wmod = sb("wmod", [P, 2, KC, D])
        xn = sb("xn", [P, TH, D])
        h32 = sb("h32", [P, 2, KC, S])
        ident = sb("ident", [P, P])
        ident_r = sb("ident_r", [P, P], FR)
        ident_bf = sb("ident_bf", [P, P], BF)
        causal = sb("causal", [P, P])
        causal_bf = sb("causal_bf", [P, P], BF)
        cond = sb("cond", [P, 2, KC, B])
        silu_c = sb("silu_c", [P, 2, KC, B])
        mod_row = sb("mod_row", [B, 2, D])
        gate_row = sb("gate_row", [B, 2, D])
        row_of = sb("row_of", [B, B, P])
        modc = sb("modc", [P, 2, MOD_CH * KC, B])
        sign = sb("sign", [B, D])
        stats = sb("stats", [P, TH, 6])
        mv = sb("mv", [P, TH, 2])
        var_eps = sb("var_eps", [P, TH])
        rstd = sb("rstd", [P, TH])
        mv0 = sb("mv0", [P, T // P, 2])
        rstd0 = sb("rstd0", [P, T // P])
        minus_half = sb("minus_half", [P, TH])
        scales = sb("scales", [P, 3])
        one = sb("one", [P, 1])
        bq = sb("bq", [P, H1])
        iota_e = sb("iota_e", [P, E])
        ones_row = sb("ones_row", [SHARED, P])
        gw = sb("gw", [P, KC, E])
        gw_parts = sb("gw_parts", [P, KC, 2 * E], FR)

        early = ExitStack()
        wo_hi = sb("wo_hi", [P, KC, D], FR, early)
        wo_lo = sb("wo_lo", [P, KC, D], FR, early)
        wqkv_hi = sb("wqkv_hi", [P, KC, QKV], FR, early)
        wqkv_lo = sb("wqkv_lo", [P, KC, QKV], FR, early)
        xa_hi = sb("xa_hi", [P, KC, S], FR, early)
        xa_lo = sb("xa_lo", [P, KC, S], FR, early)
        q_parts = sb("q_parts", [P, 2, NH, 4, HD], FR, early)
        k_parts = sb("k_parts", [P, 2, NKV, 4, HD], FR, early)
        v_next = sb("v_next", [P, 2, NKV, HD], FP, early)
        v1 = sb("v1", [P, 2, NKV, VW], FP, early)
        row_max = sb("row_max", [P, 2, REP], FP, early)
        rsum = sb("rsum", [P, 2, 16], FP, early)
        loading = ExitStack()
        wqkv_in = sb("wqkv_in", [P, KC, QKV], FP, loading)
        wo_in = sb("wo_in", [P, KC, D], FP, loading)
        loading.close()
        q_stack = sb("q_stack", [P, 2, PAIRS, P], FR, early)
        k_stack = sb("k_stack", [P, NKV // 2, S], FR, early)
        shifted = sb("shifted", [P, 2, REP, S], FP, early)
        probsT = sb("probsT", [P, 2, 2, REP * P], FP, early)
        early.close()

        w_in = sb("w_in", [P, 2, HEAD_W])
        w_hi = sb("w_hi", [P, 2, FFN_W], FR)
        w_lo = sb("w_lo", [P, 2, FFN_W], FR)
        silu = sb("silu", [P, 2, HALF])
        inner = sb("inner", [P, 2, HALF])
        inner_hi = sb("inner_hi", [P, 2, HALF], FR)
        inner_lo = sb("inner_lo", [P, 2, HALF], FR)
        share = sb("share", [P, 2, HALF])
        below = sb("below", [P, HALF])
        sig = sb("sig", [P, HALF])
        sig_hi = sb("sig_hi", [P, HALF], FR)
        sig_lo = sb("sig_lo", [P, HALF], FR)
        den = sb("den", [P, 2, 2])
        rden = sb("rden", [P, 2, 2])
        logits = sb("logits", [P, TH, E])
        top8 = sb("top8", [P, TH, 8])
        top_at = sb("top_at", [P, TH, 8], U32)
        top_f = sb("top_f", [P, TH, 2])
        gap = sb("gap", [P, TH])
        e2 = sb("e2", [P, TH])
        w1 = sb("w1", [P, TH])
        w2 = sb("w2", [P, TH])
        pick1 = sb("pick1", [P, TH, E])
        pick2 = sb("pick2", [P, TH, E])
        combT = sb("combT", [E, HALF])
        logitsT = sb("logitsT", [2 * E, HALF])
        gate1b = sb("gate1b", [P, B, D])
        gates = sb("gates", [P, 2, B, D])

        heads_out = xn[:, 2:4, :]
        sums = h32[0:VW, 1].rearrange("v k s -> v (k s)").rearrange("v (r q) -> v r q", r=2)
        ps = ctx.enter_context(nc.psum_tensor("ps", [P, 8, 512], FP))

        x_in = [sem(f"x_in{h}") for h in range(2)]
        small_in = sem("small_in")
        late_in = sem("late_in")
        wqkv_arrived = sem("wqkv_arrived")
        wo_arrived = sem("wo_arrived")
        wmod_in = [sem(f"wmod_in{r}") for r in range(2)]
        up_arrived = [sem(f"up_arrived{r}") for r in range(2)]
        down_arrived = [sem(f"down_arrived{r}") for r in range(2)]
        ones_stored = sem("ones_stored")
        comb_stored = sem("comb_stored")
        sum_stored = [sem(f"sum_stored{r}") for r in range(2)]
        share_in = [sem(f"share_in{r}") for r in range(2)]
        out_stored = sem("out_stored")
        const_zero = sem("const_zero")
        const_ready = sem("const_ready")
        const_bf = sem("const_bf")
        ones_ready = sem("ones_ready")
        silu_c_done = sem("silu_c_done")
        mod_mm = sem("mod_mm")
        row_ev = sem("row_ev")
        mod_turned = sem("mod_turned")
        mod_cols = sem("mod_cols")
        gate_row_done = sem("gate_row_done")
        gate_mm = sem("gate_mm")
        gate_ev = sem("gate_ev")
        ln_tmp = sem("ln_tmp")
        ln_stats = sem("ln_stats")
        ln_eps = sem("ln_eps")
        ln_rstd = sem("ln_rstd")
        xn0_done = sem("xn0_done")
        ln_xn = sem("ln_xn")
        turned = sem("turned")
        half_taken = sem("half_taken")
        h32_done = sem("h32_done")
        act_hi_done = sem("act_hi_done")
        act_lo_done = sem("act_lo_done")
        gw_split = sem("gw_split")
        wqkv_hi_done = sem("wqkv_hi_done")
        wqkv_lo_done = sem("wqkv_lo_done")
        qkv_mm = sem("qkv_mm")
        qkv_hi_done = sem("qkv_hi_done")
        qkv_lo_done = sem("qkv_lo_done")
        q_turned = sem("q_turned")
        q_ev = sem("q_ev")
        k_turned = sem("k_turned")
        k_ev = sem("k_ev")
        v_ev = sem("v_ev")
        scored = sem("scored")
        max_done = sem("max_done")
        shift_done = sem("shift_done")
        probs_turned = sem("probs_turned")
        exp_done = sem("exp_done")
        pv_done = sem("pv_done")
        sums_ev = sem("sums_ev")
        sums_turned = sem("sums_turned")
        rsum_done = sem("rsum_done")
        heads_ev = sem("heads_ev")
        heads_turned = sem("heads_turned")
        heads_hi = sem("heads_hi")
        heads_taken = sem("heads_taken")
        proj_done = sem("proj_done")
        addend_done = sem("addend_done")
        resid_done = sem("resid_done")
        logits_mm = sem("logits_mm")
        logits_ev = sem("logits_ev")
        logits_turned = sem("logits_turned")
        logits_done = sem("logits_done")
        router = sem("router")
        gap_done = sem("gap_done")
        e2_done = sem("e2_done")
        comb_done = sem("comb_done")
        comb_turned = sem("comb_turned")
        comb_ev = sem("comb_ev")
        group_pair = sem("group_pair")
        group_sum = sem("group_sum")
        up_hi = sem("up_hi")
        up_lo = sem("up_lo")
        down_hi = sem("down_hi")
        down_lo = sem("down_lo")
        up_done = sem("up_done")
        down_done = sem("down_done")
        silu_done = sem("silu_done")
        scaled_done = sem("scaled_done")
        inner_done = sem("inner_done")
        inner_hi_done = sem("inner_hi_done")
        inner_lo_done = sem("inner_lo_done")
        q1_done = sem("q1_done")
        below_done = sem("below_done")
        above_done = sem("above_done")
        elu_done = sem("elu_done")
        sig_done = sem("sig_done")
        sig_hi_done = sem("sig_hi_done")
        sig_lo_done = sem("sig_lo_done")
        den_done = sem("den_done")
        rden_done = sem("rden_done")
        ret_done = sem("ret_done")
        ret_turned = sem("ret_turned")

        block = ctx.enter_context(nc.Block())

        def cols_count(l, q):
            return 4 * l + (0, 1, None, 2, 3)[q]

        def mod_used(at):
            l, q = at // MOD_CH, at % MOD_CH
            return (gate_row_done, 2 * l + (1 if q == 2 else 2)) if q in (2, 5) else \
                (mod_turned, cols_count(l, q) + 1)

        def turn_banks(a, kind):
            q = 2 * ((a + 1) % 2)
            return (q, q if kind == HEADS else q + 1)

        def half_tiles(half):
            return range(half * TH, (half + 1) * TH)

        def kind_of(a):
            return next(k for k, _, base, n in SEGMENTS if base <= a < base + n)

        def ffn_count(a):
            return a if a < HEAD0 else a - 2 * H1

        def chunk_of(a, i):
            kind, _, base, _ = next(s for s in SEGMENTS if s[2] <= a < s[2] + s[3])
            return kind, a - base + 2 * i

        @block.sync
        def _(sp):
            for l in range(2):
                sp.dma_start(cond[:, l], d["cond"][l]).then_inc(small_in, 16)
            sp.dma_start(wmod[:, 0], d["wmod"][0, 0]).then_inc(wmod_in[0], 16)
            sp.dma_start(x[:, 0:TH], d["x"][:, 0:TH]).then_inc(x_in[0], 16)
            sp.dma_start(wmod[:, 1], d["wmod"][0, 1]).then_inc(wmod_in[1], 16)
            sp.dma_start(wqkv_in[:], d["wqkv"]).then_inc(wqkv_arrived, 16)
            sp.dma_start(x[:, TH:2 * TH], d["x"][:, TH:2 * TH]).then_inc(x_in[1], 16)
            for j in range(2, 4):
                sp.wait_ge(mod_mm, j - 1)
                sp.dma_start(wmod[:, j % 2], d["wmod"][0, j]).then_inc(wmod_in[j % 2], 16)
            sp.dma_start(wo_in[:], d["wo"]).then_inc(wo_arrived, 16)
            sp.dma_start(gw[:], d["gate_w"]).then_inc(late_in, 16)
            sp.dma_start(bq[:], d["bq"]).then_inc(late_in, 16)
            sp.dma_start(scales[:], d["scales"].to_broadcast([P, 3])).then_inc(late_in, 16)
            sp.wait_ge(ones_ready, 1)
            sp.dma_start(d["comb"][0:SHARED, :].rearrange("s (r t) -> s r t", t=P),
                         ones_row[:].unsqueeze(1).to_broadcast([SHARED, T // P, P])).then_inc(ones_stored, 16)
            for j in range(4, 2 * MOD_CH):
                sp.wait_ge(mod_mm, j - 1)
                sp.dma_start(wmod[:, j % 2], d["wmod"][j // MOD_CH, j % MOD_CH]).then_inc(wmod_in[j % 2], 16)

            def load(a, i, s):
                if a == 0:
                    sp.wait_ge(proj_done, 2)
                kind, c = chunk_of(a, i)
                up, end = (MZ + MZ_W, HEAD_W) if kind == HEADS else (UP_W, FFN_W)
                source = d["chunks"][kind][c]
                if a >= 2:
                    sp.wait_ge(up_lo, a - 1 + 2 * i)
                    if kind_of(a - 2) != kind:
                        sp.wait_ge(down_lo, a - 1)
                sp.dma_start(w_in[:, a % 2, 0:up], source[..., 0:up]).then_inc(up_arrived[a % 2], 16)
                if a >= 2:
                    sp.wait_ge(down_lo, a - 1 + 2 * i)
                if HEAD0 + 2 <= a < HEAD0 + H1:
                    sp.wait_ge(sum_stored[a % 2], 16 * ((a - HEAD0) // 2))
                if HEAD0 + H1 <= a < HEAD0 + 2 * H1:
                    sp.wait_ge(sum_stored[a % 2], 16 * H1 // 2)
                    sp.dma_start(w_in[:, a % 2, up:up + D], d["group_sums"][c]).then_inc(down_arrived[a % 2], 16)
                    return
                sp.dma_start(w_in[:, a % 2, up:end], source[..., up:end]).then_inc(down_arrived[a % 2], 16)

            for _, _, base, n in SEGMENTS:
                steps(sp, base, n, load)
            for h in range(2):
                sp.wait_ge(resid_done, 7 + h)
                sp.dma_start(d["out"][:, h * TH:(h + 1) * TH], x[:, h * TH:(h + 1) * TH]).then_inc(out_stored, 16)
            sp.wait_ge(out_stored, 32)

        @block.gpsimd
        def _(pool):
            g = nc.gpsimd
            g.memset(ident[:], 0.0).then_inc(const_zero, 1)
            g.memset(causal[:], 0.0).then_inc(const_zero, 1)
            g.memset(minus_half[:], -0.5).then_inc(const_zero, 1)
            g.memset(one[:], 1.0).then_inc(const_zero, 1)
            g.memset(ones_row[:], 1.0).then_inc(ones_ready, 1)
            g.memset(row_of[:], 0.0).then_inc(const_zero, 1)
            g.iota(iota_e[:], pattern=[[1, E]], base=0, channel_multiplier=0,
                   allow_small_or_imprecise_dtypes=True).then_inc(const_zero, 1)
            pool.wait_ge(const_zero, 6)
            g.affine_select(out=ident[:], in_=ident[:], compare_op=ALU.not_equal, fill=1.0,
                            base=0, pattern=[[-1, P]], channel_multiplier=1).then_inc(const_ready, 1)
            g.affine_select(out=causal[:], in_=causal[:], compare_op=ALU.is_ge, fill=NEG,
                            base=0, pattern=[[-1, P]], channel_multiplier=1).then_inc(const_ready, 1)
            g.affine_select(out=row_of[:], in_=row_of[:], compare_op=ALU.not_equal, fill=1.0,
                            base=0, pattern=[[-1, B], [0, P]], channel_multiplier=1).then_inc(const_ready, 1)

            def ln_root(n):
                h = slice(n * TH, (n + 1) * TH)
                var, root = (mv0[:, h, 1], rstd0[:, h]) if n < 2 else (mv[:, :, 1], rstd[:])
                pool.wait_ge(ln_stats, n + 1)
                g.tensor_scalar(var_eps[:], var, EPS, 1.0, ALU.add, ALU.mult).then_inc(ln_eps, 1)
                pool.wait_ge(ln_eps, n + 1)
                g.tensor_tensor(root, var_eps[:], minus_half[:], ALU.pow).then_inc(ln_rstd, 1)

            def rest_of_batch(c):
                pool.wait_ge(act_hi_done, c + 1)
                g.tensor_tensor(xa_lo[:], h32[:, 0], xa_hi[:].bitcast(FP), ALU.subtract).then_inc(act_lo_done, 1)

            def rest_of_act(m):
                b = m % B
                pool.wait_ge(act_hi_done, m + 1)
                cols = slice(b * S, (b + 1) * S)
                g.tensor_tensor(act_lo[:, :, cols], h32[:, m % 2], act_hi[:, :, cols].bitcast(FP),
                                ALU.subtract).then_inc(act_lo_done, 1)

            def sum_group(a, i):
                r, k, q = a % 2, a - HEAD0, MZ + MZ_W
                pool.wait_ge(down_arrived[r], 16 * (a // 2 + 1) + 16 * i)
                g.tensor_tensor(w_in[:, r, q:q + 2 * D], w_in[:, r, q:q + 2 * D],
                                w_in[:, r, q + 2 * D:q + 4 * D], ALU.add).then_inc(group_pair, 1)
                pool.wait_ge(group_pair, k + 1 + 2 * i)
                g.tensor_tensor(w_in[:, r, q:q + D], w_in[:, r, q:q + D],
                                w_in[:, r, q + D:q + 2 * D], ALU.add).then_inc(group_sum, 1)
                pool.wait_ge(group_sum, k + 1 + 2 * i)

            def rest_of_up(a, i):
                r, used = a % 2, MZ + MZ_W if kind_of(a) == HEADS else UP_W
                pool.wait_ge(up_hi, a + 1 + 2 * i)
                g.tensor_tensor(w_lo[:, r, 0:used], w_in[:, r, 0:used], w_hi[:, r, 0:used].bitcast(FP),
                                ALU.subtract).then_inc(up_lo, 1)

            def rest_of_down(a, i):
                r, down = a % 2, MZ + MZ_W if kind_of(a) == HEADS else UP_W
                pool.wait_ge(down_hi, a + 1 + 2 * i)
                g.tensor_tensor(w_lo[:, r, UP_W:UP_W + D], w_in[:, r, down:down + D],
                                w_hi[:, r, UP_W:UP_W + D].bitcast(FP), ALU.subtract).then_inc(down_lo, 1)

            ln_root(0)
            rest_of_batch(0)
            ln_root(1)
            with pool.Fori(0, B - 1) as b:
                rest_of_batch(b + 1)
            ln_root(2)
            rest_of_act(4)
            rest_of_act(5)
            ln_root(3)
            rest_of_up(0, 0)
            rest_of_down(0, 0)
            for seg, (kind, half, base, n) in enumerate(SEGMENTS):
                def body(a, i, s):
                    if a < LAST_STEP:
                        next_is_head = HEAD0 <= a + 1 < HEAD0 + H1
                        if kind == HEADS:
                            rest_of_up(a + 1, i)
                            if not is_first(seg, s):
                                rest_of_down(a, i)
                            if next_is_head:
                                sum_group(a + 1, i)
                        else:
                            if next_is_head:
                                sum_group(a + 1, i)
                            rest_of_up(a + 1, i)
                            rest_of_down(a + 1, i)
                    if 1 <= seg < 5 and s == other_half(seg)[2]:
                        ln_root(3 + seg)
                    if turning(seg, s) is not None:
                        rest_of_act(turning(seg, s))

                steps(pool, base, n, body)
                if seg == 3:
                    rest_of_down(base + n, 0)

        @block.scalar
        def _(act):
            a_ = nc.scalar
            act.wait_ge(small_in, 2 * 16)
            a_.activation(silu_c[:], cond[:], ACT.Silu).then_inc(silu_c_done, 1)

            def take_row(at):
                act.wait_ge(mod_mm, at + 1)
                if at >= 2:
                    done, count = mod_used(at - 2)
                    act.wait_ge(done, count)
                a_.activation(mod_row[:, at % 2], ps[0:B, MOD_BANK[at], :], ACT.Copy).then_inc(row_ev, 1)

            def split_act(m):
                b = m % B
                act.wait_ge(h32_done, m + 1)
                a_.activation(act_hi[:, :, b * S:(b + 1) * S], h32[:, m % 2], ACT.Copy).then_inc(act_hi_done, 1)

            def split_batch(c):
                act.wait_ge(h32_done, c + 1)
                a_.activation(xa_hi[:], h32[:, 0], ACT.Copy).then_inc(act_hi_done, 1)

            def split_qkv(c, j):
                act.wait_ge(qkv_mm, 2 * c + (j + 1))
                a_.activation(q_parts[:, j, :, 0::2, :], ps[:, 4, :].rearrange("p (h e) -> p h e", e=HD)
                              .unsqueeze(2).to_broadcast([P, NH, 2, HD]), ACT.Copy)
                k = ps[:, 5, 0:P].rearrange("p (g e) -> p g e", e=HD)
                a_.activation(k_parts[:, j, :, 0:2, :], k.unsqueeze(2).to_broadcast([P, NKV, 2, HD]),
                              ACT.Copy).then_inc(qkv_hi_done, 1)

            def take_q(c, iblk, part):
                act.wait_ge(q_turned, 4 * c + (2 * iblk + part + 1))
                a_.activation(q_stack[:, iblk, part * PAIRS // 2:(part + 1) * PAIRS // 2, :], ps[:, 4:6, :],
                              ACT.Copy).then_inc(q_ev, 1)

            def take_k(c):
                act.wait_ge(k_turned, c + 1)
                a_.activation(k_stack[:, 0:2, :].rearrange("p g t -> p (g t)"), ps[:, 4, :], ACT.Copy).then_inc(k_ev, 1)

            take_row(0)
            take_row(1)
            act.wait_ge(wqkv_arrived, 16)
            a_.activation(wqkv_hi[:], wqkv_in[:], ACT.Copy).then_inc(wqkv_hi_done, 1)
            split_batch(0)
            act.wait_ge(wo_arrived, 16)
            a_.activation(wo_hi[:], wo_in[:], ACT.Copy).then_inc(wqkv_hi_done, 1)
            split_qkv(0, 0)
            take_row(2)
            split_qkv(0, 1)
            take_row(3)
            act.wait_ge(const_ready, 1)
            act.wait_ge(wqkv_lo_done, 2)
            take_q(0, 0, 0)
            take_q(0, 0, 1)
            take_k(0)
            act.wait_ge(late_in, 3 * 16)
            a_.activation(gw_parts[:, :, 0:E], gw[:], ACT.Copy).then_inc(gw_split, 1)
            take_row(4)
            take_row(5)


            def exponentials(b, n):
                nj = n // NKV + 1
                act.wait_ge(probs_turned, UNITS * b + (n + 1))
                if n >= 2:
                    act.wait_ge(pv_done, UNITS * b + (n - 1))
                a_.activation(probsT[:, n % 2, 0:nj, :], ps[:, 2 * (n % 2):2 * (n % 2) + nj, :], ACT.Exp,
                              scale=float(HD) ** -0.5).then_inc(exp_done, 1)

            def attend(b, more):
                def take_sums(n):
                    act.wait_ge(pv_done, UNITS * b + (n + 1))
                    if n >= 2:
                        act.wait_ge(sums_turned, UNITS * b + (n - 1))
                    a_.activation(sums[:, n % 2], ps[0:VW, 6, :], ACT.Copy).then_inc(sums_ev, 1)

                for n in range(1, UNITS):
                    exponentials(b, n)
                    take_sums(n - 1)
                    for part in range(2):
                        if n + 1 == TURN_Q1[part]:
                            take_q(b, 1, part)
                        if more and n + 1 == PROJECT[part]:
                            split_qkv(b + 1, part)
                        if more and n + 1 == TURN_Q0[part]:
                            take_q(b + 1, 0, part)
                    if more and n + 1 == TURN_XN + 2:
                        split_batch(b + 1)
                    if more and n + 1 == UNITS - 1:
                        take_k(b + 1)
                take_sums(UNITS - 1)
                if more:
                    exponentials(b + 1, 0)
                act.wait_ge(heads_turned, b + 1)
                a_.activation(act_hi[:, :, b * S:(b + 1) * S] if isinstance(b, int) else act_hi[:, :, bass.ts(b, S)],
                              ps[:, 4:6, :].rearrange("p c (m s) -> p (c m) s", s=S),
                              ACT.Copy).then_inc(heads_hi, 1)

            exponentials(0, 0)
            with act.Fori(0, B - 1) as b:
                attend(b, True)
            attend(B - 1, False)

            def take_logits(h):
                act.wait_ge(logits_mm, h + 1)
                a_.activation(logitsT[:], ps[0:2 * E, ROUTE_BANK[h], :], ACT.Copy).then_inc(logits_ev, 1)

            def soften(h):
                act.wait_ge(gap_done, h + 1)
                a_.activation(e2[:], gap[:], ACT.Exp).then_inc(e2_done, 1)

            def store_shares(h):
                act.wait_ge(comb_turned, h + 1)
                if h == 1:
                    act.wait_ge(comb_stored, 16)
                a_.activation(combT[:], ps[0:E, SHARES_BANK[h], :], ACT.Copy).then_inc(comb_ev, 1)
                act.wait_ge(comb_ev, h + 1)
                act.dma_start(d["comb"][SHARED:SHARED + E, h * HALF:(h + 1) * HALF], combT[:]).then_inc(comb_stored, 16)

            def gate_rows(c):
                dst = gate1b[:] if c == 3 else gates[:, c % 2]
                act.wait_ge(gate_mm, c + 1)
                if c == 2:
                    act.wait_ge(resid_done, 2)
                a_.activation(dst, ps[:, 0:4, :], ACT.Copy).then_inc(gate_ev, 1)

            def split_up(a, i):
                kind, r = kind_of(a), a % 2
                used = MZ + MZ_W if kind == HEADS else UP_W
                act.wait_ge(up_arrived[r], 16 * (a // 2 + 1) + 16 * i)
                if a >= 2:
                    act.wait_ge(up_done, a - 1 + 2 * i)
                a_.activation(w_hi[:, r, 0:used], w_in[:, r, 0:used], ACT.Copy).then_inc(up_hi, 1)

            def split_down(a, i):
                kind, r = kind_of(a), a % 2
                at = MZ + MZ_W if kind == HEADS else UP_W
                if HEAD0 <= a < HEAD0 + H1:
                    act.wait_ge(group_sum, a - HEAD0 + 1 + 2 * i)
                    act.dma_start(d["group_sums"][a - HEAD0], w_in[:, r, at:at + D]).then_inc(sum_stored[r], 16)
                else:
                    act.wait_ge(down_arrived[r], 16 * (a // 2 + 1) + 16 * i)
                if a >= 2:
                    act.wait_ge(down_done, a - 1 + 2 * i)
                a_.activation(w_hi[:, r, UP_W:UP_W + D], w_in[:, r, at:at + D], ACT.Copy).then_inc(down_hi, 1)

            gate_rows(0)
            split_act(4)
            split_act(5)
            for at in range(MOD_CH, MOD_CH + 4):
                take_row(at)
            gate_rows(1)
            take_logits(0)
            take_row(MOD_CH + 4)
            soften(0)
            take_row(MOD_CH + 5)
            split_up(0, 0)
            split_down(0, 0)
            gate_rows(2)
            store_shares(0)
            gate_rows(3)

            def split_inner(a, i):
                if a >= 2:
                    act.wait_ge(down_done, a - 1 + 2 * i)
                a_.activation(inner_hi[:, a % 2], inner[:, a % 2], ACT.Copy).then_inc(inner_hi_done, 1)

            def ffn_step(a, i, half, layer0):
                r = a % 2
                if layer0:
                    c = a - half * N_STEPS[FFN0] + 2 * i
                    if a >= 2:
                        act.wait_ge(inner_done, a - 1 + 2 * i)
                    act.dma_start(share[:, r], d["comb"][bass.ds(c, 1), half * HALF:(half + 1) * HALF]
                                  .to_broadcast([P, HALF])).then_inc(share_in[r], 16)
                k = ffn_count(a)
                act.wait_ge(up_done, a + 1 + 2 * i)
                if k >= 2:
                    act.wait_ge(inner_done, k - 1 + 2 * i)
                gate_scale = one[:, 0:1] if layer0 else scales[:, 0:1]
                a_.activation(silu[:, r], ps[:, 2 * r, :], ACT.Silu, scale=gate_scale).then_inc(silu_done, 1)
                act.wait_ge(inner_done, k + 1 + 2 * i)
                split_inner(a, i)

            def split_retrieved(a, i):
                act.wait_ge(ret_turned, a - HEAD0 + 1 + 2 * i)
                act.wait_ge(down_done, a - 1 + 2 * i)
                a_.activation(inner_hi[:, a % 2], ps[:, 1, :], ACT.Copy).then_inc(inner_hi_done, 1)

            def head_step(a, i, first):
                k = a - HEAD0
                act.wait_ge(below_done, k + 1 + 2 * i)
                if k >= 1:
                    act.wait_ge(sig_done, k + 2 * i)
                a_.activation(silu[:, 0], below[:], ACT.Exp).then_inc(elu_done, 1)
                split_up(a + 1, i)
                act.wait_ge(sig_done, k + 1 + 2 * i)
                if k >= 1:
                    act.wait_ge(up_done, a + 2 * i)
                a_.activation(sig_hi[:], sig[:], ACT.Copy).then_inc(sig_hi_done, 1)
                if not first:
                    split_down(a, i)
                    split_retrieved(a - 1, i)

            act.wait_ge(ones_stored, 16)
            for seg, (kind, half, base, n) in enumerate(SEGMENTS):
                if kind == FFN0:
                    act.wait_ge(comb_stored, 16 * (half + 1))

                def body(a, i, s):
                    if kind == HEADS:
                        head_step(a, i, is_first(seg, s))
                    else:
                        if a < LAST_STEP:
                            split_up(a + 1, i)
                        ffn_step(a, i, half, kind == FFN0)
                        if a < LAST_STEP:
                            split_down(a + 1, i)
                    if turning(seg, s) is not None:
                        split_act(turning(seg, s))
                    if seg == 0 and s == n - 2:
                        take_logits(1)
                        soften(1)
                    if seg == 0 and s == n - 1:
                        store_shares(1)

                steps(act, base, n, body)
                if seg == 3:
                    split_retrieved(base + n - 1, 0)
                    split_down(base + n, 0)

        @block.vector
        def _(dve):
            v = nc.vector
            links = [0]

            def link(ins):
                links[0] += 1
                ins.then_inc(router, 1)
                dve.wait_ge(router, links[0])

            dve.wait_ge(const_ready, 3)
            v.tensor_copy(ident_r[:], ident[:])
            v.tensor_copy(ident_bf[:], ident[:])
            v.tensor_copy(causal_bf[:], causal[:]).then_inc(const_bf, 1)

            def mod_columns(l, q):
                dve.wait_ge(mod_turned, cols_count(l, q) + 1)
                v.tensor_scalar(modc[:, l, q * KC:(q + 1) * KC, :],
                                ps[:, MOD_BANK[MOD_CH * l + q], 0:KC * B].rearrange("p (m b) -> p m b", b=B),
                                1.0 if q in (1, 4) else 0.0, None, ALU.add).then_inc(mod_cols, 1)

            def make_gate(l, w):
                at = MOD_CH * l + (2, 5)[w]
                dve.wait_ge(row_ev, at + 1)
                if l == 1:
                    dve.wait_ge(gate_mm, w + 1)
                row = mod_row[:, at % 2]
                link(v.tensor_scalar(sign[:], row, 0.0, 2.0, ALU.is_ge, ALU.mult))
                gate = gate_row[:, w]
                link(v.scalar_tensor_tensor(gate, sign[:], -1.0, row, ALU.add, ALU.mult))
                link(v.tensor_scalar(gate, gate, 0.25, None, ALU.max))
                v.scalar_tensor_tensor(gate, sign[:], -1.0, gate, ALU.add, ALU.mult).then_inc(gate_row_done, 1)
                dve.wait_ge(gate_row_done, 2 * l + w + 1)

            def norm_stats(n):
                tiles = half_tiles(n % 2)
                if n < 2:
                    dve.wait_ge(x_in[n % 2], 16)
                for j, t in enumerate(tiles):
                    v.bn_stats(stats[:, j, :], x[:, t, :]).then_inc(ln_tmp, 1)
                dve.wait_ge(ln_tmp, TH * (n + 1))
                for j, t in enumerate(tiles):
                    ins = v.bn_aggr(mv0[:, t, :] if n < 2 else mv[:, j, :], stats[:, j, :])
                ins.then_inc(ln_stats, 1)
                dve.wait_ge(ln_stats, n + 1)

            def norm(n):
                dve.wait_ge(ln_rstd, n + 1)
                for j, t in enumerate(half_tiles(n % 2)):
                    ins = v.tensor_scalar(xn[:, j, :], x[:, t, :], mv[:, j, 0:1], rstd[:, j:j + 1],
                                          ALU.subtract, ALU.mult)
                ins.then_inc(ln_xn, 1)

            def norm_batch(c):
                for j in range(2):
                    t = bass.ds(2 * c + j, 1)
                    ins = v.tensor_scalar(xn[:, j:j + 1, :], x[:, t, :], mv0[:, t, 0], rstd0[:, t],
                                          ALU.subtract, ALU.mult)
                ins.then_inc(xn0_done, 1)

            def modulate_batch(c, part):
                if part == 0:
                    dve.wait_ge(turned, 2 * c + 2)
                    dve.wait_ge(act_lo_done, c)
                for k in (2 * part, 2 * part + 1):
                    src = ps[:, 4 + part, (k % 2) * S:(k % 2 + 1) * S]
                    ins = v.tensor_scalar(h32[:, 0, k, :], src, modc[:, 0, KC + k, bass.ds(c, 1)],
                                          modc[:, 0, k, bass.ds(c, 1)], ALU.mult, ALU.add)
                if part == 1:
                    ins.then_inc(h32_done, 1)

            def rest_of_q(c, j):
                dve.wait_ge(qkv_hi_done, 2 * c + (j + 1))
                q = ps[:, 4, :].rearrange("p (h e) -> p h e", e=HD)
                v.tensor_tensor(q_parts[:, j, :, 1::2, :], q.unsqueeze(2).to_broadcast([P, NH, 2, HD]),
                                q_parts[:, j, :, 0::2, :].bitcast(FP), ALU.subtract)

            def rest_of_kv(c, j):
                k = ps[:, 5, 0:P].rearrange("p (g e) -> p g e", e=HD)
                v.tensor_tensor(k_parts[:, j, :, 2:4, :], k.unsqueeze(2).to_broadcast([P, NKV, 2, HD]),
                                k_parts[:, j, :, 0:2, :].bitcast(FP), ALU.subtract)
                v.tensor_copy(v_next[:, j], ps[:, 5, P:2 * P].rearrange("p (g e) -> p g e", e=HD)).then_inc(qkv_lo_done, 1)

            def take_k(c):
                dve.wait_ge(k_turned, c + 1)
                v.tensor_copy(k_stack[:, 2:4, :].rearrange("p g t -> p (g t)"), ps[:, 5, :]).then_inc(k_ev, 1)

            def take_v(c):
                dve.wait_ge(qkv_lo_done, 2 * c + 2)
                v.tensor_copy(v1[:, :, :, 0:HD], v_next[:]).then_inc(v_ev, 1)

            def modulate(m, banks, parts=(0, 1)):
                ln, b = m // B, m % B
                l, q = ln // 2, 3 * (ln % 2)
                if parts[0] == 0:
                    dve.wait_ge(act_lo_done, m - 1)
                for part in parts:
                    dve.wait_ge(turned, 2 * m + (1 + part if banks[0] == banks[1] else 2))
                    for k in (2 * part, 2 * part + 1):
                        src = ps[:, banks[part], (k % 2) * S:(k % 2 + 1) * S]
                        ins = v.tensor_scalar(h32[:, m % 2, k, :], src, modc[:, l, (q + 1) * KC + k, b:b + 1],
                                              modc[:, l, q * KC + k, b:b + 1], ALU.mult, ALU.add)
                    if part == 0 and banks[0] == banks[1]:
                        ins.then_inc(half_taken, 1)
                if parts[-1] == 1:
                    ins.then_inc(h32_done, 1)

            def residual(seq, gate, down_scale, bank):
                for j, t in enumerate(half_tiles(seq % 2)):
                    ins = v.scalar_tensor_tensor(xn[:, j, :], ps[:, bank + j, :], down_scale,
                                                 gate[:, t // 2, :], ALU.mult, ALU.mult)
                ins.then_inc(addend_done, 1)

            def add_residual(seq):
                dve.wait_ge(addend_done, seq + 1)
                tiles = half_tiles(seq % 2)
                v.tensor_tensor(x[:, tiles[0]:tiles[0] + TH, :], x[:, tiles[0]:tiles[0] + TH, :], xn[:],
                                ALU.add).then_inc(resid_done, 1)
                dve.wait_ge(resid_done, seq + 1)

            norm_stats(0)
            mod_columns(0, 0)
            mod_columns(0, 1)
            dve.wait_ge(mod_cols, 2)
            dve.wait_ge(ln_rstd, 1)
            norm_batch(0)
            modulate_batch(0, 0)
            modulate_batch(0, 1)
            dve.wait_ge(wqkv_hi_done, 1)
            v.tensor_tensor(wqkv_lo[:], wqkv_in[:], wqkv_hi[:].bitcast(FP), ALU.subtract).then_inc(wqkv_lo_done, 1)
            norm_stats(1)
            dve.wait_ge(wqkv_hi_done, 2)
            v.tensor_tensor(wo_lo[:], wo_in[:], wo_hi[:].bitcast(FP), ALU.subtract).then_inc(wqkv_lo_done, 1)
            for part in range(2):
                rest_of_q(0, part)
                rest_of_kv(0, part)
                if part == 0:
                    make_gate(0, 0)
            v.memset(v1[:, :, :, HD:VW], 1.0).then_inc(heads_taken, 1)
            take_v(0)
            dve.wait_ge(wqkv_lo_done, 2)
            mod_columns(0, 3)
            take_k(0)
            dve.wait_ge(ln_rstd, 2)

            def shift(b, n):
                r, w = n % 2, P * (n // NKV + 1)
                sc = ps[:, 2 * r:2 * r + 2, 0:2 * w].rearrange("p c (h s) -> p c h s", h=2)
                dve.wait_ge(scored, UNITS * b + (n + 1))
                v.tensor_reduce(row_max[:, r, :].rearrange("p (c h) -> p c h", c=2), sc, AX.X, ALU.max).then_inc(max_done, 1)
                dve.wait_ge(max_done, UNITS * b + (n + 1))
                if not (isinstance(b, int) and b == 0 and n < 2):
                    dve.wait_ge(probs_turned, UNITS * b + (n - 1))
                v.tensor_tensor(shifted[:, r, :, 0:w].rearrange("p (c h) s -> p c h s", c=2), sc,
                                row_max[:, r, :].rearrange("p (c h) -> p c h", c=2).unsqueeze(3)
                                .to_broadcast([P, 2, 2, w]), ALU.subtract).then_inc(shift_done, 1)

            def attend(b, more):
                def normalise(q):
                    iblk = q // 2
                    dve.wait_ge(sums_turned, UNITS * b + (4 * q + 4))
                    o = ps[:, 7, 0:16 * VW].rearrange("p (h e) -> p h e", e=VW)
                    v.reciprocal(rsum[:, q % 2, :], o[:, :, HD]).then_inc(rsum_done, 1)
                    dve.wait_ge(rsum_done, 4 * b + (q + 1))
                    dst = heads_out[:, iblk, (q % 2) * 256:(q % 2 + 1) * 256].rearrange("p (h e) -> p h e", e=HD)
                    v.tensor_tensor(dst, o[:, :, 0:HD], rsum[:, q % 2, :].unsqueeze(2).to_broadcast([P, 16, HD]),
                                    ALU.mult).then_inc(heads_ev, 1)

                for n in range(2, UNITS):
                    shift(b, n)
                    if n >= 6 and (n - 6) % 4 == 0:
                        normalise((n - 6) // 4)
                    if more:
                        if n == TURN_XN - 2:
                            norm_batch(b + 1)
                        for part in range(2):
                            if n == TURN_XN + part:
                                modulate_batch(b + 1, part)
                            if n == PROJECT[part]:
                                rest_of_q(b + 1, part)
                            if n == PROJECT[part] + 1:
                                rest_of_kv(b + 1, part)
                if more:
                    take_k(b + 1)
                    shift(b + 1, 0)
                    shift(b + 1, 1)
                normalise(3)
                if more:
                    take_v(b + 1)
                dve.wait_ge(heads_hi, b + 1)
                lo = act_lo[:, :, b * S:(b + 1) * S] if isinstance(b, int) else act_lo[:, :, bass.ts(b, S)]
                hi = act_hi[:, :, b * S:(b + 1) * S] if isinstance(b, int) else act_hi[:, :, bass.ts(b, S)]
                v.tensor_tensor(lo, ps[:, 4:6, :].rearrange("p c (m s) -> p (c m) s", s=S),
                                hi.bitcast(FP), ALU.subtract).then_inc(heads_taken, 1)

            shift(0, 0)
            shift(0, 1)
            dve.wait_ge(gw_split, 1)
            v.tensor_tensor(gw_parts[:, :, E:2 * E], gw[:], gw_parts[:, :, 0:E].bitcast(FP), ALU.subtract).then_inc(gw_split, 1)
            mod_columns(0, 4)
            make_gate(0, 1)
            with dve.Fori(0, B - 1) as b:
                attend(b, True)
            attend(B - 1, False)

            def route(h):
                dve.wait_ge(logits_turned, h + 1)
                parts = ps[:, ROUTE_BANK[h], 0:2 * TH * E].rearrange("p (t a e) -> p t a e", a=2, e=E)
                link(v.tensor_copy(logits[:], parts[:, :, 0, :]))
                v.tensor_tensor(logits[:], logits[:], parts[:, :, 1, :], ALU.add).then_inc(logits_done, 1)
                dve.wait_ge(logits_done, h + 1)
                for j in range(TH):
                    link(v.max(top8[:, j, :], logits[:, j, :]))
                    link(v.max_index(top_at[:, j, :], top8[:, j, :], logits[:, j, :]))
                v.tensor_tensor(gap[:], top8[:, :, 1], top8[:, :, 0], ALU.subtract).then_inc(gap_done, 1)
                link(v.tensor_copy(top_f[:], top_at[:, :, 0:2]))
                dve.wait_ge(e2_done, h + 1)
                link(v.tensor_scalar(w2[:], e2[:], 1.0, None, ALU.add))
                link(v.reciprocal(w1[:], w2[:]))
                link(v.tensor_tensor(w2[:], w1[:], e2[:], ALU.mult))
                for j in range(TH):
                    v.tensor_scalar(pick1[:, j, :], iota_e[:], top_f[:, j, 0:1], w1[:, j:j + 1], ALU.is_equal, ALU.mult)
                    ins = v.tensor_scalar(pick2[:, j, :], iota_e[:], top_f[:, j, 1:2], w2[:, j:j + 1], ALU.is_equal, ALU.mult)
                link(ins)
                v.tensor_tensor(pick1[:], pick1[:], pick2[:], ALU.add).then_inc(comb_done, 1)

            dve.wait_ge(proj_done, 1)
            dve.wait_ge(gate_ev, 1)
            residual(0, gates[:, 0], 1.0, 4)
            add_residual(0)
            norm_stats(2)
            norm(2)
            modulate(4, (4, 5))
            modulate(5, (6, 7))
            dve.wait_ge(proj_done, 2)
            residual(1, gates[:, 0], 1.0, 0)
            add_residual(1)
            norm_stats(3)
            norm(3)
            mod_columns(1, 0)
            mod_columns(1, 1)
            make_gate(1, 0)
            route(0)
            mod_columns(1, 3)
            make_gate(1, 1)
            mod_columns(1, 4)

            def rest_of_inner(a, i):
                dve.wait_ge(inner_hi_done, a + 1 + 2 * i)
                if a >= 2:
                    dve.wait_ge(down_done, a - 1 + 2 * i)

            def ffn_step(a, i, layer0):
                r = a % 2
                dve.wait_ge(silu_done, ffn_count(a) + 1 + 2 * i)
                up_scale = 1.0 if layer0 else scales[:, 1:2]
                dst = inner[:, r]
                ins = v.scalar_tensor_tensor(dst, ps[:, 2 * r + 1, :], up_scale, silu[:, r], ALU.mult, ALU.mult)
                if layer0:
                    ins.then_inc(scaled_done, 1)
                    dve.wait_ge(scaled_done, a + 1 + 2 * i)
                    dve.wait_ge(share_in[r], 16 * (a // 2 + 1) + 16 * i)
                    ins = v.tensor_tensor(dst, inner[:, r], share[:, r], ALU.mult)
                ins.then_inc(inner_done, 1)
                rest_of_inner(a, i)
                v.tensor_tensor(inner_lo[:, r], inner[:, r], inner_hi[:, r].bitcast(FP),
                                ALU.subtract).then_inc(inner_lo_done, 1)

            def rest_of_retrieved(a, i):
                rest_of_inner(a, i)
                v.tensor_tensor(inner_lo[:, a % 2], ps[:, 1, :], inner_hi[:, a % 2].bitcast(FP),
                                ALU.subtract).then_inc(inner_lo_done, 1)

            def retrieve(a, i):
                r, k = a % 2, a - HEAD0
                dve.wait_ge(up_done, a + 1 + 2 * i)
                nd = [ps[:, c, 0:2 * MZ_W].rearrange("p (t w) -> p t w", w=MZ_W) for c in (1, 3)]
                for c in range(2):
                    ins = v.tensor_scalar(den[:, c, :], nd[c][:, :, P], DEN_EPS, None, ALU.add)
                ins.then_inc(den_done, 1)
                dve.wait_ge(den_done, k + 1 + 2 * i)
                v.reciprocal(rden[:], den[:]).then_inc(rden_done, 1)
                dve.wait_ge(rden_done, k + 1 + 2 * i)
                for c in range(2):
                    ins = v.tensor_tensor(inner[:, r, c * S:(c + 1) * S].rearrange("p (t e) -> p t e", t=2),
                                          nd[c][:, :, 0:P], rden[:, c, :].unsqueeze(2).to_broadcast([P, 2, P]), ALU.mult)
                ins.then_inc(ret_done, 1)

            def head_step(a, i, first, m):
                k = a - HEAD0
                dve.wait_ge(q1_done, k + 1 + 2 * i)
                if k >= 1:
                    dve.wait_ge(elu_done, k + 2 * i)
                bias = bq[:, bass.ds(k % H1 + 2 * i, 1)]
                q = ps[:, 2 * (a % 2), :]
                v.tensor_scalar(below[:], q, bias, 0.0, ALU.add, ALU.min).then_inc(below_done, 1)
                v.tensor_scalar(silu[:, 1], q, bias, 0.0, ALU.add, ALU.max).then_inc(above_done, 1)
                if not first:
                    retrieve(a - 1, i)
                if m is not None:
                    modulate(m, turn_banks(a, HEADS), (0,))
                dve.wait_ge(above_done, k + 1 + 2 * i)
                dve.wait_ge(elu_done, k + 1 + 2 * i)
                if k >= 1:
                    dve.wait_ge(sig_lo_done, k + 2 * i)
                v.tensor_tensor(sig[:], silu[:, 0], silu[:, 1], ALU.add).then_inc(sig_done, 1)
                if m is not None:
                    modulate(m, turn_banks(a, HEADS), (1,))
                dve.wait_ge(sig_hi_done, k + 1 + 2 * i)
                v.tensor_tensor(sig_lo[:], sig[:], sig_hi[:].bitcast(FP), ALU.subtract).then_inc(sig_lo_done, 1)
                if not first:
                    rest_of_retrieved(a - 1, i)

            def take_output(seg):
                kind, _, base, n = SEGMENTS[seg]
                dve.wait_ge(down_done, base + n)
                gate = (gates[:, 1], gates[:, 0], gate1b[:])[kind]
                residual(2 + seg, gate, scales[:, 2:3] if kind == FFN1 else 1.0, 4)

            for seg, (kind, half, base, n) in enumerate(SEGMENTS):
                def body(a, i, s):
                    m = turning(seg, s)
                    if kind == HEADS:
                        head_step(a, i, is_first(seg, s), m)
                    else:
                        if m is not None:
                            modulate(m, turn_banks(a, kind))
                        ffn_step(a, i, kind == FFN0)
                    out_at, add_at, stats_at, norm_at = other_half(seg)[:4]
                    if seg >= 1 and s == out_at:
                        take_output(seg - 1)
                    if seg >= 1 and s == add_at:
                        add_residual(1 + seg)
                    if 1 <= seg < 5 and s == stats_at:
                        norm_stats(3 + seg)
                    if 1 <= seg < 5 and s == norm_at:
                        norm(3 + seg)
                    if seg == 0 and s == n - 2:
                        route(1)

                steps(dve, base, n, body)
                if seg == 3:
                    retrieve(base + n - 1, 0)
                    rest_of_retrieved(base + n - 1, 0)
            take_output(5)
            add_residual(7)

        @block.tensor
        def _(pe):
            t_ = nc.tensor

            def three(out, w, xs, first, last):
                t_.matmul(out, w[0], xs[0], start=first, stop=False)
                t_.matmul(out, w[0], xs[1], start=False, stop=False)
                return t_.matmul(out, w[1], xs[0], start=False, stop=last)

            def modulation(at):
                pe.wait_ge(wmod_in[at % 2], 16 * (at // 2 + 1))
                for k in range(KC):
                    ins = t_.matmul(ps[0:B, MOD_BANK[at], :], silu_c[:, at // MOD_CH, k, :], wmod[:, at % 2, k, :],
                                    start=k == 0, stop=k == KC - 1)
                ins.then_inc(mod_mm, 1)

            def turn_row(at):
                pe.wait_ge(row_ev, at + 1)
                for m in range(KC):
                    c = m * B
                    ins = t_.transpose(ps[:, MOD_BANK[at], c:c + B], mod_row[:, at % 2, m * P:(m + 1) * P],
                                       ident[0:B, 0:B])
                ins.then_inc(mod_turned, 1)

            def gate_rows(c):
                pe.wait_ge(gate_row_done, c + 1)
                if c >= 1:
                    pe.wait_ge(gate_ev, c)
                for b in range(B):
                    ins = t_.matmul(ps[:, b, :], row_of[:, b, :], gate_row[:, c % 2, :], start=True, stop=True)
                ins.then_inc(gate_mm, 1)

            def turn(m, banks, parts=(0, 1)):
                for k in range(2 * parts[0], 2 * parts[-1] + 2):
                    for j in range(2):
                        c = (k % 2) * S + j * P
                        ins = t_.transpose(ps[:, banks[k // 2], c:c + P],
                                           xn[:, 2 * (m % 2) + j, k * P:(k + 1) * P], ident[:])
                ins.then_inc(turned, len(parts))

            def turn_batch(c):
                pe.wait_ge(xn0_done, c + 1)
                for k in range(KC):
                    for j in range(2):
                        at = (k % 2) * S + j * P
                        ins = t_.transpose(ps[:, 4 + k // 2, at:at + P], xn[:, j, k * P:(k + 1) * P], ident[:])
                ins.then_inc(turned, 2)

            def project(c, j):
                pe.wait_ge(act_lo_done, c + 1)
                if j == 0:
                    pe.wait_ge(h32_done, c + 1)
                else:
                    pe.wait_ge(qkv_lo_done, 2 * c + 1)
                for bank, cols in ((4, slice(0, D)), (5, slice(D, QKV))):
                    for k in range(KC):
                        ins = three(ps[:, bank, 0:cols.stop - cols.start],
                                    (xa_hi[:, k, j * P:(j + 1) * P], xa_lo[:, k, j * P:(j + 1) * P]),
                                    (wqkv_hi[:, k, cols], wqkv_lo[:, k, cols]), k == 0, k == KC - 1)
                ins.then_inc(qkv_mm, 1)

            def stack_q(c, iblk, part):
                if part == 0 and iblk == 0:
                    pe.wait_ge(qkv_lo_done, 2 * c + 2)
                elif part == 0:
                    pe.wait_ge(heads_taken, c + 1)
                    pe.wait_ge(k_ev, 2 * c + 2)
                else:
                    pe.wait_ge(q_ev, 4 * c + (2 * iblk + 1))
                for a in range(PAIRS // 2):
                    h = 2 * (part * PAIRS // 2 + a)
                    both = q_parts[:, iblk, h:h + 2, :, :].rearrange("p h a e -> p (h a e)")
                    ins = t_.matmul(ps[:, 4 + a // 4, (a % 4) * P:(a % 4 + 1) * P], both, ident_r[:],
                                    start=True, stop=True)
                ins.then_inc(q_turned, 1)

            def stack_k(c):
                pe.wait_ge(q_ev, 4 * c + 2)
                for a in range(NKV // 2):
                    for j in range(2):
                        both = k_parts[:, j, 2 * a:2 * a + 2, :, :].rearrange("p g a e -> p (g a e)")
                        at = (a % 2) * S + j * P
                        ins = t_.matmul(ps[:, 4 + a // 2, at:at + P], both, ident_r[:], start=True, stop=True)
                ins.then_inc(k_turned, 1)

            def score(b, n):
                iblk, gr, r = n // NKV, n % NKV, n % 2
                w = P * (iblk + 1)
                if not (isinstance(b, int) and b == 0 and n < 2):
                    pe.wait_ge(exp_done, UNITS * b + (n - 1))
                if n == 0:
                    pe.wait_ge(k_ev, 2 * b + 2)
                    pe.wait_ge(q_ev, 4 * b + 2)
                if n == NKV:
                    pe.wait_ge(q_ev, 4 * b + 4)
                rows = slice(STACK * (gr % 2), STACK * (gr % 2 + 1))
                for h in range(REP):
                    t_.matmul(ps[:, 2 * r + h // 2, (h % 2) * w:(h % 2 + 1) * w],
                              q_stack[rows, iblk, gr // 2 * REP + h, :], k_stack[rows, gr // 2, 0:w],
                              start=h % 2 == 0, stop=True, skip_group_check=True)
                for c in range(2):
                    ins = t_.matmul(ps[:, 2 * r + c, 0:2 * w].rearrange("p (h s) -> p h s", h=2)[:, :, w - P:w],
                                    ident_bf[:], causal_bf[:].unsqueeze(1).to_broadcast([P, 2, P]),
                                    start=False, stop=True, skip_group_check=True)
                ins.then_inc(scored, 1)

            def turn_scores(b, n):
                r = n % 2
                pe.wait_ge(shift_done, UNITS * b + (n + 1))
                for j in range(n // NKV + 1):
                    for h in range(REP):
                        ins = t_.transpose(ps[:, 2 * r + j, h * P:(h + 1) * P],
                                           shifted[:, r, h, j * P:(j + 1) * P], ident[:])
                ins.then_inc(probs_turned, 1)

            pe.wait_ge(silu_c_done, 1)
            pe.wait_ge(const_ready, 3)
            modulation(0)
            modulation(1)
            turn_row(0)
            turn_row(1)
            turn_batch(0)
            pe.wait_ge(const_bf, 1)
            pe.wait_ge(wqkv_lo_done, 1)
            project(0, 0)
            modulation(2)
            project(0, 1)
            modulation(3)
            stack_q(0, 0, 0)
            turn_row(3)
            stack_q(0, 0, 1)
            stack_k(0)
            pe.wait_ge(row_ev, 4)
            pe.wait_ge(mod_cols, 3)
            score(0, 0)
            score(0, 1)
            modulation(4)
            modulation(5)
            turn_row(4)
            turn_scores(0, 0)
            pe.wait_ge(mod_cols, 4)
            pe.wait_ge(row_ev, 6)

            def attend(b, more):
                def weigh(n):
                    iblk, gr, r = n // NKV, n % NKV, n % 2
                    pe.wait_ge(exp_done, UNITS * b + (n + 1))
                    if n == 0:
                        pe.wait_ge(v_ev, b + 1)
                    else:
                        pe.wait_ge(sums_ev, UNITS * b + n)
                    if n % 4 == 1 and n > 4:
                        pe.wait_ge(heads_ev, 4 * b + n // 4)
                    for j in range(iblk + 1):
                        ins = t_.matmul(ps[0:VW, 6, :], v1[:, j, gr, :], probsT[:, r, j, :], start=j == 0, stop=j == iblk)
                    ins.then_inc(pv_done, 1)

                def turn_sums(n):
                    for h in range(REP):
                        c = (n % 4 * REP + h) * VW
                        ins = t_.transpose(ps[:, 7, c:c + VW], sums[:, n % 2, h * P:(h + 1) * P], ident[0:VW, 0:VW])
                    ins.then_inc(sums_turned, 1)

                def meanwhile(n):
                    for part in range(2):
                        if n == TURN_Q1[part]:
                            stack_q(b, 1, part)
                        if more and n == TURN_Q0[part]:
                            stack_q(b + 1, 0, part)
                        if more and n == PROJECT[part]:
                            project(b + 1, part)
                    if more and n == TURN_XN:
                        pe.wait_ge(q_ev, 4 * b + 4)
                        turn_batch(b + 1)

                for n in range(2, UNITS):
                    score(b, n)
                    turn_scores(b, n - 1)
                    weigh(n - 2)
                    if n >= 3:
                        turn_sums(n - 3)
                    if n < UNITS - 1:
                        meanwhile(n)
                if more:
                    stack_k(b + 1)
                turn_scores(b, UNITS - 1)
                weigh(UNITS - 2)
                if more:
                    score(b + 1, 0)
                turn_sums(UNITS - 3)
                weigh(UNITS - 1)
                if more:
                    score(b + 1, 1)
                    turn_scores(b + 1, 0)
                turn_sums(UNITS - 2)

                def turn_heads(iblk):
                    for k in range(KC):
                        c = (k % 2) * S + iblk * P
                        ins = t_.transpose(ps[:, 4 + k // 2, c:c + P], heads_out[:, iblk, k * P:(k + 1) * P], ident[:])
                    return ins

                pe.wait_ge(sums_ev, UNITS * b + UNITS)
                turn_heads(0)
                turn_sums(UNITS - 1)
                pe.wait_ge(heads_ev, 4 * b + 4)
                ins = turn_heads(1)
                ins.then_inc(heads_turned, 1)

            with pe.Fori(0, B - 1) as b:
                attend(b, True)
            attend(B - 1, False)

            gate_rows(0)
            pe.wait_ge(heads_taken, B + 1)
            pe.wait_ge(wqkv_lo_done, 2)
            for half in range(2):
                if half == 1:
                    pe.wait_ge(gate_ev, 1)
                for j in range(TH):
                    t = half * TH + j
                    for k in range(KC):
                        ins = three(ps[:, 4 * (1 - half) + j, :],
                                    (act_hi[:, k, t * P:(t + 1) * P], act_lo[:, k, t * P:(t + 1) * P]),
                                    (wo_hi[:, k, :], wo_lo[:, k, :]), k == 0, k == KC - 1)
                ins.then_inc(proj_done, 1)
            for m in (4, 5):
                pe.wait_ge(ln_xn, 1)
                turn(m, (4 + 2 * (m % 2), 5 + 2 * (m % 2)))
            for at, freed in ((0, 5), (1, 5), (2, 6), (3, 6)):
                pe.wait_ge(h32_done, freed)
                modulation(MOD_CH + at)
                if at == 2:
                    turn_row(MOD_CH)
                    turn_row(MOD_CH + 1)
            pe.wait_ge(addend_done, 2)
            gate_rows(1)

            def route(h, bank):
                pe.wait_ge(act_lo_done, 6 + 2 * h)
                cols = slice(h * HALF, (h + 1) * HALF)
                for k in range(KC):
                    for q, xa in enumerate((act_hi, act_lo)):
                        ins = t_.matmul(ps[0:2 * E, bank, :], gw_parts[:, k, :], xa[:, k, cols],
                                        start=(k, q) == (0, 0), stop=(k, q) == (KC - 1, 1))
                ins.then_inc(logits_mm, 1)
                pe.wait_ge(logits_ev, h + 1)
                for j in range(TH):
                    ins = t_.transpose(ps[:, bank, 2 * j * E:2 * (j + 1) * E], logitsT[:, j * P:(j + 1) * P],
                                       ident[0:2 * E, 0:2 * E])
                ins.then_inc(logits_turned, 1)

            def turn_shares(h, bank):
                pe.wait_ge(comb_done, h + 1)
                for j in range(TH):
                    ins = t_.transpose(ps[0:E, bank, j * P:(j + 1) * P], pick1[:, j, :], ident[:])
                ins.then_inc(comb_turned, 1)

            pe.wait_ge(row_ev, MOD_CH + 4)
            pe.wait_ge(gw_split, 2)
            route(0, ROUTE_BANK[0])
            pe.wait_ge(mod_cols, 6)
            modulation(MOD_CH + 4)
            turn_row(MOD_CH + 3)
            modulation(MOD_CH + 5)
            gate_rows(2)
            turn_row(MOD_CH + 4)
            turn_shares(0, SHARES_BANK[0])
            gate_rows(3)
            pe.wait_ge(gate_ev, 4)
            pe.wait_ge(mod_cols, 8)
            pe.wait_ge(comb_ev, 1)

            def down(a, i, s, seg, tiles=range(TH)):
                r = a % 2
                pe.wait_ge(down_lo, a + 1 + 2 * i)
                pe.wait_ge(inner_lo_done, a + 1 + 2 * i)
                if s == 0:
                    pe.wait_ge(addend_done, seg + 2)
                last = s is not None and s == SEGMENTS[seg][3] - 1
                for j in tiles:
                    ins = three(ps[:, 4 + j, :], (inner_hi[:, r, j * P:(j + 1) * P], inner_lo[:, r, j * P:(j + 1) * P]),
                                (w_hi[:, r, UP_W:UP_W + D], w_lo[:, r, UP_W:UP_W + D]), s == 0, last)
                if tiles[-1] == TH - 1:
                    ins.then_inc(down_done, 1)

            def down_before(a, i, s, seg, back, tiles=range(TH)):
                if s is not None and s < back:
                    kind, _, base, n = SEGMENTS[seg - 1]
                    if seg > 0 and (kind == SEGMENTS[seg][0] or s == 0):
                        left = back - s if kind == HEADS else 1
                        down(base + n - left, 0, n - left, seg - 1, tiles)
                    return
                down(a - back, i, None if s is None else s - back, seg, tiles)

            def xs_of(half):
                cols = slice(half * HALF, (half + 1) * HALF)
                return lambda k: (act_hi[:, k, cols], act_lo[:, k, cols])

            def ffn_step(a, i, s, seg, half, m):
                r, xs = a % 2, xs_of(half)
                pe.wait_ge(up_lo, a + 1 + 2 * i)
                if a >= 2:
                    pe.wait_ge(inner_done_of(a - 2), inner_count(a - 2) + 1 + 2 * i)
                for q in range(2):
                    for k in range(KC):
                        c = (2 * k + q) * P
                        ins = three(ps[:, 2 * r + q, :], (w_hi[:, r, c:c + P], w_lo[:, r, c:c + P]), xs(k),
                                    k == 0, k == KC - 1)
                ins.then_inc(up_done, 1)
                if m is not None:
                    pe.wait_ge(ln_xn, m // 2 - 1)
                    pe.wait_ge(inner_done_of(a - 1), inner_count(a - 1) + 1)
                    turn(m, turn_banks(a, FFN0))
                if not (s == 0 and SEGMENTS[seg - 1][0] == HEADS):
                    down_before(a, i, s, seg, 1)

            def inner_done_of(a):
                return ret_done if kind_of(a) == HEADS else inner_done

            def inner_count(a):
                if kind_of(a) == HEADS:
                    return a - HEAD0
                return ffn_count(a)

            def turn_retrieved(a, i):
                pe.wait_ge(ret_done, a - HEAD0 + 1 + 2 * i)
                for j in range(TH):
                    ins = t_.transpose(ps[:, 1, j * P:(j + 1) * P], inner[:, a % 2, j * P:(j + 1) * P], ident[:])
                ins.then_inc(ret_turned, 1)

            def query(a, i, half):
                r, xs = a % 2, xs_of(half)
                pe.wait_ge(up_lo, a + 1 + 2 * i)
                for k in range(KC):
                    ins = three(ps[:, 2 * r, :], (w_hi[:, r, k * P:(k + 1) * P], w_lo[:, r, k * P:(k + 1) * P]),
                                xs(k), k == 0, k == KC - 1)
                ins.then_inc(q1_done, 1)

            def retrieve(a, i):
                r, k_ = a % 2, a - HEAD0
                pe.wait_ge(sig_lo_done, k_ + 1 + 2 * i)
                if k_ >= 1:
                    pe.wait_ge(inner_lo_done, a + 2 * i)
                for j in range(TH):
                    c = (j % 2) * MZ_W
                    ins = three(ps[:, 2 * (j // 2) + 1, c:c + MZ_W],
                                (sig_hi[:, j * P:(j + 1) * P], sig_lo[:, j * P:(j + 1) * P]),
                                (w_hi[:, r, MZ:MZ + MZ_W], w_lo[:, r, MZ:MZ + MZ_W]), True, True)
                ins.then_inc(up_done, 1)

            def head_step(a, i, s, seg, half, m):
                query(a, i, half)
                if is_first(seg, s):
                    down_before(a, i, s, seg, 2)
                    return
                retrieve(a - 1, i)
                if m is None:
                    down_before(a, i, s, seg, 2)
                else:
                    pe.wait_ge(ln_xn, m // 2 - 1)
                    turn(m, turn_banks(a, HEADS), (0,))
                    down_before(a, i, s, seg, 2, range(TH // 2))
                    pe.wait_ge(half_taken, half_turns(m))
                    turn(m, turn_banks(a, HEADS), (1,))
                    down_before(a, i, s, seg, 2, range(TH // 2, TH))
                turn_retrieved(a - 1, i)

            def half_turns(m):
                return m + 1 - (6 + 2 * 2)

            for seg, (kind, half, base, n) in enumerate(SEGMENTS):
                pe.wait_ge(act_lo_done, 6 + 2 * seg)

                def body(a, i, s):
                    if seg == 0 and s == n - 1:
                        pe.wait_ge(logits_done, 2)
                    if seg == 1 and s == 0:
                        pe.wait_ge(comb_ev, 2)
                    m = turning(seg, s)
                    (head_step if kind == HEADS else ffn_step)(a, i, s, seg, half, m)
                    if m is not None:
                        pe.wait_ge(h32_done, m + 1)
                    if seg == 0 and s in (n - 2, n - 1):
                        pe.wait_ge(inner_done_of(a - 1), inner_count(a - 1) + 1)
                        if s == n - 2:
                            route(1, ROUTE_BANK[1])
                        else:
                            turn_shares(1, SHARES_BANK[1])
                steps(pe, base, n, body)
                a = base + n - 1
                if seg == 3:
                    retrieve(a, 0)
                    down(a - 1, 0, n - 2, seg)
                    turn_retrieved(a, 0)
                    down(a, 0, n - 1, seg)
                if seg == 5:
                    down(a, 0, n - 1, seg)


def _chunks(w_gate, w_up, w_down):
    gu = np.stack([w_gate, w_up])
    gu = gu.reshape(2, P, KC, P).transpose(3, 2, 0, 1).reshape(P, UP_W)
    return np.concatenate([gu, w_down.T], axis=1)


def _by_k(w):
    return np.ascontiguousarray(w.reshape(KC, P, -1).transpose(1, 0, 2))


def kernel(**inputs):
    import concourse.bacc as bacc
    from concourse.bass_utils import run_bass_kernel_spmd

    f = {k: np.asarray(v) for k, v in inputs.items()}
    nc = bacc.Bacc("TRN2", target_bir_lowering=False, num_devices=1)

    wq = f["L0_attn_wq"].reshape(D, NKV // 2, 2, REP, HD).transpose(0, 1, 3, 2, 4).reshape(D, NH * HD)
    wqkv = np.concatenate([wq, f["L0_attn_wk"], f["L0_attn_wv"]], axis=1)
    sgu, sdn = f["L0_ffn_shared_w_gate_up"], f["L0_ffn_shared_w_down"]
    rows = [slice(c * P, (c + 1) * P) for c in range(SHARED)]
    ffn0 = [_chunks(sgu[:D][r], sgu[D:][r], sdn[:, r]) for r in rows]
    ffn0 += [_chunks(f["L0_ffn_w_gate_up"][e, :P], f["L0_ffn_w_gate_up"][e, P:], f["L0_ffn_w_down"][e])
             for e in range(E)]
    pad = N_STEPS[FFN1] * P - FF
    gate, up = (np.pad(f[k], ((0, pad), (0, 0))) for k in ("L1_ffn_gate_w", "L1_ffn_up_w"))
    down = np.pad(f["L1_ffn_down_w"], ((0, 0), (0, pad)))
    rows = [slice(c * P, (c + 1) * P) for c in range(N_STEPS[FFN1])]
    ffn1 = [_chunks(gate[r], up[r], down[:, r]) for r in rows]
    heads = []
    for h in range(H1):
        q = f["L1_attn_Wq"][h * G1 * P:(h * G1 + 1) * P]
        q = q.reshape(P, KC, P).transpose(2, 1, 0).reshape(P, KC * P)
        z = f["L1_attn_z"][h][:, None]
        wo = f["L1_attn_Wo"][:, h * G1 * P:(h + 1) * G1 * P]
        wo = wo.reshape(D, G1, P).transpose(2, 1, 0).reshape(P, G1 * D)
        heads.append(np.concatenate([q, f["L1_attn_M"][h], z, z, wo], axis=1))
    arrays = {
        "x": f["L0_attn_x"].reshape(T // P, P, D).transpose(1, 0, 2),
        "cond": np.stack([f[f"L{l}_c"].reshape(B, KC, P).transpose(2, 1, 0) for l in range(2)]),
        "wmod": np.stack([f[f"L{l}_wmod"].reshape(KC, P, MOD_CH, D).transpose(2, 1, 0, 3) for l in range(2)]),
        "wqkv": _by_k(wqkv),
        "wo": _by_k(f["L0_attn_wo"]),
        "gate_w": _by_k(f["L0_ffn_gate_w"].T),
        "bq": f["L1_attn_bq"].reshape(H1, G1, P)[:, 0].T,
        "scales": np.stack([f[f"L1_ffn_{k}_scale"].reshape(()) for k in ("gate", "up", "down")]).reshape(1, 3),
        "ffn0": np.stack(ffn0), "heads": np.stack(heads), "ffn1": np.stack(ffn1),
    }
    arrays = {f"in_{k}": np.ascontiguousarray(a) for k, a in arrays.items()}
    d = {k[3:]: nc.dram_tensor(k, a.shape, FP, kind="ExternalInput").ap() for k, a in arrays.items()}
    d["chunks"] = {FFN0: d["ffn0"], HEADS: d["heads"], FFN1: d["ffn1"]}
    d["group_sums"] = nc.dram_tensor("group_sums", [H1, P, D], FP, kind="Internal").ap()
    d["comb"] = nc.dram_tensor("comb", [SHARED + E, T], FP, kind="Internal").ap()
    d["out"] = nc.dram_tensor("out", [P, T // P, D], FP, kind="ExternalOutput").ap()
    build(nc, d)
    r = run_bass_kernel_spmd(nc, [arrays], core_ids=[0])
    return np.asarray(r.results[0]["out"]).transpose(1, 0, 2).reshape(B, S, D)
```
